# Optimizing a Trainium2 kernel written in Bass

```python
import numpy as np
import jax
import jax.numpy as jnp

def _softmax(x, axis=-1):
    return jax.nn.softmax(x, axis=axis)

def _gelu(x):
    return jax.nn.gelu(x, approximate=True)

def _silu(x):
    return jax.nn.silu(x)

def _sigmoid(x):
    return jax.nn.sigmoid(x)

def _layernorm(x, axis=-1, eps=1e-05):
    m = jnp.mean(x, axis=axis, keepdims=True)
    v = jnp.var(x, axis=axis, keepdims=True)
    return (x - m) / jnp.sqrt(v + eps)

def _scatter_add(tgt, idx, src, axis=0):
    return tgt.at[idx].add(src)

def _segment_sum(src, seg, n):
    return jax.ops.segment_sum(src, seg, n)
kernel_name = 'mk_decoder_postln_d4_seqx_r8_2b7f1e'

def setup_inputs(seed: int=0):
    np.random.seed(seed)
    _w = jnp.asarray

    def _rec_inputs():
        import jax
        import jax.numpy as jnp
        _rk = jax.random.key(seed)
        x = -0.0002928 + 1 * jax.random.normal(jax.random.fold_in(_rk, 1), (8, 56, 256), jnp.float32)
        _lenS = 56 - jax.random.randint(jax.random.fold_in(_rk, 7), (8,), 0, max(1, 56 // 4) + 1, jnp.int32)
        _lenS2 = 1500 - jax.random.randint(jax.random.fold_in(_rk, 8), (8,), 0, max(1, 1500 // 4) + 1, jnp.int32)
        _ctx_512P = jax.random.normal(jax.random.fold_in(_rk, 11), (8, 16, 64), jnp.float32)
        _ctx_512c = jax.random.dirichlet(jax.random.fold_in(_rk, 511), 0.3 * jnp.ones((16,), jnp.float32), (8, 1500))
        _ctx_512t = jnp.einsum('bsk,bkd->bsd', _ctx_512c, _ctx_512P)
        _ctx_512t = _ctx_512t * jax.lax.rsqrt(jnp.mean(jnp.square(_ctx_512t)) + 1e-12) * 0.953939
        ctx_512 = 0.000227908 + 0.99994 * (_ctx_512t + 0.3 * jax.random.normal(jax.random.fold_in(_rk, 611), (8, 1500, 64), jnp.float32))
        return (x, ctx_512)
    x, ctx_512 = _rec_inputs()

    def _L0_attn_setup():
        import jax, jax.numpy as jnp
        import numpy as np
        H = 8
        R = 2
        D = 128
        DEG = 2
        GATE_OFFSET = 6.906768

        def _power_attention(q, k, v, log_g):
            B, T, hq, d = q.shape
            scale = 1.0 / d ** 0.5
            k = jnp.repeat(k, R, axis=2)
            v = jnp.repeat(v, R, axis=2)
            logG = jnp.cumsum(log_g, axis=1)
            logG = jnp.repeat(logG, R, axis=2)
            logG = jnp.transpose(logG, (0, 2, 1))
            qk = jnp.einsum('bthd,bshd->bhts', q, k) * scale
            a = qk ** DEG
            gate = logG[:, :, :, None] - logG[:, :, None, :]
            causal = jnp.tril(jnp.ones((T, T), dtype=bool))
            a = jnp.where(causal, a * jnp.exp(gate), 0.0)
            norm = jnp.sum(a, axis=-1) + 1e-06
            y = jnp.einsum('bhts,bshd->bthd', a, v)
            y = y / jnp.transpose(norm, (0, 2, 1))[..., None]
            return y
        key = jax.random.key(seed)
        ks = jax.random.split(key, 7)
        B, T, C = (1, 256, 256)
        q_dim = H * R * D
        kv_dim = H * D
        s = 0.02
        return {'hidden_states': jax.random.normal(ks[0], (B, T, C), dtype=jnp.float32), 'Wq': jax.random.normal(ks[1], (C, q_dim), dtype=jnp.float32) * s, 'Wk': jax.random.normal(ks[2], (C, kv_dim), dtype=jnp.float32) * s, 'Wv': jax.random.normal(ks[3], (C, kv_dim), dtype=jnp.float32) * s, 'Wg': jax.random.normal(ks[4], (C, H), dtype=jnp.float32) * s, 'Wc': jax.random.normal(ks[5], (q_dim, C), dtype=jnp.float32) * s, 'bc': jnp.zeros((C,), dtype=jnp.float32)}
    _L0_attn_all = _L0_attn_setup()
    _L0_attn_in = {k: v for k, v in _L0_attn_all.items() if k in ('Wq', 'Wk', 'Wv', 'Wg', 'Wc', 'bc')}
    del _L0_attn_all

    def _L0_xattn_setup():
        import jax, jax.numpy as jnp
        import numpy as np
        B, S, L = (2, 128, 128)
        DIM_Q, H, K, D_C, D_CQ, R = (256, 16, 128, 64, 192, 64)

        def _rope_tables(length, dim):
            inv = 1.0 / 10000.0 ** (jnp.arange(0, dim, 2, dtype=jnp.float32) / dim)
            f = jnp.arange(length, dtype=jnp.float32)[:, None] * inv[None, :]
            sin = jnp.repeat(jnp.sin(f), 2, axis=-1)
            cos = jnp.repeat(jnp.cos(f), 2, axis=-1)
            return (sin, cos)

        def _rotate_half(x):
            half = x.shape[-1] // 2
            return jnp.concatenate([-x[..., half:], x[..., :half]], axis=-1)

        def _apply_rope(x, sin, cos):
            return x * cos + _rotate_half(x) * sin
        key = jax.random.key(seed)
        ks = jax.random.split(key, 8)
        return {'hidden_q': jax.random.normal(ks[0], (B, S, DIM_Q), jnp.float32), 'kv_c': jax.random.normal(ks[1], (B, L, D_C), jnp.float32), 'Wq': jax.random.normal(ks[2], (H * K, DIM_Q), jnp.float32) / np.sqrt(DIM_Q).astype(np.float32), 'w_kc_q': jax.random.normal(ks[3], (H, K, D_CQ), jnp.float32) / np.sqrt(K).astype(np.float32), 'w_kc_kv': jax.random.normal(ks[4], (H, K, D_C), jnp.float32) / np.sqrt(K).astype(np.float32), 'W_qr': jax.random.normal(ks[5], (H, D_CQ, R), jnp.float32) / np.float32(np.sqrt(D_CQ) * np.sqrt(R)), 'W_kr': jax.random.normal(ks[6], (H, D_C, R), jnp.float32) / np.sqrt(D_C).astype(np.float32), 'Wo': jax.random.normal(ks[7], (DIM_Q, H * K), jnp.float32) / np.sqrt(H * K).astype(np.float32)}
    _L0_xattn_all = _L0_xattn_setup()
    _L0_xattn_in = {k: v for k, v in _L0_xattn_all.items() if k in ('Wq', 'w_kc_q', 'w_kc_kv', 'W_qr', 'W_kr', 'Wo')}
    del _L0_xattn_all

    def _L0_ffn_setup():
        import jax, jax.numpy as jnp
        import numpy as np
        H = 256
        I = 128
        K = 8
        E = 128
        TOPK = 4
        EPS = 1e-08
        key = jax.random.key(seed)
        ks = jax.random.split(key, 10)
        s = 0.02
        return {'x': jax.random.normal(ks[0], (4, 256, H), jnp.float32), 'w_router': jax.random.normal(ks[1], (H, E), jnp.float32) * s, 'w_gate': jax.random.normal(ks[2], (H, K * I), jnp.float32) * s, 'w_up': jax.random.normal(ks[3], (H, K * I), jnp.float32) * s, 'w_down': jax.random.normal(ks[4], (I, H), jnp.float32) * s, 'amplitudes': jax.random.normal(ks[5], (E, K, 2), jnp.float32) * 0.1, 'expert_scale': jnp.ones((E,), jnp.float32), 'shared_w_gate': jax.random.normal(ks[6], (H, 2 * I), jnp.float32) * s, 'shared_w_up': jax.random.normal(ks[7], (H, 2 * I), jnp.float32) * s, 'shared_w_down': jax.random.normal(ks[8], (2 * I, H), jnp.float32) * s}
    _L0_ffn_all = _L0_ffn_setup()
    _L0_ffn_in = {k: v for k, v in _L0_ffn_all.items() if k in ('w_router', 'w_gate', 'w_up', 'w_down', 'amplitudes', 'expert_scale', 'shared_w_gate', 'shared_w_up', 'shared_w_down')}
    del _L0_ffn_all

    def _L1_attn_setup():
        import jax, jax.numpy as jnp
        import numpy as np
        EMBED = 256
        HEADS = 32
        HEAD_DIM = EMBED // HEADS
        Q_BITS = 4
        Q_MAX = 2 ** (Q_BITS - 1) - 1
        DECOMP = 8
        CHUNK = 32

        def _sym_qdq(x, scale):
            s = jnp.clip(jnp.abs(scale), 1e-09, None)
            return jnp.clip(jnp.round(x / s), -(Q_MAX + 1), Q_MAX) * s

        def _quant_weight(w):
            w = w.astype(jnp.float32)
            s = jnp.max(jnp.abs(w), axis=-1, keepdims=True) / Q_MAX
            return _sym_qdq(w, s)

        def _chunk_decompose(x2d):
            T, H = x2d.shape
            chunks = (T + CHUNK - 1) // CHUNK
            pad = chunks * CHUNK - T
            xp = jnp.pad(x2d, ((0, pad), (0, 0))).reshape(chunks, CHUNK, H).astype(jnp.float32)
            ch_bias = (jnp.max(xp, axis=1, keepdims=True) + jnp.min(xp, axis=1, keepdims=True)) / 2
            xz = xp - ch_bias
            tmax = jnp.max(jnp.abs(xz), axis=(1, 2))
            cmax = jnp.max(jnp.abs(xz), axis=1)
            thr = tmax[:, None] / 2.0 ** jnp.arange(DECOMP - 1, -1, -1, dtype=jnp.float32)
            idx = jnp.sum(cmax[:, :, None] > thr[:, None, :DECOMP - 1], axis=-1)
            scale = tmax[:, None] / 2.0 ** (DECOMP - 1 - idx).astype(jnp.float32) / Q_MAX
            result = _sym_qdq(xz, scale[:, None, :])
            return (result, ch_bias, T)
        key = jax.random.key(seed)
        ks = jax.random.split(key, 10)
        B, T = (2, 128)
        inp = {'hidden_states': jax.random.normal(ks[0], (B, T, EMBED), dtype=jnp.float32), 'q_weight': jax.random.normal(ks[1], (EMBED, EMBED), dtype=jnp.float32) * 0.02, 'k_weight': jax.random.normal(ks[2], (EMBED, EMBED), dtype=jnp.float32) * 0.02, 'v_weight': jax.random.normal(ks[3], (EMBED, EMBED), dtype=jnp.float32) * 0.02, 'o_weight': jax.random.normal(ks[4], (EMBED, EMBED), dtype=jnp.float32) * 0.02, 'q_bias': jax.random.normal(ks[5], (EMBED,), dtype=jnp.float32) * 0.02, 'k_bias': jax.random.normal(ks[6], (EMBED,), dtype=jnp.float32) * 0.02, 'v_bias': jax.random.normal(ks[7], (EMBED,), dtype=jnp.float32) * 0.02, 'o_bias': jax.random.normal(ks[8], (EMBED,), dtype=jnp.float32) * 0.02}
        return inp
    _L1_attn_all = _L1_attn_setup()
    _L1_attn_in = {k: v for k, v in _L1_attn_all.items() if k in ('q_weight', 'k_weight', 'v_weight', 'o_weight', 'q_bias', 'k_bias', 'v_bias', 'o_bias')}
    del _L1_attn_all

    def _L1_xattn_setup():
        import jax, jax.numpy as jnp
        import numpy as np
        B, S, H, NH, L = (2, 256, 256, 16, 64)
        HD = H // NH
        key = jax.random.key(seed)
        k1, k2, k3, k4, k5 = jax.random.split(key, 5)
        scale = 0.02
        return {'q': jax.random.normal(k1, (B, S, H), dtype=jnp.float32), 'latent_kv': jax.random.normal(k2, (B, S, L), dtype=jnp.float32), 'Wq': jax.random.normal(k3, (H, H), dtype=jnp.float32) * scale, 'Wkv_expand': jax.random.normal(k4, (2 * H, L), dtype=jnp.float32) * scale, 'Wout': jax.random.normal(k5, (H, H), dtype=jnp.float32) * scale}
    _L1_xattn_all = _L1_xattn_setup()
    _L1_xattn_in = {k: v for k, v in _L1_xattn_all.items() if k in ('Wq', 'Wkv_expand', 'Wout')}
    del _L1_xattn_all

    def _L1_ffn_setup():
        import jax, jax.numpy as jnp
        import numpy as np
        DIM = 256
        EXPERT_DIM = 128
        N_EXPERTS = 16
        TOPK = 2
        N_SHARED = 1
        B, T = (4, 256)
        key = jax.random.key(seed)
        ks = jax.random.split(key, 9)
        s = 0.02
        return {'x': jax.random.normal(ks[0], (B, T, DIM), jnp.float32), 'router_w': jax.random.normal(ks[1], (N_EXPERTS, DIM), jnp.float32) * s, 'router_bias': jnp.zeros((N_EXPERTS,), jnp.float32), 'Wu': jax.random.normal(ks[2], (N_EXPERTS, DIM, EXPERT_DIM), jnp.float32) * s, 'Wg': jax.random.normal(ks[3], (N_EXPERTS, DIM, EXPERT_DIM), jnp.float32) * s, 'Wd': jax.random.normal(ks[4], (N_EXPERTS, EXPERT_DIM, DIM), jnp.float32) * s, 'Su': jax.random.normal(ks[5], (N_SHARED, DIM, EXPERT_DIM * TOPK), jnp.float32) * s, 'Sg': jax.random.normal(ks[6], (N_SHARED, DIM, EXPERT_DIM * TOPK), jnp.float32) * s, 'Sd': jax.random.normal(ks[7], (N_SHARED, EXPERT_DIM * TOPK, DIM), jnp.float32) * s}
    _L1_ffn_all = _L1_ffn_setup()
    _L1_ffn_in = {k: v for k, v in _L1_ffn_all.items() if k in ('router_w', 'router_bias', 'Wu', 'Wg', 'Wd', 'Su', 'Sg', 'Sd')}
    del _L1_ffn_all

    def _L2_attn_setup():
        import jax, jax.numpy as jnp
        import numpy as np
        import math
        D_MODEL = 256
        N_HEADS = 16
        N_KV_HEADS = 4
        MAX_SEQ_LEN = 256
        ROPE_THETA = 10000.0
        DK = D_MODEL // N_HEADS
        B, T = (2, 256)

        def rope_tables(T, dk, theta, dtype=jnp.float32):
            pairs = jnp.arange(dk // 2, dtype=dtype)
            freqs = 1.0 / theta ** (2.0 * pairs / dk)
            pos = jnp.arange(T, dtype=dtype)
            angles = pos[:, None] * freqs[None, :]
            return (jnp.cos(angles), jnp.sin(angles))

        def apply_rope(t, cos, sin):
            te = t[..., 0::2]
            to = t[..., 1::2]
            oe = te * cos - to * sin
            oo = te * sin + to * cos
            return jnp.stack([oe, oo], axis=-1).reshape(t.shape)
        key = jax.random.key(seed)
        k1, k2, k3, k4 = jax.random.split(key, 4)
        s = 1.0 / math.sqrt(D_MODEL)
        x = jax.random.normal(k1, (B, T, D_MODEL), dtype=jnp.float32)
        q_w = jax.random.normal(k2, (D_MODEL, D_MODEL), dtype=jnp.float32) * s
        kv_w = jax.random.normal(k3, (2 * N_KV_HEADS * DK, D_MODEL), dtype=jnp.float32) * s
        c_w = jax.random.normal(k4, (D_MODEL, D_MODEL), dtype=jnp.float32) * s
        return {'x': x, 'q_w': q_w, 'kv_w': kv_w, 'c_w': c_w}
    _L2_attn_all = _L2_attn_setup()
    _L2_attn_in = {k: v for k, v in _L2_attn_all.items() if k in ('q_w', 'kv_w', 'c_w')}
    del _L2_attn_all

    def _L2_xattn_setup():
        import jax, jax.numpy as jnp
        import numpy as np
        B, S, L = (2, 128, 128)
        DIM_Q, H, K, D_C, D_CQ, R = (256, 16, 128, 64, 192, 64)

        def _rope_tables(length, dim):
            inv = 1.0 / 10000.0 ** (jnp.arange(0, dim, 2, dtype=jnp.float32) / dim)
            f = jnp.arange(length, dtype=jnp.float32)[:, None] * inv[None, :]
            sin = jnp.repeat(jnp.sin(f), 2, axis=-1)
            cos = jnp.repeat(jnp.cos(f), 2, axis=-1)
            return (sin, cos)

        def _rotate_half(x):
            half = x.shape[-1] // 2
            return jnp.concatenate([-x[..., half:], x[..., :half]], axis=-1)

        def _apply_rope(x, sin, cos):
            return x * cos + _rotate_half(x) * sin
        key = jax.random.key(seed)
        ks = jax.random.split(key, 8)
        return {'hidden_q': jax.random.normal(ks[0], (B, S, DIM_Q), jnp.float32), 'kv_c': jax.random.normal(ks[1], (B, L, D_C), jnp.float32), 'Wq': jax.random.normal(ks[2], (H * K, DIM_Q), jnp.float32) / np.sqrt(DIM_Q).astype(np.float32), 'w_kc_q': jax.random.normal(ks[3], (H, K, D_CQ), jnp.float32) / np.sqrt(K).astype(np.float32), 'w_kc_kv': jax.random.normal(ks[4], (H, K, D_C), jnp.float32) / np.sqrt(K).astype(np.float32), 'W_qr': jax.random.normal(ks[5], (H, D_CQ, R), jnp.float32) / np.float32(np.sqrt(D_CQ) * np.sqrt(R)), 'W_kr': jax.random.normal(ks[6], (H, D_C, R), jnp.float32) / np.sqrt(D_C).astype(np.float32), 'Wo': jax.random.normal(ks[7], (DIM_Q, H * K), jnp.float32) / np.sqrt(H * K).astype(np.float32)}
    _L2_xattn_all = _L2_xattn_setup()
    _L2_xattn_in = {k: v for k, v in _L2_xattn_all.items() if k in ('Wq', 'w_kc_q', 'w_kc_kv', 'W_qr', 'W_kr', 'Wo')}
    del _L2_xattn_all

    def _L2_ffn_setup():
        import jax, jax.numpy as jnp
        import numpy as np
        N_EXPERTS = 8
        TOP_K = 2
        C = 256
        H = 128
        HS = 256
        B, T = (1, 64)
        SCALE = 0.02
        key = jax.random.key(seed)
        ks = jax.random.split(key, 10)
        x = jax.random.normal(ks[0], (B, T, C), dtype=jnp.float32)
        gate_w = jax.random.normal(ks[1], (N_EXPERTS, C), dtype=jnp.float32) * SCALE
        w_gate = jax.random.normal(ks[2], (N_EXPERTS, H, C), dtype=jnp.float32) * SCALE
        w_up = jax.random.normal(ks[3], (N_EXPERTS, H, C), dtype=jnp.float32) * SCALE
        w_down = jax.random.normal(ks[4], (N_EXPERTS, C, H), dtype=jnp.float32) * SCALE
        sh_gate = jax.random.normal(ks[5], (HS, C), dtype=jnp.float32) * SCALE
        sh_up = jax.random.normal(ks[6], (HS, C), dtype=jnp.float32) * SCALE
        sh_down = jax.random.normal(ks[7], (C, HS), dtype=jnp.float32) * SCALE
        se_gate_w = jax.random.normal(ks[8], (1, C), dtype=jnp.float32) * SCALE
        return {'x': x, 'gate_w': gate_w, 'w_gate': w_gate, 'w_up': w_up, 'w_down': w_down, 'sh_gate': sh_gate, 'sh_up': sh_up, 'sh_down': sh_down, 'se_gate_w': se_gate_w}
    _L2_ffn_all = _L2_ffn_setup()
    _L2_ffn_in = {k: v for k, v in _L2_ffn_all.items() if k in ('gate_w', 'w_gate', 'w_up', 'w_down', 'sh_gate', 'sh_up', 'sh_down', 'se_gate_w')}
    del _L2_ffn_all

    def _L3_attn_setup():
        import jax, jax.numpy as jnp
        import numpy as np
        import math
        B, L, D = (2, 256, 256)
        H, DH = (16, 128)
        R = 16
        WIN = 64
        EPS = 1e-06

        def _lora_proj(h, Wb, A, Bm, scale):
            return h @ Wb.T + h @ A.T @ Bm.T * scale

        def _rope_freqs(seq_len, d_head):
            half = d_head // 2
            theta = 1.0 / 10000.0 ** (jnp.arange(half, dtype=jnp.float32) / half)
            freqs = jnp.arange(seq_len, dtype=jnp.float32)[:, None] * theta[None, :]
            emb = jnp.concatenate([freqs, freqs], axis=-1)
            return (jnp.cos(emb), jnp.sin(emb))

        def _apply_rope(x, cos, sin):
            half = x.shape[-1] // 2
            x1, x2 = (x[..., :half], x[..., half:])
            rotated = jnp.concatenate([-x2, x1], axis=-1)
            return x * cos[None, None] + rotated * sin[None, None]
        key = jax.random.key(seed)
        ks = jax.random.split(key, 16)

        def rn(k, shape, s=1.0):
            return jax.random.normal(k, shape, dtype=jnp.float32) * s
        d_in_std = 1.0 / math.sqrt(D)
        return {'x': rn(ks[0], (B, L, D)), 'norm_w': jnp.ones((D,), jnp.float32), 'wq': rn(ks[1], (H * DH, D), d_in_std), 'wk': rn(ks[2], (H * DH, D), d_in_std), 'wv': rn(ks[3], (H * DH, D), d_in_std), 'wo': rn(ks[4], (D, H * DH), d_in_std), 'qA': rn(ks[5], (R, D), 0.02), 'qB': rn(ks[6], (H * DH, R), 0.02), 'kA': rn(ks[7], (R, D), 0.02), 'kB': rn(ks[8], (H * DH, R), 0.02), 'vA': rn(ks[9], (R, D), 0.02), 'vB': rn(ks[10], (H * DH, R), 0.02), 'oA': rn(ks[11], (R, H * DH), 0.02), 'oB': rn(ks[12], (D, R), 0.02)}
    _L3_attn_all = _L3_attn_setup()
    _L3_attn_in = {k: v for k, v in _L3_attn_all.items() if k in ('norm_w', 'wq', 'wk', 'wv', 'wo', 'qA', 'qB', 'kA', 'kB', 'vA', 'vB', 'oA', 'oB')}
    del _L3_attn_all

    def _L3_xattn_setup():
        import jax, jax.numpy as jnp
        import numpy as np
        B, S, L = (2, 128, 128)
        DIM_Q, H, K, D_C, D_CQ, R = (256, 16, 128, 64, 192, 64)

        def _rope_tables(seq_len, dim, dtype):
            inv_freq = 1.0 / 10000.0 ** (jnp.arange(0, dim, 2, dtype=dtype) / dim)
            t = jnp.arange(seq_len, dtype=dtype)
            freqs = t[:, None] * inv_freq[None, :]
            sin = jnp.repeat(jnp.sin(freqs), 2, axis=-1)
            cos = jnp.repeat(jnp.cos(freqs), 2, axis=-1)
            return (sin, cos)

        def _rotate_half(x):
            h = x.shape[-1] // 2
            return jnp.concatenate([-x[..., h:], x[..., :h]], axis=-1)
        key = jax.random.key(seed)
        ks = jax.random.split(key, 8)
        s_in = 1.0 / np.sqrt(DIM_Q)
        s_k = 1.0 / np.sqrt(K)
        s_cq = 1.0 / np.sqrt(D_CQ)
        s_c = 1.0 / np.sqrt(D_C)
        return {'hidden_q': jax.random.normal(ks[0], (B, S, DIM_Q), jnp.float32), 'kv_c': jax.random.normal(ks[1], (B, L, D_C), jnp.float32), 'Wq': jax.random.normal(ks[2], (H * K, DIM_Q), jnp.float32) * s_in, 'w_kc_q': jax.random.normal(ks[3], (H, K, D_CQ), jnp.float32) * s_k, 'w_kc_kv': jax.random.normal(ks[4], (H, K, D_C), jnp.float32) * s_k, 'W_qr': jax.random.normal(ks[5], (H, D_CQ, R), jnp.float32) * s_cq / np.sqrt(R), 'W_kr': jax.random.normal(ks[6], (H, D_C, R), jnp.float32) * s_c, 'Wo': jax.random.normal(ks[7], (DIM_Q, H * K), jnp.float32) * s_k}
    _L3_xattn_all = _L3_xattn_setup()
    _L3_xattn_in = {k: v for k, v in _L3_xattn_all.items() if k in ('Wq', 'w_kc_q', 'w_kc_kv', 'W_qr', 'W_kr', 'Wo')}
    del _L3_xattn_all

    def _L3_ffn_setup():
        import jax, jax.numpy as jnp
        import numpy as np
        from jax import lax
        E = 8
        K = 2
        D = 256
        H = 176
        NS = 2
        B, T = (2, 256)
        EPS = 1e-20
        HS = H * NS

        def _silu(v):
            return v * jax.nn.sigmoid(v)
        key = jax.random.key(seed)
        ks = jax.random.split(key, 8)
        s = 0.02
        return {'x': jax.random.normal(ks[0], (B, T, D), jnp.float32), 'router_w': jax.random.normal(ks[1], (E, D), jnp.float32) * 0.006, 'wg': jax.random.normal(ks[2], (E, D, H), jnp.float32) * s, 'wu': jax.random.normal(ks[3], (E, D, H), jnp.float32) * s, 'wd': jax.random.normal(ks[4], (E, H, D), jnp.float32) * s, 'sg': jax.random.normal(ks[5], (D, HS), jnp.float32) * s, 'su': jax.random.normal(ks[6], (D, HS), jnp.float32) * s, 'sd': jax.random.normal(ks[7], (HS, D), jnp.float32) * s}
    _L3_ffn_all = _L3_ffn_setup()
    _L3_ffn_in = {k: v for k, v in _L3_ffn_all.items() if k in ('router_w', 'wg', 'wu', 'wd', 'sg', 'su', 'sd')}
    del _L3_ffn_all
    return {'x': x, 'ctx_512': ctx_512, 'L0_attn_Wq': _L0_attn_in['Wq'], 'L0_attn_Wk': _L0_attn_in['Wk'], 'L0_attn_Wv': _L0_attn_in['Wv'], 'L0_attn_Wg': _L0_attn_in['Wg'], 'L0_attn_Wc': _L0_attn_in['Wc'], 'L0_attn_bc': _L0_attn_in['bc'], 'L0_xattn_Wq': _L0_xattn_in['Wq'], 'L0_xattn_w_kc_q': _L0_xattn_in['w_kc_q'], 'L0_xattn_w_kc_kv': _L0_xattn_in['w_kc_kv'], 'L0_xattn_W_qr': _L0_xattn_in['W_qr'], 'L0_xattn_W_kr': _L0_xattn_in['W_kr'], 'L0_xattn_Wo': _L0_xattn_in['Wo'], 'L0_ffn_w_router': _L0_ffn_in['w_router'], 'L0_ffn_w_gate': _L0_ffn_in['w_gate'], 'L0_ffn_w_up': _L0_ffn_in['w_up'], 'L0_ffn_w_down': _L0_ffn_in['w_down'], 'L0_ffn_amplitudes': _L0_ffn_in['amplitudes'], 'L0_ffn_expert_scale': _L0_ffn_in['expert_scale'], 'L0_ffn_shared_w_gate': _L0_ffn_in['shared_w_gate'], 'L0_ffn_shared_w_up': _L0_ffn_in['shared_w_up'], 'L0_ffn_shared_w_down': _L0_ffn_in['shared_w_down'], 'L1_attn_q_weight': _L1_attn_in['q_weight'], 'L1_attn_k_weight': _L1_attn_in['k_weight'], 'L1_attn_v_weight': _L1_attn_in['v_weight'], 'L1_attn_o_weight': _L1_attn_in['o_weight'], 'L1_attn_q_bias': _L1_attn_in['q_bias'], 'L1_attn_k_bias': _L1_attn_in['k_bias'], 'L1_attn_v_bias': _L1_attn_in['v_bias'], 'L1_attn_o_bias': _L1_attn_in['o_bias'], 'L1_xattn_Wq': _L1_xattn_in['Wq'], 'L1_xattn_Wkv_expand': _L1_xattn_in['Wkv_expand'], 'L1_xattn_Wout': _L1_xattn_in['Wout'], 'L1_ffn_router_w': _L1_ffn_in['router_w'], 'L1_ffn_router_bias': _L1_ffn_in['router_bias'], 'L1_ffn_Wu': _L1_ffn_in['Wu'], 'L1_ffn_Wg': _L1_ffn_in['Wg'], 'L1_ffn_Wd': _L1_ffn_in['Wd'], 'L1_ffn_Su': _L1_ffn_in['Su'], 'L1_ffn_Sg': _L1_ffn_in['Sg'], 'L1_ffn_Sd': _L1_ffn_in['Sd'], 'L2_attn_q_w': _L2_attn_in['q_w'], 'L2_attn_kv_w': _L2_attn_in['kv_w'], 'L2_attn_c_w': _L2_attn_in['c_w'], 'L2_xattn_Wq': _L2_xattn_in['Wq'], 'L2_xattn_w_kc_q': _L2_xattn_in['w_kc_q'], 'L2_xattn_w_kc_kv': _L2_xattn_in['w_kc_kv'], 'L2_xattn_W_qr': _L2_xattn_in['W_qr'], 'L2_xattn_W_kr': _L2_xattn_in['W_kr'], 'L2_xattn_Wo': _L2_xattn_in['Wo'], 'L2_ffn_gate_w': _L2_ffn_in['gate_w'], 'L2_ffn_w_gate': _L2_ffn_in['w_gate'], 'L2_ffn_w_up': _L2_ffn_in['w_up'], 'L2_ffn_w_down': _L2_ffn_in['w_down'], 'L2_ffn_sh_gate': _L2_ffn_in['sh_gate'], 'L2_ffn_sh_up': _L2_ffn_in['sh_up'], 'L2_ffn_sh_down': _L2_ffn_in['sh_down'], 'L2_ffn_se_gate_w': _L2_ffn_in['se_gate_w'], 'L3_attn_norm_w': _L3_attn_in['norm_w'], 'L3_attn_wq': _L3_attn_in['wq'], 'L3_attn_wk': _L3_attn_in['wk'], 'L3_attn_wv': _L3_attn_in['wv'], 'L3_attn_wo': _L3_attn_in['wo'], 'L3_attn_qA': _L3_attn_in['qA'], 'L3_attn_qB': _L3_attn_in['qB'], 'L3_attn_kA': _L3_attn_in['kA'], 'L3_attn_kB': _L3_attn_in['kB'], 'L3_attn_vA': _L3_attn_in['vA'], 'L3_attn_vB': _L3_attn_in['vB'], 'L3_attn_oA': _L3_attn_in['oA'], 'L3_attn_oB': _L3_attn_in['oB'], 'L3_xattn_Wq': _L3_xattn_in['Wq'], 'L3_xattn_w_kc_q': _L3_xattn_in['w_kc_q'], 'L3_xattn_w_kc_kv': _L3_xattn_in['w_kc_kv'], 'L3_xattn_W_qr': _L3_xattn_in['W_qr'], 'L3_xattn_W_kr': _L3_xattn_in['W_kr'], 'L3_xattn_Wo': _L3_xattn_in['Wo'], 'L3_ffn_router_w': _L3_ffn_in['router_w'], 'L3_ffn_wg': _L3_ffn_in['wg'], 'L3_ffn_wu': _L3_ffn_in['wu'], 'L3_ffn_wd': _L3_ffn_in['wd'], 'L3_ffn_sg': _L3_ffn_in['sg'], 'L3_ffn_su': _L3_ffn_in['su'], 'L3_ffn_sd': _L3_ffn_in['sd']}

def reference(x, ctx_512, L0_attn_Wq, L0_attn_Wk, L0_attn_Wv, L0_attn_Wg, L0_attn_Wc, L0_attn_bc, L0_xattn_Wq, L0_xattn_w_kc_q, L0_xattn_w_kc_kv, L0_xattn_W_qr, L0_xattn_W_kr, L0_xattn_Wo, L0_ffn_w_router, L0_ffn_w_gate, L0_ffn_w_up, L0_ffn_w_down, L0_ffn_amplitudes, L0_ffn_expert_scale, L0_ffn_shared_w_gate, L0_ffn_shared_w_up, L0_ffn_shared_w_down, L1_attn_q_weight, L1_attn_k_weight, L1_attn_v_weight, L1_attn_o_weight, L1_attn_q_bias, L1_attn_k_bias, L1_attn_v_bias, L1_attn_o_bias, L1_xattn_Wq, L1_xattn_Wkv_expand, L1_xattn_Wout, L1_ffn_router_w, L1_ffn_router_bias, L1_ffn_Wu, L1_ffn_Wg, L1_ffn_Wd, L1_ffn_Su, L1_ffn_Sg, L1_ffn_Sd, L2_attn_q_w, L2_attn_kv_w, L2_attn_c_w, L2_xattn_Wq, L2_xattn_w_kc_q, L2_xattn_w_kc_kv, L2_xattn_W_qr, L2_xattn_W_kr, L2_xattn_Wo, L2_ffn_gate_w, L2_ffn_w_gate, L2_ffn_w_up, L2_ffn_w_down, L2_ffn_sh_gate, L2_ffn_sh_up, L2_ffn_sh_down, L2_ffn_se_gate_w, L3_attn_norm_w, L3_attn_wq, L3_attn_wk, L3_attn_wv, L3_attn_wo, L3_attn_qA, L3_attn_qB, L3_attn_kA, L3_attn_kB, L3_attn_vA, L3_attn_vB, L3_attn_oA, L3_attn_oB, L3_xattn_Wq, L3_xattn_w_kc_q, L3_xattn_w_kc_kv, L3_xattn_W_qr, L3_xattn_W_kr, L3_xattn_Wo, L3_ffn_router_w, L3_ffn_wg, L3_ffn_wu, L3_ffn_wd, L3_ffn_sg, L3_ffn_su, L3_ffn_sd):
    import jax
    import jax.numpy as jnp

    def _L0_attn_ref(hidden_states, Wq, Wk, Wv, Wg, Wc, bc):
        import jax, jax.numpy as jnp
        import numpy as np
        H = 8
        R = 2
        D = 128
        DEG = 2
        GATE_OFFSET = 6.906768

        def _power_attention(q, k, v, log_g):
            B, T, hq, d = q.shape
            scale = 1.0 / d ** 0.5
            k = jnp.repeat(k, R, axis=2)
            v = jnp.repeat(v, R, axis=2)
            logG = jnp.cumsum(log_g, axis=1)
            logG = jnp.repeat(logG, R, axis=2)
            logG = jnp.transpose(logG, (0, 2, 1))
            qk = jnp.einsum('bthd,bshd->bhts', q, k) * scale
            a = qk ** DEG
            gate = logG[:, :, :, None] - logG[:, :, None, :]
            causal = jnp.tril(jnp.ones((T, T), dtype=bool))
            a = jnp.where(causal, a * jnp.exp(gate), 0.0)
            norm = jnp.sum(a, axis=-1) + 1e-06
            y = jnp.einsum('bhts,bshd->bthd', a, v)
            y = y / jnp.transpose(norm, (0, 2, 1))[..., None]
            return y
        B, T, C = hidden_states.shape
        q = (hidden_states @ Wq).reshape(B, T, H * R, D)
        k = (hidden_states @ Wk).reshape(B, T, H, D)
        v = (hidden_states @ Wv).reshape(B, T, H, D)
        g = hidden_states @ Wg
        log_g = jax.nn.log_sigmoid(GATE_OFFSET + g.astype(jnp.float32))
        y = _power_attention(q, k, v, log_g)
        y = y.reshape(B, T, H * R * D)
        return y @ Wc + bc

    def _L0_xattn_ref(hidden_q, kv_c, Wq, w_kc_q, w_kc_kv, W_qr, W_kr, Wo):
        import jax, jax.numpy as jnp
        import numpy as np
        B, S, L = (2, 128, 128)
        DIM_Q, H, K, D_C, D_CQ, R = (256, 16, 128, 64, 192, 64)

        def _rope_tables(length, dim):
            inv = 1.0 / 10000.0 ** (jnp.arange(0, dim, 2, dtype=jnp.float32) / dim)
            f = jnp.arange(length, dtype=jnp.float32)[:, None] * inv[None, :]
            sin = jnp.repeat(jnp.sin(f), 2, axis=-1)
            cos = jnp.repeat(jnp.cos(f), 2, axis=-1)
            return (sin, cos)

        def _rotate_half(x):
            half = x.shape[-1] // 2
            return jnp.concatenate([-x[..., half:], x[..., :half]], axis=-1)

        def _apply_rope(x, sin, cos):
            return x * cos + _rotate_half(x) * sin
        Bv, Sv, _ = hidden_q.shape
        _, Lv, _ = kv_c.shape
        q_hk = (hidden_q @ Wq.T).reshape(Bv, Sv, H, K)
        q_big = jnp.einsum('bshk,hkq->bshq', q_hk, w_kc_q)
        sin_q, cos_q = _rope_tables(Sv, D_CQ)
        q_big = _apply_rope(q_big, sin_q[None, :, None, :], cos_q[None, :, None, :])
        sin_k, cos_k = _rope_tables(Lv, D_C)
        kv_r = _apply_rope(kv_c, sin_k[None], cos_k[None])
        q_r = jnp.einsum('bshq,hqr->bhsr', q_big, W_qr)
        k_r = jnp.einsum('bld,hdr->bhlr', kv_r, W_kr)
        scores = jnp.einsum('bhsr,bhlr->bhsl', q_r, k_r)
        attn = jax.nn.softmax(scores, axis=-1)
        ctx_c = jnp.einsum('bhsl,bld->bhsd', attn, kv_r)
        ctx_lat = jnp.einsum('bhsd,hkd->bhsk', ctx_c, w_kc_kv)
        ctx = ctx_lat.transpose(0, 2, 1, 3).reshape(Bv, Sv, H * K)
        return ctx @ Wo.T

    def _L0_ffn_ref(x, w_router, w_gate, w_up, w_down, amplitudes, expert_scale, shared_w_gate, shared_w_up, shared_w_down):
        import jax, jax.numpy as jnp
        import numpy as np
        H = 256
        I = 128
        K = 8
        E = 128
        TOPK = 4
        EPS = 1e-08
        B, S, _ = x.shape
        T = B * S
        xt = x.reshape(T, H)
        probs = jax.nn.softmax(xt @ w_router, axis=-1)
        topk_p, topk_idx = jax.lax.top_k(probs, TOPK)
        topk_w = topk_p / (jnp.sum(topk_p, axis=-1, keepdims=True) + EPS)
        gate = (xt @ w_gate).reshape(T, K, I)
        up = (xt @ w_up).reshape(T, K, I)
        basis = jax.nn.silu(gate) * up
        p = amplitudes[..., 0] ** 2 + amplitudes[..., 1] ** 2
        mix = p / (jnp.sum(p, axis=-1, keepdims=True) + EPS)
        mix_sel = mix[topk_idx]
        mixed = jnp.einsum('tek,tki->tei', mix_sel, basis)
        down = jnp.einsum('tei,ih->teh', mixed, w_down)
        coeff = topk_w * expert_scale[topk_idx]
        out = jnp.einsum('teh,te->th', down, coeff)
        shared = jax.nn.silu(xt @ shared_w_gate) * (xt @ shared_w_up) @ shared_w_down
        out = out + shared
        return out.reshape(B, S, H)

    def _L1_attn_ref(hidden_states, q_weight, k_weight, v_weight, o_weight, q_bias, k_bias, v_bias, o_bias):
        import jax, jax.numpy as jnp
        import numpy as np
        EMBED = 256
        HEADS = 32
        HEAD_DIM = EMBED // HEADS
        Q_BITS = 4
        Q_MAX = 2 ** (Q_BITS - 1) - 1
        DECOMP = 8
        CHUNK = 32

        def _sym_qdq(x, scale):
            s = jnp.clip(jnp.abs(scale), 1e-09, None)
            return jnp.clip(jnp.round(x / s), -(Q_MAX + 1), Q_MAX) * s

        def _quant_weight(w):
            w = w.astype(jnp.float32)
            s = jnp.max(jnp.abs(w), axis=-1, keepdims=True) / Q_MAX
            return _sym_qdq(w, s)

        def _chunk_decompose(x2d):
            T, H = x2d.shape
            chunks = (T + CHUNK - 1) // CHUNK
            pad = chunks * CHUNK - T
            xp = jnp.pad(x2d, ((0, pad), (0, 0))).reshape(chunks, CHUNK, H).astype(jnp.float32)
            ch_bias = (jnp.max(xp, axis=1, keepdims=True) + jnp.min(xp, axis=1, keepdims=True)) / 2
            xz = xp - ch_bias
            tmax = jnp.max(jnp.abs(xz), axis=(1, 2))
            cmax = jnp.max(jnp.abs(xz), axis=1)
            thr = tmax[:, None] / 2.0 ** jnp.arange(DECOMP - 1, -1, -1, dtype=jnp.float32)
            idx = jnp.sum(cmax[:, :, None] > thr[:, None, :DECOMP - 1], axis=-1)
            scale = tmax[:, None] / 2.0 ** (DECOMP - 1 - idx).astype(jnp.float32) / Q_MAX
            result = _sym_qdq(xz, scale[:, None, :])
            return (result, ch_bias, T)
        bsz, tgt, H = hidden_states.shape
        WQ = _quant_weight(q_weight).T
        WK = _quant_weight(k_weight).T
        WV = _quant_weight(v_weight).T
        WO = _quant_weight(o_weight).T
        result, ch_bias, n = _chunk_decompose(hidden_states.reshape(bsz * tgt, H))

        def proj(w_orig, w_dq_t, b):
            y = result @ w_dq_t + ch_bias @ w_orig.astype(jnp.float32).T
            return y.reshape(-1, H)[:n] + b
        scaling = HEAD_DIM ** (-0.5)
        Q = (proj(q_weight, WQ, q_bias) * scaling).reshape(bsz, tgt, HEADS, HEAD_DIM)
        K = proj(k_weight, WK, k_bias).reshape(bsz, tgt, HEADS, HEAD_DIM)
        V = proj(v_weight, WV, v_bias).reshape(bsz, tgt, HEADS, HEAD_DIM)
        attn = jnp.einsum('bqhd,bkhd->bhqk', Q, K)
        probs = jax.nn.softmax(attn, axis=-1)
        ctx = jnp.einsum('bhqk,bkhd->bqhd', probs, V).reshape(bsz * tgt, H)
        r2, cb2, n2 = _chunk_decompose(ctx)
        out = (r2 @ WO + cb2 @ o_weight.astype(jnp.float32).T).reshape(-1, H)[:n2] + o_bias
        return out.reshape(bsz, tgt, H)

    def _L1_xattn_ref(q, latent_kv, Wq, Wkv_expand, Wout):
        import jax, jax.numpy as jnp
        import numpy as np
        B, S, H, NH, L = (2, 256, 256, 16, 64)
        HD = H // NH
        b, sq, _ = q.shape
        sk = latent_kv.shape[1]
        qp = q @ Wq.T
        kv = latent_kv @ Wkv_expand.T
        k, v = jnp.split(kv, 2, axis=-1)
        qh = qp.reshape(b, sq, NH, HD).transpose(0, 2, 1, 3)
        kh = k.reshape(b, sk, NH, HD).transpose(0, 2, 1, 3)
        vh = v.reshape(b, sk, NH, HD).transpose(0, 2, 1, 3)
        inv_sqrt_d = 1.0 / jnp.sqrt(jnp.float32(HD))
        scores = jnp.einsum('bhqd,bhkd->bhqk', qh, kh) * inv_sqrt_d
        causal = jnp.tril(jnp.ones((sq, sk), dtype=bool))
        scores = jnp.where(causal, scores, jnp.finfo(scores.dtype).min)
        attn = jax.nn.softmax(scores, axis=-1)
        out = jnp.einsum('bhqk,bhkd->bhqd', attn, vh)
        out = out.transpose(0, 2, 1, 3).reshape(b, sq, H)
        return out @ Wout.T

    def _L1_ffn_ref(x, router_w, router_bias, Wu, Wg, Wd, Su, Sg, Sd):
        import jax, jax.numpy as jnp
        import numpy as np
        DIM = 256
        EXPERT_DIM = 128
        N_EXPERTS = 16
        TOPK = 2
        N_SHARED = 1
        B, T = (4, 256)
        Bx, Tx, D = x.shape
        flat = x.reshape(Bx * Tx, D)
        logits = flat @ router_w.T
        scores = jax.nn.softmax(logits, axis=-1)
        _, topk_idx = jax.lax.top_k(logits + router_bias, TOPK)
        topk_scores = jnp.take_along_axis(scores, topk_idx, axis=-1)
        topk_scores = topk_scores / topk_scores.sum(-1, keepdims=True)
        combine = jnp.einsum('nk,nke->ne', topk_scores, jax.nn.one_hot(topk_idx, N_EXPERTS, dtype=scores.dtype))
        out = jnp.zeros_like(flat)
        for e in range(N_EXPERTS):
            h = jax.nn.silu(flat @ Wu[e]) * (flat @ Wg[e])
            out = out + combine[:, e:e + 1] * (h @ Wd[e])
        for s in range(N_SHARED):
            out = out + jax.nn.silu(flat @ Su[s]) * (flat @ Sg[s]) @ Sd[s]
        return out.reshape(Bx, Tx, D)

    def _L2_attn_ref(x, q_w, kv_w, c_w):
        import jax, jax.numpy as jnp
        import numpy as np
        import math
        D_MODEL = 256
        N_HEADS = 16
        N_KV_HEADS = 4
        MAX_SEQ_LEN = 256
        ROPE_THETA = 10000.0
        DK = D_MODEL // N_HEADS
        B, T = (2, 256)

        def rope_tables(T, dk, theta, dtype=jnp.float32):
            pairs = jnp.arange(dk // 2, dtype=dtype)
            freqs = 1.0 / theta ** (2.0 * pairs / dk)
            pos = jnp.arange(T, dtype=dtype)
            angles = pos[:, None] * freqs[None, :]
            return (jnp.cos(angles), jnp.sin(angles))

        def apply_rope(t, cos, sin):
            te = t[..., 0::2]
            to = t[..., 1::2]
            oe = te * cos - to * sin
            oo = te * sin + to * cos
            return jnp.stack([oe, oo], axis=-1).reshape(t.shape)
        Bx, Tx, _ = x.shape
        H, HKV, dk = (N_HEADS, N_KV_HEADS, DK)
        rep = H // HKV
        q = x @ q_w.T
        kv = x @ kv_w.T
        k, v = jnp.split(kv, 2, axis=-1)
        q = q.reshape(Bx, Tx, H, dk).transpose(0, 2, 1, 3)
        k = k.reshape(Bx, Tx, HKV, dk).transpose(0, 2, 1, 3)
        v = v.reshape(Bx, Tx, HKV, dk).transpose(0, 2, 1, 3)
        cos, sin = rope_tables(Tx, dk, ROPE_THETA, x.dtype)
        q = apply_rope(q, cos, sin)
        k = apply_rope(k, cos, sin)
        k_ctx = jnp.repeat(k, rep, axis=1)
        v_ctx = jnp.repeat(v, rep, axis=1)
        logits = jnp.einsum('bhqd,bhkd->bhqk', q, k_ctx) / math.sqrt(dk)
        row = jnp.arange(Tx)
        mask = jnp.where(row[None, :] > row[:, None], -jnp.inf, 0.0).astype(x.dtype)
        logits = logits + mask[None, None]
        probs = jax.nn.softmax(logits, axis=-1)
        out = jnp.einsum('bhqk,bhkd->bhqd', probs, v_ctx)
        out = out.transpose(0, 2, 1, 3).reshape(Bx, Tx, D_MODEL)
        return out @ c_w.T

    def _L2_xattn_ref(hidden_q, kv_c, Wq, w_kc_q, w_kc_kv, W_qr, W_kr, Wo):
        import jax, jax.numpy as jnp
        import numpy as np
        B, S, L = (2, 128, 128)
        DIM_Q, H, K, D_C, D_CQ, R = (256, 16, 128, 64, 192, 64)

        def _rope_tables(length, dim):
            inv = 1.0 / 10000.0 ** (jnp.arange(0, dim, 2, dtype=jnp.float32) / dim)
            f = jnp.arange(length, dtype=jnp.float32)[:, None] * inv[None, :]
            sin = jnp.repeat(jnp.sin(f), 2, axis=-1)
            cos = jnp.repeat(jnp.cos(f), 2, axis=-1)
            return (sin, cos)

        def _rotate_half(x):
            half = x.shape[-1] // 2
            return jnp.concatenate([-x[..., half:], x[..., :half]], axis=-1)

        def _apply_rope(x, sin, cos):
            return x * cos + _rotate_half(x) * sin
        Bv, Sv, _ = hidden_q.shape
        _, Lv, _ = kv_c.shape
        q_hk = (hidden_q @ Wq.T).reshape(Bv, Sv, H, K)
        q_big = jnp.einsum('bshk,hkq->bshq', q_hk, w_kc_q)
        sin_q, cos_q = _rope_tables(Sv, D_CQ)
        q_big = _apply_rope(q_big, sin_q[None, :, None, :], cos_q[None, :, None, :])
        sin_k, cos_k = _rope_tables(Lv, D_C)
        kv_r = _apply_rope(kv_c, sin_k[None], cos_k[None])
        q_r = jnp.einsum('bshq,hqr->bhsr', q_big, W_qr)
        k_r = jnp.einsum('bld,hdr->bhlr', kv_r, W_kr)
        scores = jnp.einsum('bhsr,bhlr->bhsl', q_r, k_r)
        attn = jax.nn.softmax(scores, axis=-1)
        ctx_c = jnp.einsum('bhsl,bld->bhsd', attn, kv_r)
        ctx_lat = jnp.einsum('bhsd,hkd->bhsk', ctx_c, w_kc_kv)
        ctx = ctx_lat.transpose(0, 2, 1, 3).reshape(Bv, Sv, H * K)
        return ctx @ Wo.T

    def _L2_ffn_ref(x, gate_w, w_gate, w_up, w_down, sh_gate, sh_up, sh_down, se_gate_w):
        import jax, jax.numpy as jnp
        import numpy as np
        N_EXPERTS = 8
        TOP_K = 2
        C = 256
        H = 128
        HS = 256
        B, T = (1, 64)
        SCALE = 0.02
        Bb, Tt, Cc = x.shape
        xf = x.reshape(-1, Cc)
        scores = xf @ gate_w.T
        ew, ei = jax.lax.top_k(scores, TOP_K)
        ew = jax.nn.softmax(ew, axis=-1)
        x1 = jax.nn.silu(jnp.einsum('td,ehd->teh', xf, w_gate))
        x3 = jnp.einsum('td,ehd->teh', xf, w_up)
        expert_out = jnp.einsum('teh,edh->ted', x1 * x3, w_down)
        onehot = jax.nn.one_hot(ei, N_EXPERTS, dtype=ew.dtype)
        comb = jnp.einsum('ta,tae->te', ew, onehot)
        routed = jnp.einsum('te,ted->td', comb, expert_out)
        shared = jax.nn.silu(xf @ sh_gate.T) * (xf @ sh_up.T) @ sh_down.T
        sgate = jax.nn.sigmoid(xf @ se_gate_w.T)
        return (routed + sgate * shared).reshape(Bb, Tt, Cc)

    def _L3_attn_ref(x, norm_w, wq, wk, wv, wo, qA, qB, kA, kB, vA, vB, oA, oB):
        import jax, jax.numpy as jnp
        import numpy as np
        import math
        B, L, D = (2, 256, 256)
        H, DH = (16, 128)
        R = 16
        WIN = 64
        EPS = 1e-06

        def _lora_proj(h, Wb, A, Bm, scale):
            return h @ Wb.T + h @ A.T @ Bm.T * scale

        def _rope_freqs(seq_len, d_head):
            half = d_head // 2
            theta = 1.0 / 10000.0 ** (jnp.arange(half, dtype=jnp.float32) / half)
            freqs = jnp.arange(seq_len, dtype=jnp.float32)[:, None] * theta[None, :]
            emb = jnp.concatenate([freqs, freqs], axis=-1)
            return (jnp.cos(emb), jnp.sin(emb))

        def _apply_rope(x, cos, sin):
            half = x.shape[-1] // 2
            x1, x2 = (x[..., :half], x[..., half:])
            rotated = jnp.concatenate([-x2, x1], axis=-1)
            return x * cos[None, None] + rotated * sin[None, None]
        lora_scale = 1.0 / qA.shape[0]
        residual = x
        h = x * jax.lax.rsqrt(jnp.mean(x * x, axis=-1, keepdims=True) + EPS) * norm_w
        Q = _lora_proj(h, wq, qA, qB, lora_scale)
        K = _lora_proj(h, wk, kA, kB, lora_scale)
        V = _lora_proj(h, wv, vA, vB, lora_scale)
        b, l, _ = x.shape
        Q = Q.reshape(b, l, H, DH).transpose(0, 2, 1, 3)
        K = K.reshape(b, l, H, DH).transpose(0, 2, 1, 3)
        V = V.reshape(b, l, H, DH).transpose(0, 2, 1, 3)
        cos, sin = _rope_freqs(l, DH)
        Q = _apply_rope(Q, cos, sin)
        K = _apply_rope(K, cos, sin)
        i = jnp.arange(l)[:, None]
        j = jnp.arange(l)[None, :]
        valid = (j <= i) & (j >= i - WIN + 1)
        mask = jnp.where(valid, 0.0, -jnp.inf).astype(x.dtype)
        scores = jnp.einsum('bhqd,bhkd->bhqk', Q, K) / math.sqrt(DH)
        attn = jax.nn.softmax(scores + mask[None, None], axis=-1)
        out = jnp.einsum('bhqk,bhkd->bhqd', attn, V)
        out = out.transpose(0, 2, 1, 3).reshape(b, l, H * DH)
        out = _lora_proj(out, wo, oA, oB, lora_scale)
        return residual + out

    def _L3_xattn_ref(hidden_q, kv_c, Wq, w_kc_q, w_kc_kv, W_qr, W_kr, Wo):
        import jax, jax.numpy as jnp
        import numpy as np
        B, S, L = (2, 128, 128)
        DIM_Q, H, K, D_C, D_CQ, R = (256, 16, 128, 64, 192, 64)

        def _rope_tables(seq_len, dim, dtype):
            inv_freq = 1.0 / 10000.0 ** (jnp.arange(0, dim, 2, dtype=dtype) / dim)
            t = jnp.arange(seq_len, dtype=dtype)
            freqs = t[:, None] * inv_freq[None, :]
            sin = jnp.repeat(jnp.sin(freqs), 2, axis=-1)
            cos = jnp.repeat(jnp.cos(freqs), 2, axis=-1)
            return (sin, cos)

        def _rotate_half(x):
            h = x.shape[-1] // 2
            return jnp.concatenate([-x[..., h:], x[..., :h]], axis=-1)
        b, s, _ = hidden_q.shape
        l = kv_c.shape[1]
        q_hk = (hidden_q @ Wq.T).reshape(b, s, H, K)
        q_big = jnp.einsum('bshk,hkq->bshq', q_hk, w_kc_q)
        sin, cos = _rope_tables(l, D_C, kv_c.dtype)
        kv_rope = kv_c * cos[None] + _rotate_half(kv_c) * sin[None]
        q_r = jnp.einsum('bshq,hqr->bhsr', q_big, W_qr)
        k_r = jnp.einsum('bld,hdr->bhlr', kv_rope, W_kr)
        scores = jnp.einsum('bhsr,bhlr->bhsl', q_r, k_r)
        attn = jax.nn.softmax(scores, axis=-1)
        ctx_c = jnp.einsum('bhsl,bld->bhsd', attn, kv_rope)
        ctx_lat = jnp.einsum('bhsd,hkd->bshk', ctx_c, w_kc_kv)
        out = ctx_lat.reshape(b, s, H * K) @ Wo.T
        return out

    def _L3_ffn_ref(x, router_w, wg, wu, wd, sg, su, sd):
        import jax, jax.numpy as jnp
        import numpy as np
        from jax import lax
        E = 8
        K = 2
        D = 256
        H = 176
        NS = 2
        B, T = (2, 256)
        EPS = 1e-20
        HS = H * NS

        def _silu(v):
            return v * jax.nn.sigmoid(v)
        b, t, d = x.shape
        xf = x.reshape(b * t, d)
        n = xf.shape[0]
        gates = jax.nn.softmax(xf @ router_w.T, axis=-1)
        topv, topi = lax.top_k(gates, K)
        masked = jnp.zeros_like(gates).at[jnp.arange(n)[:, None], topi].set(topv)
        masked = masked / (masked.sum(axis=-1, keepdims=True) + EPS)

        def step(acc, p):
            wg_e, wu_e, wd_e, g_e = p
            y = _silu(xf @ wg_e) * (xf @ wu_e) @ wd_e
            return (acc + y * g_e[:, None], None)
        routed, _ = lax.scan(step, jnp.zeros_like(xf), (wg, wu, wd, masked.T))
        shared = _silu(xf @ sg) * (xf @ su) @ sd
        return (routed + shared).reshape(b, t, d)
    x = _layernorm(x + _L0_attn_ref(x, L0_attn_Wq, L0_attn_Wk, L0_attn_Wv, L0_attn_Wg, L0_attn_Wc, L0_attn_bc), axis=-1)
    x = _layernorm(x + _L0_xattn_ref(x, ctx_512, L0_xattn_Wq, L0_xattn_w_kc_q, L0_xattn_w_kc_kv, L0_xattn_W_qr, L0_xattn_W_kr, L0_xattn_Wo), axis=-1)
    x = _layernorm(x + _L0_ffn_ref(x, L0_ffn_w_router, L0_ffn_w_gate, L0_ffn_w_up, L0_ffn_w_down, L0_ffn_amplitudes, L0_ffn_expert_scale, L0_ffn_shared_w_gate, L0_ffn_shared_w_up, L0_ffn_shared_w_down), axis=-1)
    x = _layernorm(x + _L1_attn_ref(x, L1_attn_q_weight, L1_attn_k_weight, L1_attn_v_weight, L1_attn_o_weight, L1_attn_q_bias, L1_attn_k_bias, L1_attn_v_bias, L1_attn_o_bias), axis=-1)
    x = _layernorm(x + _L1_xattn_ref(x, ctx_512, L1_xattn_Wq, L1_xattn_Wkv_expand, L1_xattn_Wout), axis=-1)
    x = _layernorm(x + _L1_ffn_ref(x, L1_ffn_router_w, L1_ffn_router_bias, L1_ffn_Wu, L1_ffn_Wg, L1_ffn_Wd, L1_ffn_Su, L1_ffn_Sg, L1_ffn_Sd), axis=-1)
    x = _layernorm(x + _L2_attn_ref(x, L2_attn_q_w, L2_attn_kv_w, L2_attn_c_w), axis=-1)
    x = _layernorm(x + _L2_xattn_ref(x, ctx_512, L2_xattn_Wq, L2_xattn_w_kc_q, L2_xattn_w_kc_kv, L2_xattn_W_qr, L2_xattn_W_kr, L2_xattn_Wo), axis=-1)
    x = _layernorm(x + _L2_ffn_ref(x, L2_ffn_gate_w, L2_ffn_w_gate, L2_ffn_w_up, L2_ffn_w_down, L2_ffn_sh_gate, L2_ffn_sh_up, L2_ffn_sh_down, L2_ffn_se_gate_w), axis=-1)
    x = _layernorm(x + _L3_attn_ref(x, L3_attn_norm_w, L3_attn_wq, L3_attn_wk, L3_attn_wv, L3_attn_wo, L3_attn_qA, L3_attn_qB, L3_attn_kA, L3_attn_kB, L3_attn_vA, L3_attn_vB, L3_attn_oA, L3_attn_oB), axis=-1)
    x = _layernorm(x + _L3_xattn_ref(x, ctx_512, L3_xattn_Wq, L3_xattn_w_kc_q, L3_xattn_w_kc_kv, L3_xattn_W_qr, L3_xattn_W_kr, L3_xattn_Wo), axis=-1)
    x = _layernorm(x + _L3_ffn_ref(x, L3_ffn_router_w, L3_ffn_wg, L3_ffn_wu, L3_ffn_wd, L3_ffn_sg, L3_ffn_su, L3_ffn_sd), axis=-1)
    return x

_drawn_inputs = setup_inputs


def setup_inputs(seed=0):
    import zlib

    import numpy as np

    out = dict(_drawn_inputs(seed))
    spreads = {'L0_attn_bc': (0.0, 0.1),
     'L0_ffn_expert_scale': (1.0, 0.6),
     'L1_ffn_router_bias': (0.0, 0.8),
     'L3_attn_norm_w': (1.0, 0.2)}
    factors = {'L0_attn_Wg': 8.0,
     'L0_ffn_w_router': 8.0,
     'L0_ffn_w_gate': 8.0,
     'L0_ffn_w_up': 8.0,
     'L0_ffn_w_down': 8.0,
     'L0_ffn_amplitudes': 8.0,
     'L0_ffn_shared_w_gate': 4.275,
     'L0_ffn_shared_w_up': 4.323,
     'L0_ffn_shared_w_down': 4.208,
     'L1_attn_q_weight': 8.0,
     'L1_attn_k_weight': 8.0,
     'L1_attn_q_bias': 8.0,
     'L1_attn_k_bias': 8.0,
     'L1_attn_v_bias': 6.934,
     'L1_xattn_Wq': 8.0,
     'L1_ffn_router_w': 8.0,
     'L1_ffn_Wu': 8.0,
     'L1_ffn_Wg': 8.0,
     'L1_ffn_Wd': 8.0,
     'L1_ffn_Su': 4.268,
     'L1_ffn_Sg': 4.257,
     'L1_ffn_Sd': 4.226,
     'L2_ffn_gate_w': 8.0,
     'L2_ffn_w_gate': 8.0,
     'L2_ffn_w_up': 8.0,
     'L2_ffn_w_down': 8.0,
     'L2_ffn_sh_gate': 8.0,
     'L2_ffn_sh_up': 8.0,
     'L2_ffn_sh_down': 8.0,
     'L2_ffn_se_gate_w': 8.0,
     'L3_attn_qA': 8.0,
     'L3_attn_qB': 8.0,
     'L3_attn_kA': 8.0,
     'L3_attn_kB': 8.0,
     'L3_attn_vA': 8.0,
     'L3_attn_vB': 8.0,
     'L3_attn_oA': 8.0,
     'L3_attn_oB': 8.0,
     'L3_ffn_router_w': 6.876,
     'L3_ffn_wg': 5.803,
     'L3_ffn_wu': 5.651,
     'L3_ffn_wd': 5.689,
     'L3_ffn_sg': 2.904,
     'L3_ffn_su': 2.848,
     'L3_ffn_sd': 2.883}
    for name, (base, spread) in spreads.items():
        noise = np.random.default_rng([zlib.crc32(name.encode()), seed]).standard_normal(out[name].shape)
        drawn = base * np.exp(spread * noise) if base else spread * noise
        out[name] = jnp.asarray(drawn.astype(out[name].dtype))
    for name, factor in factors.items():
        out[name] = (out[name] * factor).astype(out[name].dtype)
    return out
```

```python
import concourse.bass as bass
from concourse import mybir
from contextlib import ExitStack

F32 = mybir.dt.float32
ALU = mybir.AluOpType
ACT = mybir.ActivationFunctionType
AX = mybir.AxisListType

B, T, D = 8, 56, 256
TP = 64
NT = B * T
J = B // 2
KT = D // 128
L, LC, LT = 1500, 64, 12
LP = L // LT
ARENA = 37800

class Sem:

    def __init__(self, handle):
        self.handle = handle
        self.base = 0
        self.n = 0

    def next(self):
        self.n += 1
        return self.handle, 1

    def at(self, k):
        return self.base + k

    def last(self):
        return self.base + self.n


class Core:

    def __init__(self, nc, ctx, dram):
        self.nc, self.ctx, self.dram = nc, ctx, dram
        sb = lambda name, shape: ctx.enter_context(nc.sbuf_tensor(name, shape, F32))
        self.arena = sb("arena", [128, ARENA])
        self.x_tok = sb("x_tok", [128, J, D])
        self.x_feat = sb("x_feat", [128, KT, B, TP])
        self.ctx_pos = sb("ctx_pos", [LP, J, LT, 2, LC])
        self.ctx_feat = sb("ctx_feat", [128, J, L])
        self.ident = sb("ident", [128, 128])
        self.heads8 = sb("heads8", [128, 4])
        self.heads16 = sb("heads16", [128, 2])
        self.stats = sb("stats", [128, J, 6])
        self.mv = sb("mv", [128, J, 2])
        self.std = sb("std", [128, J])
        self.rstd = sb("rstd", [128, J])
        self.ps = ctx.enter_context(nc.psum_tensor("ps", [128, 8, 512], F32))
        self.loaded = {}
        self.shared, self.taken = [], 0

    def at(self, off, n, parts=128):
        assert off + n <= ARENA, (off, n)
        return self.arena[0:parts, off:off + n]

    def sem(self, name):
        return Sem(self.ctx.enter_context(self.nc.semaphore(name)))

    def stage_sem(self):
        if self.taken == len(self.shared):
            self.shared.append(self.sem("stage_%d" % self.taken))
        self.taken += 1
        sem = self.shared[self.taken - 1]
        sem.base, sem.n = sem.base + sem.n, 0
        return sem

    def load(self, eng, group, items):
        if group not in self.loaded:
            self.loaded[group] = self.sem("load_" + group)
        for name, dst in items:
            eng.dma_start(dst, self.dram[name]).then_inc(self.loaded[group].handle, 16)
            self.loaded[group].n += 16


class Stage:

    def __init__(self, c, name):
        self.c, self.name = c, name
        c.taken = 0
        self.dve_chain = c.stage_sem()
        self.act_chain = c.stage_sem()
        self.y_done = c.stage_sem()
        self.var_ready = c.stage_sem()
        self.std_ready = c.stage_sem()
        self.x_normed = c.stage_sem()
        self.x_turned = c.stage_sem()

    def sem(self, what):
        return self.c.stage_sem()



def norm_vector(c, s, dve, last):
    dve.wait_ge(s.y_done.handle, s.y_done.at(1))
    x2 = c.x_tok[:].rearrange("p (a b) d -> p a (b d)", a=2)
    c.nc.vector.tensor_tensor(x2, c.ps[:, 0:2, :], x2, ALU.add).then_inc(*s.dve_chain.next())
    dve.wait_ge(s.dve_chain.handle, s.dve_chain.last())
    for j in range(J):
        c.nc.vector.bn_stats(c.stats[:, j, :], c.x_tok[:, j, :]).then_inc(*s.dve_chain.next())
        dve.wait_ge(s.dve_chain.handle, s.dve_chain.last())
    for j in range(J):
        c.nc.vector.bn_aggr(c.mv[:, j, :], c.stats[:, j, :]).then_inc(*s.dve_chain.next())
        dve.wait_ge(s.dve_chain.handle, s.dve_chain.last())
    c.nc.vector.tensor_scalar(c.std[:], c.mv[:, :, 1], 1e-5, None, ALU.add).then_inc(*s.var_ready.next())
    dve.wait_ge(s.var_ready.handle, s.var_ready.last())
    dve.wait_ge(s.std_ready.handle, s.std_ready.at(1))
    c.nc.vector.reciprocal(c.rstd[:], c.std[:]).then_inc(*s.dve_chain.next())
    dve.wait_ge(s.dve_chain.handle, s.dve_chain.last())
    for j in range(J):
        c.nc.vector.tensor_scalar(c.x_tok[:, j, :], c.x_tok[:, j, :], c.mv[:, j, 0:1], c.rstd[:, j:j + 1],
                                       ALU.subtract, ALU.mult).then_inc(*s.x_normed.next())
        dve.wait_ge(s.x_normed.handle, s.x_normed.last())
    if not last:
        dve.wait_ge(s.x_turned.handle, s.x_turned.at(1))
        c.nc.vector.tensor_copy(c.x_feat[:, 1, :, :], c.ps[:, 3, :].rearrange("p (b t) -> p b t", b=B)).then_inc(*s.dve_chain.next())
        dve.wait_ge(s.dve_chain.handle, s.dve_chain.last())


def norm_scalar(c, s, act, last):
    act.wait_ge(s.var_ready.handle, s.var_ready.at(1))
    c.nc.scalar.activation(c.std[:], c.std[:], ACT.Sqrt).then_inc(*s.std_ready.next())
    act.wait_ge(s.std_ready.handle, s.std_ready.last())
    if not last:
        act.wait_ge(s.x_turned.handle, s.x_turned.at(1))
        c.nc.scalar.copy(c.x_feat[:, 0, :, :], c.ps[:, 2, :].rearrange("p (b t) -> p b t", b=B)).then_inc(*s.act_chain.next())
        act.wait_ge(s.act_chain.handle, s.act_chain.last())


def norm_tensor(c, s, pe, last):
    if last:
        return
    for j in range(J):
        pe.wait_ge(s.x_normed.handle, s.x_normed.at(j + 1))
        for k in range(KT):
            t = c.nc.tensor.transpose(c.ps[:, 2 + k, j * 128:(j + 1) * 128],
                                      c.x_tok[:, j, k * 128:(k + 1) * 128], c.ident[:])
    t.then_inc(*s.x_turned.next())


def norm_store(c, s, sp, out):
    rows = out.rearrange("(j h) t d -> h t j d", h=2)
    sp.wait_ge(s.x_normed.handle, s.x_normed.at(J))
    stored = s.sem("stored")
    for h in range(2):
        sp.dma_start(rows[h], c.x_tok[h * TP:h * TP + T, :, :]).then_inc(stored.handle, 16)
    sp.wait_ge(stored.handle, stored.at(32))


def valid(ap):
    return ap.rearrange("p (b t) -> p b t", b=B)


def project_out(c, pe, j, k, lhsT, rhs, first, last):
    return c.nc.tensor.matmul(c.ps[:, j // 2, (j % 2) * D:(j % 2 + 1) * D], lhsT, rhs,
                              start=first and j % 2 == 0, stop=last, skip_group_check=True)



def context_stage(c):
    nc, s = c.nc, Stage(c, "context")
    raw = c.at(13312, J * LT * 2 * LC, LP).rearrange("p (j l h d) -> p j l h d", j=J, l=LT, h=2)
    turned = c.at(19456, J * LT * 2 * LC, LP).rearrange("p (j l h d) -> p j l h d", j=J, l=LT, h=2)
    cos = c.at(25600, LT * LC, LP)
    sin = c.at(26368, LT * LC, LP)
    rotated, flipped, kept = s.sem("rotated"), s.sem("flipped"), s.sem("kept")
    GROUPS = LT // 4

    with nc.Block(no_gpsimd_drain=True) as block:
        @block.sync
        def _(sp):
            c.load(sp, "context", [("ctx", c.at(13312, 6144, LP)), ("ctx_cos", cos), ("ctx_sin", sin)])
            c.load(sp, "common", [("ident", c.ident[:]), ("heads8", c.heads8[:]), ("heads16", c.heads16[:]),
                                  ("x_tok", c.x_tok[:].rearrange("p j d -> p (j d)")),
                                  ("x_feat", c.x_feat[:].rearrange("p k b t -> p (k b t)"))])
            c.load(sp, "L0_attn", L0_ATTN_LOADS(c))

        @block.vector
        def _(dve):
            dve.wait_ge(c.loaded["context"].handle, 16 * 3)
            co = cos.rearrange("p (l o d) -> p l o d", l=LT, o=1).broadcast_to([LP, LT, 2, LC])
            sn = sin.rearrange("p (l o d) -> p l o d", l=LT, o=1).broadcast_to([LP, LT, 2, LC])
            for j in range(J):
                nc.vector.tensor_tensor(c.ctx_pos[:, j], raw[:, j], co, ALU.mult).then_inc(*s.dve_chain.next())
                nc.vector.tensor_tensor(turned[:, j, :, :, 0:32], raw[:, j, :, :, 32:64], sn[:, :, :, 0:32],
                                               ALU.mult).then_inc(*s.dve_chain.next())
                nc.vector.tensor_tensor(turned[:, j, :, :, 32:64], raw[:, j, :, :, 0:32], sn[:, :, :, 32:64],
                                             ALU.mult).then_inc(*s.dve_chain.next())
                dve.wait_ge(s.dve_chain.handle, s.dve_chain.last())
                nc.vector.tensor_tensor(c.ctx_pos[:, j], c.ctx_pos[:, j], turned[:, j], ALU.add).then_inc(*rotated.next())
                dve.wait_ge(rotated.handle, rotated.last())

        @block.tensor
        def _(pe):
            pe.wait_ge(c.loaded["common"].handle, 16 * 5)
            for n in range(J * GROUPS):
                j, g = n // GROUPS, n % GROUPS
                pe.wait_ge(rotated.handle, rotated.at(j + 1))
                if n - 7 > 0:
                    pe.wait_ge(kept.handle, kept.at(n - 7))
                for i in range(4):
                    t = nc.tensor.transpose(c.ps[:, n % 8, i * LP:(i + 1) * LP],
                                            c.ctx_pos[:, j, 4 * g + i, :, :], c.ident[0:LP, 0:LP])
                t.then_inc(*flipped.next())

        @block.scalar
        def _(act):
            for n in range(J * GROUPS):
                j, g = n // GROUPS, n % GROUPS
                act.wait_ge(flipped.handle, flipped.at(n + 1))
                nc.scalar.copy(c.ctx_feat[:, j, g * 4 * LP:(g + 1) * 4 * LP], c.ps[:, n % 8, 0:4 * LP]).then_inc(*kept.next())
            if kept.n > 0:
                act.wait_ge(kept.handle, kept.at(kept.n))



GH, HD = 8, 128


def L0_ATTN_LOADS(c):
    return [("L0a_Wk", c.at(4096, 2048)), ("L0a_Wq", c.at(0, 4096)), ("L0a_Wv", c.at(6144, 2048)),
            ("L0a_Wg", c.at(12288, 16)), ("L0a_after", c.at(12304, 128)), ("L0a_half", c.at(12432, 256)),
            ("L0a_tri", c.at(12688, T)), ("L0a_causal", c.at(12744, T)), ("L0a_bc", c.at(12800, D)),
            ("L0a_Wc", c.at(8192, 4096))]


def l0_attention(c, prefetch):
    nc, s = c.nc, Stage(c, "L0_attn")
    wq = c.at(0, 4096).rearrange("p (k n) -> p k n", k=KT)
    wk = c.at(4096, 2048).rearrange("p (k n) -> p k n", k=KT)
    wv = c.at(6144, 2048).rearrange("p (k n) -> p k n", k=KT)
    wc = c.at(8192, 4096).rearrange("p (h n) -> p h n", h=2 * GH)
    wg = c.at(12288, 16).rearrange("p (k n) -> p k n", k=KT)
    later = c.at(12304, 128)
    half = c.at(12432, 256).rearrange("p (h m) -> p h m", h=2)
    tri = c.at(12688, T)
    causal = c.at(12744, T)
    bias = c.at(12800, D)
    kT = c.at(13312, 4096).rearrange("p (g b t) -> p g b t", g=GH, b=B)
    qT = c.at(17408, 7168).rearrange("p (h b t) -> p h b t", h=2 * GH, b=B)
    v = c.at(24576, 4096).rearrange("p (j n) -> p j n", j=J)
    masked = c.at(28672, 1792).rearrange("p (g j t) -> p g j t", g=GH, j=J)
    gate = c.at(30464, 1792)
    square = [c.at(32256 + 448 * i, NT) for i in range(2)]
    a = [c.at(33152 + 448 * i, NT) for i in range(2)]
    yT = [c.at(34048 + 1024 * i, 1024).rearrange("p (r b t) -> p r b t", r=2, b=B) for i in range(2)]
    rnorm = c.at(36096, 896)
    lg = c.at(36992, 32).rearrange("p (j g) -> p j g", j=J)
    lg2 = c.at(37024, 32).rearrange("p (j g) -> p j g", j=J)
    lg3 = c.at(37056, 32).rearrange("p (j g) -> p j g", j=J)
    projected = s.sem("projected")
    out_act = s.sem("copied_act")
    out_dve = s.sem("copied_dve")
    padded = s.sem("padded")
    gates_in, lg_exp, lg_in, lg_ln, masked_in = (s.sem(x) for x in ("gates", "lg_exp", "lg_in", "lg_ln", "masked"))
    diffs, gate_exp, gate_in = s.sem("diffs"), s.sem("gate_exp"), s.sem("gate_in")
    scored, squared, a_in, summed, y_in, projected_y = (
        s.sem(x) for x in ("scored", "squared", "a_in", "summed", "y_in", "projected_y"))
    banks = [("k", g) for g in range(GH)] + [("q", h) for h in range(2 * GH)] + [("v", i) for i in range(2 * J)]
    NB = len(banks)

    def copied(eng, n):
        if n >= 0:
            done = out_act if n % 2 else out_dve
            eng.wait_ge(done.handle, done.at(n // 2 + 1))

    def copy_out(n):
        kind, i = banks[n]
        bank = c.ps[:, 2 + n % 6, :]
        if kind == "k":
            return kT[:, i, :, 0:T], valid(bank[:, 0:NT])
        if kind == "q":
            return qT[:, i, :, :], valid(bank[:, 0:NT])
        return v[:, i // 2, (i % 2) * 512:(i % 2 + 1) * 512], bank

    with nc.Block(no_gpsimd_drain=True) as block:
        @block.sync
        def _(sp):
            sp.wait_ge(projected.handle, projected.at(NB))
            prefetch(sp)

        @block.gpsimd
        def _(pool):
            nc.gpsimd.memset(kT[:, :, :, T:TP], 0.0).then_inc(*padded.next())
            for i in range(2):
                nc.gpsimd.memset(yT[i][:, :, :, T:TP], 0.0).then_inc(*padded.next())
            pool.wait_ge(padded.handle, padded.at(3))

        @block.tensor
        def _(pe):
            pe.wait_ge(c.loaded["common"].handle, 16 * 5)
            pe.wait_ge(c.loaded["L0_attn"].handle, 16 * 10)
            for j in range(J):
                for k in range(KT):
                    m = nc.tensor.matmul(c.ps[:, 0, j * GH:(j + 1) * GH], c.x_feat[:, k, 2 * j:2 * j + 2, :],
                                         wg[:, k, :], start=(k == 0), stop=(k == KT - 1))
            m.then_inc(*gates_in.next())
            for n, (kind, i) in enumerate(banks):
                copied(pe, n - 6)
                for k in range(KT):
                    if kind == "v":
                        m = nc.tensor.matmul(c.ps[:, 2 + n % 6, :], c.x_feat[:, k, i // 2 * 2:i // 2 * 2 + 2, :],
                                             wv[:, k, (i % 2) * 512:(i % 2 + 1) * 512],
                                             start=(k == 0), stop=(k == KT - 1))
                    else:
                        w = wk if kind == "k" else wq
                        m = nc.tensor.matmul(c.ps[:, 2 + n % 6, 0:NT], w[:, k, i * HD:(i + 1) * HD],
                                             c.x_feat[:, k, :, 0:T], start=(k == 0), stop=(k == KT - 1))
                m.then_inc(*projected.next())
            pe.wait_ge(masked_in.handle, masked_in.at(1))
            copied(pe, NB - 2)
            copied(pe, NB - 1)
            for g in range(GH):
                m = nc.tensor.matmul(c.ps[:, 2 + g // 2, (g % 2) * 224:(g % 2 + 1) * 224], later, masked[:, g, :, :],
                                     start=True, stop=True)
            m.then_inc(*diffs.next())
            pe.wait_ge(padded.handle, padded.at(3))

            def scores(g):
                if g - 1 > 0:
                    pe.wait_ge(squared.handle, squared.at(g - 1))
                for b in range(B):
                    m = nc.tensor.matmul(c.ps[(b % 2) * TP:(b % 2 + 1) * TP, 6 + g % 2,
                                              (b // 2) * 2 * T:(b // 2 + 1) * 2 * T],
                                         kT[:, g, b, :], qT[:, 2 * g:2 * g + 2, b, :], start=True, stop=True)
                m.then_inc(*scored.next())

            def weigh(g):
                pe.wait_ge(gate_exp.handle, gate_exp.at(4))
                pe.wait_ge(a_in.handle, a_in.at(g + 1))
                if 2 * g > 0:
                    pe.wait_ge(y_in.handle, y_in.at(2 * g))
                for b in range(B):
                    h, j = b % 2, b // 2
                    nc.tensor.matmul(c.ps[:, 2 + h, j * 2 * T:(j + 1) * 2 * T],
                                     v[h * TP:h * TP + T, j, g * HD:(g + 1) * HD],
                                     a[g % 2][h * TP:h * TP + T, j * 2 * T:(j + 1) * 2 * T], start=True, stop=True)
                for h in range(2):
                    m = nc.tensor.matmul(c.ps[:, 4 + h, 0:NT], half[:, h, :], a[g % 2], start=True, stop=True)
                m.then_inc(*summed.next())

            def out(g):
                pe.wait_ge(y_in.handle, y_in.at(2 * (g + 1)))
                for r in range(2):
                    for j in range(J):
                        m = project_out(c, pe, j, r, yT[g % 2][:, r, 2 * j:2 * j + 2, :], wc[:, 2 * g + r, :],
                                        g == 0 and r == 0, g == GH - 1 and r == 1)
                m.then_inc(*projected_y.next())
                if g == GH - 1:
                    return m

            scores(0)
            for g in range(GH):
                if g + 1 < GH:
                    scores(g + 1)
                weigh(g)
                if g >= 1:
                    out(g - 1)
            out(GH - 1)
            pe.wait_ge(projected_y.handle, projected_y.at(GH))
            pe.sem_inc(*s.y_done.next())
            norm_tensor(c, s, pe, False)

        @block.scalar
        def _(act):
            act.wait_ge(lg_in.handle, lg_in.at(1))
            nc.scalar.activation(lg2, lg2, ACT.Exp, scale=-1.0).then_inc(*lg_exp.next())
            act.wait_ge(lg_exp.handle, lg_exp.last())
            act.wait_ge(lg_in.handle, lg_in.at(2))
            nc.scalar.activation(lg2, lg2, ACT.Ln).then_inc(*lg_ln.next())
            act.wait_ge(lg_ln.handle, lg_ln.last())
            for n in range(1, NB, 2):
                act.wait_ge(projected.handle, projected.at(n + 1))
                nc.scalar.copy(*copy_out(n)).then_inc(*out_act.next())
                act.wait_ge(out_act.handle, out_act.last())
            act.wait_ge(diffs.handle, diffs.at(1))
            for i in range(4):
                nc.scalar.activation(gate[:, i * 448:(i + 1) * 448], c.ps[:, 2 + i, 0:448], ACT.Exp).then_inc(*gate_exp.next())
                act.wait_ge(gate_exp.handle, gate_exp.last())
            for g in range(GH):
                act.wait_ge(scored.handle, scored.at(g + 1))
                if g - 1 > 0:
                    act.wait_ge(a_in.handle, a_in.at(g - 1))
                nc.scalar.activation(square[g % 2], c.ps[:, 6 + g % 2, 0:NT], ACT.Square, scale=HD ** -0.5).then_inc(*squared.next())
                act.wait_ge(squared.handle, squared.last())
            norm_scalar(c, s, act, False)

        @block.vector
        def _(dve):
            dve.wait_ge(gates_in.handle, gates_in.at(1))
            nc.vector.tensor_scalar(lg, c.ps[:, 0, 0:J * GH].rearrange("p (j g) -> p j g", j=J), 6.906768, None,
                                         ALU.add).then_inc(*s.dve_chain.next())
            dve.wait_ge(s.dve_chain.handle, s.dve_chain.last())
            nc.vector.tensor_scalar(lg3, lg, 0.0, None, ALU.min).then_inc(*s.dve_chain.next())
            dve.wait_ge(s.dve_chain.handle, s.dve_chain.last())
            nc.vector.scalar_tensor_tensor(out=lg2, in0=lg3, scalar=-2.0, in1=lg, op0=ALU.mult, op1=ALU.add).then_inc(*lg_in.next())
            dve.wait_ge(lg_in.handle, lg_in.last())
            dve.wait_ge(lg_exp.handle, lg_exp.at(1))
            nc.vector.tensor_scalar(lg2, lg2, 1.0, None, ALU.add).then_inc(*lg_in.next())
            dve.wait_ge(lg_in.handle, lg_in.last())
            dve.wait_ge(lg_ln.handle, lg_ln.at(1))
            nc.vector.tensor_tensor(lg, lg3, lg2, ALU.subtract).then_inc(*s.dve_chain.next())
            dve.wait_ge(s.dve_chain.handle, s.dve_chain.last())
            nc.vector.tensor_tensor(masked, lg.rearrange("p j g -> p g j").unsqueeze(3).broadcast_to([128, GH, J, T]),
                                         tri.rearrange("p (a b t) -> p a b t", a=1, b=1).broadcast_to([128, GH, J, T]),
                                         ALU.mult).then_inc(*masked_in.next())
            dve.wait_ge(masked_in.handle, masked_in.last())
            for n in range(0, NB, 2):
                dve.wait_ge(projected.handle, projected.at(n + 1))
                nc.vector.tensor_copy(*copy_out(n)).then_inc(*out_dve.next())
                dve.wait_ge(out_dve.handle, out_dve.last())
            nc.vector.tensor_tensor(c.x_tok[:], c.x_tok[:], bias.unsqueeze(1).broadcast_to([128, J, D]), ALU.add).then_inc(*s.dve_chain.next())
            dve.wait_ge(s.dve_chain.handle, s.dve_chain.last())
            dve.wait_ge(gate_exp.handle, gate_exp.at(4))
            g3 = gate.rearrange("p (a t) -> p a t", t=T)
            nc.vector.tensor_tensor(g3, g3, causal.unsqueeze(1).broadcast_to([128, GH * J, T]), ALU.mult).then_inc(*s.dve_chain.next())
            dve.wait_ge(s.dve_chain.handle, s.dve_chain.last())
            g4 = gate.rearrange("p (g j o t) -> p g j o t", g=GH, j=J, o=1)

            def weights(g):
                dve.wait_ge(squared.handle, squared.at(g + 1))
                if g - 1 > 0:
                    dve.wait_ge(summed.handle, summed.at(g - 1))
                nc.vector.tensor_tensor(a[g % 2].rearrange("p (j r t) -> p j r t", j=J, r=2),
                                             square[g % 2].rearrange("p (j r t) -> p j r t", j=J, r=2),
                                             g4[:, g].broadcast_to([128, J, 2, T]), ALU.mult).then_inc(*a_in.next())
                dve.wait_ge(a_in.handle, a_in.last())

            def divide(g):
                dve.wait_ge(summed.handle, summed.at(g + 1))
                if g - 1 > 0:
                    dve.wait_ge(projected_y.handle, projected_y.at(g - 1))
                for h in range(2):
                    r = rnorm[:, h * NT:(h + 1) * NT]
                    nc.vector.tensor_scalar(r, c.ps[:, 4 + h, 0:NT], 1e-6, None, ALU.add).then_inc(*s.dve_chain.next())
                    dve.wait_ge(s.dve_chain.handle, s.dve_chain.last())
                    nc.vector.reciprocal(r, r).then_inc(*s.dve_chain.next())
                    dve.wait_ge(s.dve_chain.handle, s.dve_chain.last())
                    nc.vector.tensor_tensor(
                        yT[g % 2].rearrange("p r (j h) t -> p h j r t", h=2)[:, h, :, :, 0:T],
                        c.ps[:, 2 + h, 0:NT].rearrange("p (j r t) -> p j r t", j=J, r=2),
                        r.rearrange("p (j r t) -> p j r t", j=J, r=2), ALU.mult).then_inc(*y_in.next())
                    dve.wait_ge(y_in.handle, y_in.last())

            dve.wait_ge(padded.handle, padded.at(3))
            weights(0)
            for g in range(GH):
                if g + 1 < GH:
                    weights(g + 1)
                divide(g)
            norm_vector(c, s, dve, False)



NH, DQ, DH = 16, 192, 96
UNITS = NH * T // 128


def X_WEIGHTS(c, o, tag):
    if "rope" in o:
        q = {"kcq": (tag + "_kcq", c.at(o["kcq"], 3072)), "rope": ("q_rope", c.at(o["rope"], 4 * T, DH))}
    else:
        q = {"kcq": (tag + "_kcqT", c.at(o["kcq"], 4096, DH))}
    return {**q, "Wq": (tag + "_Wq", c.at(o["Wq"], 4096)),
            "Wqr": (tag + "_Wqr", c.at(o["Wqr"], 3072, 64)), "Wkr": (tag + "_Wkr", c.at(o["Wkr"], 1024, 64)),
            "kckv": (tag + "_kckv", c.at(o["kckv"], 1024)), "Wo": (tag + "_Wo", c.at(o["Wo"], 4096))}


X_AT = {"Wq": 0, "kcq": 4096, "Wqr": 7168, "Wkr": 10240, "kckv": 11264, "Wo": 12288, "QZ": 16384, "C": 23552,
        "Z": 25600, "buf": 27648, "rope": 36000, "CT": 25600, "PT": 0, "P": 10752}
X3_AT = {"Wq": 8192, "kcq": 31232, "Wqr": 0, "Wkr": 3072, "kckv": 4096, "Wo": 12288, "QZ": 16384, "C": 27648,
         "Z": 5120, "buf": 29696, "CT": 23552, "PT": 0, "P": 10752}


def cross_attention(c, name, o, rope, now, prefetch):
    nc, s = c.nc, Stage(c, name)
    if rope:
        wq = c.at(o["Wq"], 4096).rearrange("p (k h m) -> p k h m", k=KT, h=NH)
        kcq = c.at(o["kcq"], 3072).rearrange("p (h q) -> p h q", h=NH)
        tab = c.at(o["rope"], 4 * T, DH).rearrange("p (i t) -> p i t", i=4)
    else:
        wqT = c.at(o["Wq"], 4096).rearrange("p (h n) -> p h n", h=NH)
        kcqT = c.at(o["kcq"], 4096, DH).rearrange("p (e h m) -> p e h m", e=2, h=NH)
    wqr = c.at(o["Wqr"], 3072, 64).rearrange("p (h q) -> p h q", h=NH)
    wkr = c.at(o["Wkr"], 1024, 64).rearrange("p (h d) -> p h d", h=NH)
    kckv = c.at(o["kckv"], 1024).rearrange("p (h d) -> p h d", h=NH)
    wo = c.at(o["Wo"], 4096).rearrange("p (h n) -> p h n", h=NH)
    qz = c.at(o["QZ"], 7168).rearrange("p (b h t) -> p b h t", b=B, h=NH)
    cm = c.at(o["C"], 2048).rearrange("p (h n) -> p h n", h=8)
    z = c.at(o["Z"], 2048, DH).rearrange("p (h e d) -> p h e d", h=NH, e=2)
    buf = o["buf"]
    qhk = [c.at(buf + i * NT, NT) for i in range(2)]
    prod = [[c.at(buf + (2 + 4 * n + i) * NT, NT, DH) for i in range(4)] for n in range(2)]
    rot = [[c.at(buf + (10 + 2 * n + i) * NT, NT, DH) for i in range(2)] for n in range(4)]
    kz = [c.at(buf + 256 * i, 256).rearrange("p (h d) -> p h d", h=4) for i in range(2)]
    fold = [c.at(buf + 512 + 512 * i, 512).rearrange("p (k h d) -> p k h d", k=KT, h=4) for i in range(2)]
    ctxT = c.at(o["CT"], 4096).rearrange("p (h b t) -> p h b t", h=8, b=B)
    pT = c.at(o["PT"], LT * NH * T, LP).rearrange("p (l q) -> p l q", l=LT)
    probs = [c.at(o["P"] + i * L, L) for i in range(3)]
    stat = c.sb_small
    wide_mm, wide_in = s.sem("wide_mm"), s.sem("wide_in")
    kz_mm, kz_in, fold_mm, fold_in = s.sem("kz_mm"), s.sem("kz_in"), s.sem("fold_mm"), s.sem("fold_in")
    zeroed, hk_mm, hk_in, big_mm, prod_in, rot_in, lat_mm, lat_in = (
        s.sem(x) for x in ("zeroed", "hk_mm", "hk_in", "big_mm", "prod_in", "rot_in", "lat_mm", "lat_in"))
    scored, maxed, exped, recip, normed, turned, t_in, pv_mm, ct_in = (
        s.sem(x) for x in ("scored", "maxed", "exped", "recip", "normed", "turned", "t_in", "pv_mm", "ct_in"))
    padded = s.sem("padded")
    NU = B * UNITS
    steps = ([("Z", 0), ("Z", 1), ("C", 0), ("Z", 2), ("C", 1), ("Z", 3), ("C", 2), ("C", 3)] if rope else
             [("Z", 0), ("Z", 1), ("Z", 2), ("Z", 3), ("C", 0), ("C", 1), ("C", 2), ("C", 3)])

    def z_step(h):
        return steps.index(("Z", h // 4)) + 1

    TURNS = 3 * UNITS + 1

    def slot(i):
        return 3 * (i % 2)

    def turn_bank(i, k):
        return 6 + (i // UNITS * TURNS + 3 * (i % UNITS) + k) % 2

    with nc.Block(no_gpsimd_drain=True) as block:
        @block.sync
        def _(sp):
            c.load(sp, name, now)
            sp.wait_ge(wide_in.handle, wide_in.at(8))
            sp.wait_ge(lat_in.handle, lat_in.at(4 * NH // 2))
            prefetch(sp)

        @block.gpsimd
        def _(pool):
            nc.gpsimd.memset(qz[64:128, 0::2, :, :], 0.0).then_inc(*zeroed.next())
            nc.gpsimd.memset(qz[0:64, 1::2, :, :], 0.0).then_inc(*zeroed.next())
            pool.wait_ge(zeroed.handle, zeroed.at(2))
            if rope:
                for h in range(NH):
                    if h >= 4:
                        pool.wait_ge(lat_mm.handle, lat_mm.at((h - 2) // 2))
                    for e in range(2):
                        pool.wait_ge(prod_in.handle, prod_in.at(4 * h + 3 + e))
                        nc.gpsimd.tensor_tensor(rot[h % 4][e], prod[h % 2][2 * e], prod[h % 2][2 * e + 1],
                                                ALU.add).then_inc(*rot_in.next())
            pool.wait_ge(lat_in.handle, lat_in.at(4 * NH // 2))
            nc.gpsimd.memset(ctxT[:, :, :, T:TP], 0.0).then_inc(*padded.next())
            pool.wait_ge(padded.handle, padded.at(1))

        @block.tensor
        def _(pe):
            pe.wait_ge(c.loaded[name].handle, 16 * c.expect[name])
            def wide(n):
                kind, g = steps[n]
                if n >= 2:
                    pe.wait_ge(wide_in.handle, wide_in.at(n - 1))
                if kind == "Z":
                    for h in range(4 * g, 4 * g + 4):
                        for e in range(2):
                            m = nc.tensor.matmul(c.ps[0:DH, n % 2, ((h % 4) * 2 + e) * 64:((h % 4) * 2 + e + 1) * 64],
                                                 wqr[:, h, e * DH:(e + 1) * DH], wkr[:, h, :], start=True, stop=True)
                else:
                    for i in range(2):
                        for e in range(2):
                            h = 2 * g + i + 8 * e
                            m = nc.tensor.matmul(c.ps[e * 64:(e + 1) * 64, n % 2, i * D:(i + 1) * D], kckv[:, h, :],
                                                 wo[:, h, :], start=True, stop=True)
                m.then_inc(*wide_mm.next())

            def first(h):
                if h >= 2:
                    pe.wait_ge(hk_in.handle, hk_in.at(h - 1))
                for k in range(KT):
                    m = nc.tensor.matmul(c.ps[:, 2 + h % 2, 0:NT], wq[:, k, h, :], c.x_feat[:, k, :, 0:T],
                                         start=(k == 0), stop=(k == KT - 1))
                m.then_inc(*hk_mm.next())

            def second(h):
                pe.wait_ge(hk_in.handle, hk_in.at(h + 1))
                for e in range(2):
                    if h > 0:
                        pe.wait_ge(prod_in.handle, prod_in.at(4 * (h - 1) + 2 * (e + 1)))
                    m = nc.tensor.matmul(c.ps[0:DH, 4 + e, 0:NT], kcq[:, h, e * DH:(e + 1) * DH], qhk[h % 2],
                                         start=True, stop=True)
                    m.then_inc(*big_mm.next())

            def third(p):
                pe.wait_ge(rot_in.handle, rot_in.at(4 * p + 4))
                pe.wait_ge(wide_in.handle, wide_in.at(z_step(2 * p)))
                if p >= 2:
                    pe.wait_ge(lat_in.handle, lat_in.at(4 * (p - 1)))
                for e in range(2):
                    for r in range(2):
                        h = 2 * p + r
                        m = nc.tensor.matmul(c.ps[r * 64:(r + 1) * 64, 6 + p % 2, 0:NT], z[:, h, e, :], rot[h % 4][e],
                                             start=(e == 0), stop=(e == 1), skip_group_check=True)
                m.then_inc(*lat_mm.next())

            def fold_kz(g):
                pe.wait_ge(wide_in.handle, wide_in.at(z_step(4 * g)))
                if g >= 2:
                    pe.wait_ge(kz_in.handle, kz_in.at(g - 1))
                for h in range(4 * g, 4 * g + 4):
                    for e in range(2):
                        m = nc.tensor.matmul(c.ps[:, 2 + g % 2, (h % 4) * 64:(h % 4 + 1) * 64], kcqT[:, e, h, :],
                                             z[:, h, e, :], start=(e == 0), stop=(e == 1))
                m.then_inc(*kz_mm.next())

            def fold_wq(g):
                pe.wait_ge(kz_in.handle, kz_in.at(g + 1))
                if g >= 2:
                    pe.wait_ge(fold_in.handle, fold_in.at(g - 1))
                for k in range(KT):
                    for h in range(4 * g, 4 * g + 4):
                        at = k * 256 + (h % 4) * 64
                        m = nc.tensor.matmul(c.ps[:, 4 + g % 2, at:at + 64], wqT[:, h, k * 128:(k + 1) * 128],
                                             kz[g % 2][:, h % 4, :], start=True, stop=True)
                m.then_inc(*fold_mm.next())

            def folded(p):
                pe.wait_ge(fold_in.handle, fold_in.at(p // 2 + 1))
                if p >= 2:
                    pe.wait_ge(lat_in.handle, lat_in.at(4 * (p - 1)))
                for k in range(KT):
                    m = nc.tensor.matmul(c.ps[:, 6 + p % 2, 0:NT], fold[p // 2 % 2][:, k, 2 * (p % 2):2 * (p % 2) + 2, :],
                                         c.x_feat[:, k, :, 0:T], start=(k == 0), stop=(k == KT - 1))
                m.then_inc(*lat_mm.next())

            if rope:
                wide(0)
                for h in range(NH + 2):
                    if h < NH:
                        first(h)
                    if h % 2 == 1 and h < 15:
                        wide(h // 2 + 1)
                    if 1 <= h <= NH:
                        second(h - 1)
                    if h % 2 == 1 and h >= 3:
                        third(h // 2 - 1)
            else:
                for t in range(8):
                    wide(t)
                    if 1 <= t <= 4:
                        fold_kz(t - 1)
                    if 2 <= t <= 5:
                        fold_wq(t - 2)
                    if 3 <= t <= 6:
                        folded(2 * (t - 3))
                        folded(2 * (t - 3) + 1)
            pe.wait_ge(wide_in.handle, wide_in.at(8))
            pe.wait_ge(lat_in.handle, lat_in.at(4 * NH // 2))
            pe.wait_ge(zeroed.handle, zeroed.at(2))

            def scores(i, k):
                if k == 0 and i >= 2:
                    pe.wait_ge(exped.handle, exped.at(i - 1))
                q = qz[:, i // UNITS, :, :].rearrange("p h t -> p (h t)")[:, i % UNITS * 128:(i % UNITS + 1) * 128]
                m = nc.tensor.matmul(c.ps[:, slot(i) + k, 0:4 * LP], q,
                                     c.ctx_feat[:, i // UNITS // 2, k * 4 * LP:(k + 1) * 4 * LP], start=True, stop=True)
                if k == 2:
                    m.then_inc(*scored.next())

            def turn(i, k):
                if k == 0:
                    pe.wait_ge(normed.handle, normed.at(i + 1))
                if i % UNITS == 0 and k == 1 and i > 0:
                    pe.wait_ge(ct_in.handle, ct_in.at(i // UNITS))
                elif i % UNITS == 0 and k == 0 and i > 0:
                    pe.wait_ge(t_in.handle, t_in.at(3 * i))
                elif 3 * i + k - 1 > 0:
                    pe.wait_ge(t_in.handle, t_in.at(3 * i + k - 1))
                for l in range(4):
                    m = nc.tensor.transpose(
                        c.ps[0:LP, turn_bank(i, k), l * 128:(l + 1) * 128],
                        probs[i % 3].rearrange("p (k l) -> p k l", l=LP)[:, 4 * k + l, :], c.ident[:])
                m.then_inc(*turned.next())

            def weigh(b):
                pe.wait_ge(t_in.handle, t_in.at(3 * UNITS * (b + 1)))
                for l in range(LT):
                    for e in range(2):
                        m = nc.tensor.matmul(c.ps[e * 64:(e + 1) * 64, turn_bank(b * UNITS + UNITS - 1, 3), 0:NT],
                                             c.ctx_pos[:, b // 2, l, b % 2, :], pT[:, l, e * NT:(e + 1) * NT],
                                             start=(l == 0), stop=(l == LT - 1), skip_group_check=True)
                m.then_inc(*pv_mm.next())

            for i in range(NU + 2):
                for k in range(3):
                    if i < NU:
                        scores(i, k)
                    if i >= 2:
                        turn(i - 2, k)
                if i >= 2 and (i - 2) % UNITS == UNITS - 1:
                    weigh((i - 2) // UNITS)
            pe.wait_ge(ct_in.handle, ct_in.at(B))
            pe.wait_ge(padded.handle, padded.at(1))
            for h in range(8):
                for j in range(J):
                    m = project_out(c, pe, j, h, ctxT[:, h, 2 * j:2 * j + 2, :], cm[:, h, :], h == 0, h == 7)
            m.then_inc(*s.y_done.next())
            norm_tensor(c, s, pe, False)

        @block.scalar
        def _(act):
            def place(p):
                act.wait_ge(lat_mm.handle, lat_mm.at(p + 1))
                if p == 0:
                    act.wait_ge(zeroed.handle, zeroed.at(2))
                for r in range(2):
                    for e in range(2):
                        nc.scalar.copy(qz[e * 64:(e + 1) * 64, e::2, 2 * p + r, :],
                                       valid(c.ps[r * 64:(r + 1) * 64, 6 + p % 2, 0:NT])[:, e::2, :]).then_inc(*lat_in.next())

            if rope:
                for h in range(NH + 2):
                    if h < NH:
                        act.wait_ge(hk_mm.handle, hk_mm.at(h + 1))
                        if h >= 2:
                            act.wait_ge(big_mm.handle, big_mm.at(2 * (h - 1)))
                        nc.scalar.copy(qhk[h % 2], c.ps[:, 2 + h % 2, 0:NT]).then_inc(*hk_in.next())
                    if h % 2 == 1 and h >= 3:
                        place(h // 2 - 1)
            else:
                for t in range(6):
                    if t < 4:
                        act.wait_ge(kz_mm.handle, kz_mm.at(t + 1))
                        if t >= 2:
                            act.wait_ge(fold_mm.handle, fold_mm.at(t - 1))
                        nc.scalar.copy(kz[t % 2].rearrange("p h d -> p (h d)"), c.ps[:, 2 + t % 2, 0:256]).then_inc(*kz_in.next())
                    if t >= 2:
                        place(2 * (t - 2))
                        place(2 * (t - 2) + 1)
            for i in range(NU):
                act.wait_ge(maxed.handle, maxed.at(i + 1))
                if 3 * (i - 2) > 0:
                    act.wait_ge(turned.handle, turned.at(3 * (i - 2)))
                p = probs[i % 3]
                if i == 0:
                    act.wait_ge(wide_in.handle, wide_in.at(8))
                nc.scalar.activation(p.rearrange("p (k l) -> p k l", k=3), c.ps[:, slot(i):slot(i) + 3, 0:4 * LP],
                                          ACT.Exp, bias=stat[:, i % 4:i % 4 + 1],
                                          accum_out=stat[:, 4 + i % 4:5 + i % 4]).then_inc(*exped.next())
                act.wait_ge(exped.handle, exped.last())
                act.wait_ge(recip.handle, recip.at(i + 1))
                nc.scalar.activation(p, p, ACT.Copy, scale=stat[:, 8 + i % 4:9 + i % 4]).then_inc(*normed.next())
                act.wait_ge(normed.handle, normed.last())
            norm_scalar(c, s, act, False)

        @block.vector
        def _(dve):
            def wide_out(n):
                dve.wait_ge(wide_mm.handle, wide_mm.at(n + 1))
                kind, g = steps[n]
                if kind == "Z":
                    nc.vector.tensor_copy(z[:, 4 * g:4 * g + 4, :, :].rearrange("p h e d -> p (h e d)"),
                                          c.ps[0:DH, n % 2, :]).then_inc(*wide_in.next())
                else:
                    nc.vector.tensor_copy(cm[:, 2 * g:2 * g + 2, :].rearrange("p h n -> p (h n)"),
                                          c.ps[:, n % 2, :]).then_inc(*wide_in.next())

            if rope:
                wide_out(0)
                for h in range(NH):
                    if h % 2 == 0 and h < 14:
                        wide_out(h // 2 + 1)
                    if h >= 2:
                        dve.wait_ge(rot_in.handle, rot_in.at(2 * (h - 1)))
                    for e, f in ((0, 0), (1, 1), (0, 1), (1, 0)):
                        src = e if f == 0 else 1 - e
                        dve.wait_ge(big_mm.handle, big_mm.at(2 * h + 1 + src))
                        nc.vector.tensor_tensor(valid(prod[h % 2][2 * e + f]), valid(c.ps[0:DH, 4 + src, 0:NT]),
                                                tab[:, 2 * e + f, :].unsqueeze(1).broadcast_to([DH, B, T]),
                                                ALU.mult).then_inc(*prod_in.next())
            else:
                for t in range(8):
                    wide_out(t)
                    if 2 <= t <= 5:
                        g = t - 2
                        dve.wait_ge(fold_mm.handle, fold_mm.at(g + 1))
                        if g >= 2:
                            dve.wait_ge(lat_mm.handle, lat_mm.at(2 * (g - 1)))
                        nc.vector.tensor_copy(fold[g % 2].rearrange("p k h d -> p (k h d)"), c.ps[:, 4 + g % 2, :]).then_inc(*fold_in.next())

            def rowmax(i):
                dve.wait_ge(scored.handle, scored.at(i + 1))
                if i - 3 > 0:
                    dve.wait_ge(exped.handle, exped.at(i - 3))
                b0 = slot(i)
                nc.vector.tensor_reduce(stat[:, i % 4:i % 4 + 1], c.ps[:, b0:b0 + 3, 0:4 * LP], AX.XY, ALU.max,
                                             negate=True).then_inc(*maxed.next())
                dve.wait_ge(maxed.handle, maxed.last())

            def recips(i):
                dve.wait_ge(exped.handle, exped.at(i + 1))
                nc.vector.reciprocal(stat[:, 8 + i % 4:9 + i % 4], stat[:, 4 + i % 4:5 + i % 4]).then_inc(*recip.next())
                dve.wait_ge(recip.handle, recip.last())

            def copy_turned(i, k):
                if i % UNITS == 0 and k == 0 and i > 0:
                    dve.wait_ge(pv_mm.handle, pv_mm.at(i // UNITS))
                dve.wait_ge(turned.handle, turned.at(3 * i + k + 1))
                u = i % UNITS
                nc.vector.tensor_copy(pT[:, 4 * k:4 * k + 4, u * 128:(u + 1) * 128],
                                      c.ps[0:LP, turn_bank(i, k), :].rearrange("p (l q) -> p l q", l=4)).then_inc(*t_in.next())

            def keep(b):
                dve.wait_ge(pv_mm.handle, pv_mm.at(b + 1))
                dve.wait_ge(padded.handle, padded.at(1))
                nc.vector.tensor_copy(ctxT[:, :, b, 0:T], c.ps[:, turn_bank(b * UNITS + UNITS - 1, 3), 0:NT]
                                           .rearrange("p (h t) -> p h t", h=8)).then_inc(*ct_in.next())

            rowmax(0)
            for i in range(NU + 2):
                if i >= 1 and i - 1 < NU:
                    copy_turned(i - 1, 0)
                if i < NU:
                    recips(i)
                if i >= 1 and i - 1 < NU:
                    copy_turned(i - 1, 1)
                if i + 1 < NU:
                    rowmax(i + 1)
                if i >= 1 and i - 1 < NU:
                    copy_turned(i - 1, 2)
                if i >= 1 and i % UNITS == 0:
                    keep(i // UNITS - 1)
            dve.wait_ge(t_in.handle, t_in.last())
            dve.wait_ge(ct_in.handle, ct_in.last())
            norm_vector(c, s, dve, False)



class Experts:

    def __init__(self, cols, experts, top, chunks, gate_tiles, gate, up, down, downs, router, spread, extra):
        self.cols, self.experts, self.top, self.chunks = cols, experts, top, chunks
        self.hidden, self.gate, self.up, self.down, self.downs = gate_tiles, gate, up, down, downs
        self.router, self.spread, self.extra = router, spread, extra


def feed_forward(c, name, f, now, prefetch, store=None):
    nc, s = c.nc, Stage(c, name)
    kind, E, last = name[:2], f.experts, store is not None
    wg = c.at(f.gate, KT * f.hidden).rearrange("p (k n) -> p k n", k=KT)
    wu = c.at(f.up, KT * f.hidden).rearrange("p (k n) -> p k n", k=KT)
    wd = c.at(f.down, f.downs * D).rearrange("p (h n) -> p h n", n=D)
    wr = c.at(f.router, KT * f.cols).rearrange("p (k n) -> p k n", k=KT)
    W = 16384
    hid = [c.at(W + 512 * i, 512).rearrange("p (b t) -> p b t", b=B) for i in range(2)]
    silu = [c.at(W + 1024 + NT * i, NT) for i in range(2)]
    comb = c.at(W + 1920, 512).rearrange("p (j e) -> p j e", j=J)
    combT = c.at(W + 2432, NT)
    cand = c.at(W + 2880, J * (E + 8)).rearrange("p (j e) -> p j e", j=J)
    left = c.at(W + 3424, J * (E + 8)).rearrange("p (j e) -> p j e", j=J)
    ex = c.at(W + 3968, J * E).rearrange("p (j e) -> p j e", j=J)
    top8 = c.at(W + 4480, J * 8).rearrange("p (j e) -> p j e", j=J)
    small = c.at(W + 4512, 32)
    mix = c.at(W + 4544, 32)
    spread = c.at(f.spread, 2048).rearrange("p (h m) -> p h m", m=128)[:, 0:16, :]
    logits, expin, exped, comb_in, comb_t, combT_in = (
        s.sem(x) for x in ("logits", "expin", "exped", "comb_in", "comb_t", "combT_in"))
    gu_mm, bc_mm, silu_in, hid_in, down_mm, padded = (
        s.sem(x) for x in ("gu_mm", "bc_mm", "silu_in", "hid_in", "down_mm", "padded"))
    N = len(f.chunks)
    weighted = [n for n, ch in enumerate(f.chunks) if ch[2] is not None]
    mixing = kind == "L0"

    def bank(n):
        return 2 + 3 * (n % 2)

    with nc.Block(no_gpsimd_drain=True) as block:
        @block.sync
        def _(sp):
            c.load(sp, name, now)
            prefetch(sp)
            if last:
                norm_store(c, s, sp, store)

        @block.gpsimd
        def _(pool):
            for i in range(2):
                nc.gpsimd.memset(hid[i][:, :, T:TP], 0.0).then_inc(*padded.next())
            nc.gpsimd.memset(comb, 0.0).then_inc(*padded.next())
            nc.gpsimd.memset(cand[:, :, E:E + 8], -3.0e38).then_inc(*padded.next())
            nc.gpsimd.memset(top8, -3.0e38).then_inc(*padded.next())
            pool.wait_ge(padded.handle, padded.at(5))

        @block.tensor
        def _(pe):
            pe.wait_ge(c.loaded[name].handle, 16 * c.expect[name])
            for j in range(J):
                for k in range(KT):
                    m = nc.tensor.matmul(c.ps[:, 7, j * f.cols:(j + 1) * f.cols], c.x_feat[:, k, 2 * j:2 * j + 2, :],
                                         wr[:, k, :], start=(k == 0), stop=(k == KT - 1))
            m.then_inc(*logits.next())

            def gate_up(n):
                if n - 1 > 0:
                    pe.wait_ge(hid_in.handle, hid_in.at(n - 1))
                m_ = f.chunks[n][0]
                for i, w in enumerate((wg, wu)):
                    for k in range(KT):
                        m = nc.tensor.matmul(c.ps[0:m_, bank(n) + i, 0:NT], w[:, k, n * 128:n * 128 + m_],
                                             c.x_feat[:, k, :, 0:T], start=(k == 0), stop=(k == KT - 1))
                m.then_inc(*gu_mm.next())

            def weights(n):
                if n in weighted:
                    pe.wait_ge(combT_in.handle, combT_in.at(1))
                    m = nc.tensor.matmul(c.ps[:, bank(n) + 2, 0:NT], spread[:, f.chunks[n][2], :], combT,
                                         start=True, stop=True)
                    m.then_inc(*bc_mm.next())

            def down(n):
                pe.wait_ge(hid_in.handle, hid_in.at(n + 1))
                m_, t = f.chunks[n][0], f.chunks[n][1]
                for j in range(J):
                    m = project_out(c, pe, j, n, hid[n % 2][0:m_, 2 * j:2 * j + 2, :], wd[0:m_, t, :],
                                    n == 0, n == N - 1)
                m.then_inc(*down_mm.next())

            gate_up(0)
            gate_up(1)
            pe.wait_ge(comb_in.handle, comb_in.at(1))
            for j in range(J):
                t = nc.tensor.transpose(c.ps[:, 7, j * 128:(j + 1) * 128], comb[:, j, :], c.ident[:])
            t.then_inc(*comb_t.next())
            weights(0)
            weights(1)
            for n in range(N):
                down(n)
                if n + 2 < N:
                    gate_up(n + 2)
                    weights(n + 2)
            pe.wait_ge(down_mm.handle, down_mm.at(N))
            pe.sem_inc(*s.y_done.next())
            norm_tensor(c, s, pe, last)

        @block.scalar
        def _(act):
            act.wait_ge(expin.handle, expin.at(1))
            nc.scalar.activation(ex, ex, ACT.Exp).then_inc(*exped.next())
            act.wait_ge(exped.handle, exped.last())
            if f.cols > E:
                act.wait_ge(expin.handle, expin.at(2))
                nc.scalar.activation(small[:, 24:28].rearrange("p (j o) -> p j o", j=J),
                                          c.ps[:, 7, 0:J * f.cols].rearrange("p (j e) -> p j e", j=J)[:, :, E:E + 1],
                                          ACT.Exp, scale=-1.0).then_inc(*exped.next())
                act.wait_ge(exped.handle, exped.last())
            for n in range(N):
                m_ = f.chunks[n][0]
                act.wait_ge(gu_mm.handle, gu_mm.at(n + 1))
                if n - 1 > 0:
                    act.wait_ge(hid_in.handle, hid_in.at(n - 1))
                nc.scalar.activation(silu[n % 2][0:m_], c.ps[0:m_, bank(n), 0:NT], ACT.Silu).then_inc(*silu_in.next())
                act.wait_ge(silu_in.handle, silu_in.last())
            norm_scalar(c, s, act, last)

        @block.vector
        def _(dve):
            V = nc.vector
            dve.wait_ge(c.loaded[name].handle, 16 * c.expect[name])
            dve.wait_ge(padded.handle, padded.at(5))
            spr = lambda ap: ap.unsqueeze(2).broadcast_to([128, J, E])
            if mixing:
                amp = c.at(f.extra, 16)
                scale = c.at(f.extra + 16, 1)
                V.tensor_tensor(amp, amp, amp, ALU.mult).then_inc(*s.dve_chain.next())
                dve.wait_ge(s.dve_chain.handle, s.dve_chain.last())
                V.tensor_reduce(mix[:, 0:8], amp.rearrange("p (k two) -> p k two", two=2), AX.X, ALU.add).then_inc(*s.dve_chain.next())
                dve.wait_ge(s.dve_chain.handle, s.dve_chain.last())
                V.tensor_reduce(mix[:, 8:9], mix[:, 0:8], AX.X, ALU.add).then_inc(*s.dve_chain.next())
                dve.wait_ge(s.dve_chain.handle, s.dve_chain.last())
                V.tensor_scalar(mix[:, 8:9], mix[:, 8:9], 1e-8, None, ALU.add).then_inc(*s.dve_chain.next())
                dve.wait_ge(s.dve_chain.handle, s.dve_chain.last())
                V.reciprocal(mix[:, 8:9], mix[:, 8:9]).then_inc(*s.dve_chain.next())
                dve.wait_ge(s.dve_chain.handle, s.dve_chain.last())
                V.tensor_scalar(mix[:, 0:8], mix[:, 0:8], mix[:, 8:9], scale, ALU.mult, ALU.mult).then_inc(*s.dve_chain.next())
                dve.wait_ge(s.dve_chain.handle, s.dve_chain.last())
                V.tensor_copy(spread[:, 0:8, :], mix[:, 0:8].unsqueeze(2).broadcast_to([128, 8, 128])).then_inc(*s.dve_chain.next())
                dve.wait_ge(s.dve_chain.handle, s.dve_chain.last())
            dve.wait_ge(logits.handle, logits.at(1))
            lg = c.ps[:, 7, 0:J * f.cols].rearrange("p (j e) -> p j e", j=J)[:, :, 0:E]
            V.tensor_reduce(small[:, 0:4], lg, AX.X, ALU.max).then_inc(*s.dve_chain.next())
            dve.wait_ge(s.dve_chain.handle, s.dve_chain.last())
            V.tensor_tensor(ex, lg, spr(small[:, 0:4]), ALU.subtract).then_inc(*expin.next())
            dve.wait_ge(expin.handle, expin.last())
            if kind == "L1":
                bias = c.at(f.extra, 16)
                V.tensor_tensor(cand[:, :, 0:E], lg, bias.unsqueeze(1).broadcast_to([128, J, E]), ALU.add).then_inc(*s.dve_chain.next())
                dve.wait_ge(s.dve_chain.handle, s.dve_chain.last())
            elif not mixing:
                V.tensor_copy(cand[:, :, 0:E], lg).then_inc(*expin.next())
                dve.wait_ge(expin.handle, expin.last())
            dve.wait_ge(exped.handle, exped.at(1))
            if mixing:
                V.tensor_reduce(small[:, 4:8], ex, AX.X, ALU.add).then_inc(*s.dve_chain.next())
                dve.wait_ge(s.dve_chain.handle, s.dve_chain.last())
                V.reciprocal(small[:, 4:8], small[:, 4:8]).then_inc(*s.dve_chain.next())
                dve.wait_ge(s.dve_chain.handle, s.dve_chain.last())
                V.tensor_tensor(ex, ex, spr(small[:, 4:8]), ALU.mult).then_inc(*s.dve_chain.next())
                dve.wait_ge(s.dve_chain.handle, s.dve_chain.last())
                V.tensor_copy(cand[:, :, 0:E], ex).then_inc(*s.dve_chain.next())
                dve.wait_ge(s.dve_chain.handle, s.dve_chain.last())
            for j in range(J):
                V.max(mix[:, 16:24], cand[:, j, 0:E]).then_inc(*s.dve_chain.next())
                dve.wait_ge(s.dve_chain.handle, s.dve_chain.last())
                V.tensor_copy(top8[:, j, 0:f.top], mix[:, 16:16 + f.top]).then_inc(*s.dve_chain.next())
                dve.wait_ge(s.dve_chain.handle, s.dve_chain.last())
                V.match_replace(left[:, j, :], top8[:, j, :], cand[:, j, :], 3.0e38).then_inc(*s.dve_chain.next())
                dve.wait_ge(s.dve_chain.handle, s.dve_chain.last())
            V.tensor_tensor(left[:, :, 0:E], left[:, :, 0:E], cand[:, :, 0:E], ALU.not_equal).then_inc(*s.dve_chain.next())
            dve.wait_ge(s.dve_chain.handle, s.dve_chain.last())
            V.tensor_tensor(ex, ex, left[:, :, 0:E], ALU.mult).then_inc(*s.dve_chain.next())
            dve.wait_ge(s.dve_chain.handle, s.dve_chain.last())
            V.tensor_reduce(small[:, 8:12], ex, AX.X, ALU.add).then_inc(*s.dve_chain.next())
            dve.wait_ge(s.dve_chain.handle, s.dve_chain.last())
            eps = {"L0": 1e-8, "L3": 1e-20}.get(kind, 0.0)
            if eps:
                V.tensor_scalar(small[:, 8:12], small[:, 8:12], eps, None, ALU.add).then_inc(*s.dve_chain.next())
                dve.wait_ge(s.dve_chain.handle, s.dve_chain.last())
            V.reciprocal(small[:, 12:16], small[:, 8:12]).then_inc(*s.dve_chain.next())
            dve.wait_ge(s.dve_chain.handle, s.dve_chain.last())
            if f.cols > E:
                dve.wait_ge(exped.handle, exped.at(2))
                V.tensor_scalar(small[:, 24:28], small[:, 24:28], 1.0, None, ALU.add).then_inc(*s.dve_chain.next())
                dve.wait_ge(s.dve_chain.handle, s.dve_chain.last())
                V.reciprocal(comb[:, :, E:E + 1], small[:, 24:28].rearrange("p (j o) -> p j o", j=J)).then_inc(*s.dve_chain.next())
                dve.wait_ge(s.dve_chain.handle, s.dve_chain.last())
            V.tensor_tensor(comb[:, :, 0:E], ex, spr(small[:, 12:16]), ALU.mult).then_inc(*comb_in.next())
            dve.wait_ge(comb_in.handle, comb_in.last())
            dve.wait_ge(comb_t.handle, comb_t.at(1))
            V.tensor_copy(combT.rearrange("p (b t) -> p b t", b=B),
                               c.ps[:, 7, :].rearrange("p (b t) -> p b t", b=B)[:, :, 0:T]).then_inc(*combT_in.next())
            dve.wait_ge(combT_in.handle, combT_in.last())
            for n in range(N):
                m_ = f.chunks[n][0]
                dve.wait_ge(silu_in.handle, silu_in.at(n + 1))
                if n - 1 > 0:
                    dve.wait_ge(down_mm.handle, down_mm.at(n - 1))
                up = c.ps[0:m_, bank(n) + 1, 0:NT]
                h = hid[n % 2][0:m_, :, 0:T]
                sl = silu[n % 2][0:m_]
                if n in weighted:
                    V.tensor_tensor(sl, up, sl, ALU.mult).then_inc(*s.dve_chain.next())
                    dve.wait_ge(s.dve_chain.handle, s.dve_chain.last())
                    dve.wait_ge(bc_mm.handle, bc_mm.at(weighted.index(n) + 1))
                    V.tensor_tensor(h, valid(c.ps[0:m_, bank(n) + 2, 0:NT]), valid(sl), ALU.mult).then_inc(*hid_in.next())
                    dve.wait_ge(hid_in.handle, hid_in.last())
                else:
                    V.tensor_tensor(h, valid(up), valid(sl), ALU.mult).then_inc(*hid_in.next())
                    dve.wait_ge(hid_in.handle, hid_in.last())
            norm_vector(c, s, dve, last)



class SmallHeads:

    def __init__(self, c, s, base, hd, scale, mask):
        self.c, self.s, self.hd, self.nm, self.scale, self.mask = c, s, hd, 32 // hd, scale, mask
        o = base
        self.q = c.at(o, self.nm * 1024).rearrange("p (m k b t) -> p m k b t", m=self.nm, k=KT, b=B)
        o += self.nm * 1024
        self.k = c.at(o, 1024).rearrange("p (k b t) -> p k b t", k=KT, b=B)
        self.v = c.at(o + 1024, 1024).rearrange("p (g n) -> p g n", g=4)
        self.p = c.at(o + 2048, 2048).rearrange("p (i e t) -> p i e t", i=4, e=8)
        self.pT = c.at(o + 4096, 2048).rearrange("p (i e g q) -> p i e g q", i=4, e=2, g=2)
        self.ctx = c.at(o + 6144, 1024).rearrange("p (j n) -> p j n", j=J)
        self.ctxT = c.at(o + 7168, 1024).rearrange("p (k b t) -> p k b t", k=KT, b=B)
        self.mx = c.at(o + 8192, 32)
        self.rs = c.at(o + 8224, 128).rearrange("p (i q e j) -> p i q e j", i=4, q=4, e=2)
        self.end = o + 8352
        (self.scored, self.shifted, self.exped, self.turned, self.t_act, self.ctx_mm, self.summed, self.ctx_in,
         self.ctx_t, self.ctxT_in, self.padded, self.q_in, self.k_in, self.v_in) = (s.sem(i) for i in range(14))

    def pool(self, pool):
        n = self.c.nc
        for m in range(self.nm):
            n.gpsimd.memset(self.q[:, m, :, :, T:TP], 0.0).then_inc(*self.padded.next())
        n.gpsimd.memset(self.p[:, :, :, T:TP], 0.0).then_inc(*self.padded.next())
        pool.wait_ge(self.padded.handle, self.padded.at(self.padded.n))

    def tensor(self, pe, q_steps, k_steps, v_steps):
        c, nc = self.c, self.c.nc
        if q_steps > 0:
            pe.wait_ge(self.q_in.handle, self.q_in.at(q_steps))
        if k_steps > 0:
            pe.wait_ge(self.k_in.handle, self.k_in.at(k_steps))
        if v_steps > 0:
            pe.wait_ge(self.v_in.handle, self.v_in.at(v_steps))
        pe.wait_ge(self.padded.handle, self.padded.at(self.nm + 1))

        def scores(g):
            if g > 0:
                pe.wait_ge(self.shifted.handle, self.shifted.at(g))
            for e in range(2):
                k, m_ = divmod(2 * g + e, self.nm)
                for b in range(B):
                    for i in range(4):
                        m = nc.tensor.matmul(
                            c.ps[(b % 2) * TP:(b % 2 + 1) * TP, 2 + i, (e * 4 + b // 2) * T:(e * 4 + b // 2 + 1) * T],
                            self.q[32 * i:32 * i + 32, m_, k, b, :], self.k[32 * i:32 * i + 32, k, b, 0:T],
                            start=True, stop=True)
            m.then_inc(*self.scored.next())

        def context(g):
            pe.wait_ge(self.exped.handle, self.exped.at(g + 1))
            for i in range(4):
                if 4 * g + i - 1 > 0:
                    pe.wait_ge(self.t_act.handle, self.t_act.at(4 * g + i - 1))
                for e in range(2):
                    for h in range(2):
                        t = nc.tensor.transpose(c.ps[:, 6 + i % 2, (2 * e + h) * 128:(2 * e + h + 1) * 128],
                                                self.p[:, i, e * 4 + 2 * h:e * 4 + 2 * h + 2, :], c.ident[:])
                t.then_inc(*self.turned.next())
            pe.wait_ge(self.t_act.handle, self.t_act.at(4 * (g + 1)))
            for i in range(4):
                for e in range(2):
                    k, m_ = divmod(2 * g + e, self.nm)
                    f = k * 128 + 32 * i + m_ * self.hd
                    for j in range(0, J, 2):
                        for h in range(2):
                            for r in range(2):
                                m = nc.tensor.matmul(
                                    c.ps[h * TP:(h + 1) * TP, r, (j // 2) * D + f:(j // 2) * D + f + self.hd],
                                    self.pT[r * TP:r * TP + T, i, e, j // 2, h * TP:(h + 1) * TP],
                                    self.v[r * TP:r * TP + T, j + h, f:f + self.hd], start=True, stop=True,
                                    skip_group_check=True)
            m.then_inc(*self.ctx_mm.next())

        scores(0)
        for g in range(self.nm):
            if g + 1 < self.nm:
                scores(g + 1)
            context(g)
        pe.wait_ge(self.ctx_in.handle, self.ctx_in.at(J * KT))
        for k in range(KT):
            for j in range(J):
                t = nc.tensor.transpose(c.ps[:, 6 + k, j * 128:(j + 1) * 128], self.ctx[:, j, k * 128:(k + 1) * 128],
                                        c.ident[:])
            t.then_inc(*self.ctx_t.next())

    def vector(self, dve):
        c, s, V = self.c, self.s, self.c.nc.vector
        dve.wait_ge(self.padded.handle, self.padded.at(self.nm + 1))
        for g in range(self.nm):
            dve.wait_ge(self.scored.handle, self.scored.at(g + 1))
            if 4 * g > 0:
                dve.wait_ge(self.turned.handle, self.turned.at(4 * g))
            sc = c.ps[:, 2:6, 0:NT].rearrange("p i (e t) -> p i e t", t=T)
            p = self.p[:, :, :, 0:T]
            mx = self.mx.rearrange("p (i e) -> p i e", i=4)
            spread = mx.unsqueeze(3).broadcast_to([128, 4, 8, T])
            if self.mask is not None:
                V.tensor_tensor(p, sc, self.mask.rearrange("p (a b t) -> p a b t", a=1, b=1)
                                     .broadcast_to([128, 4, 8, T]), ALU.add).then_inc(*s.dve_chain.next())
                dve.wait_ge(s.dve_chain.handle, s.dve_chain.last())
                V.tensor_reduce(mx, p, AX.X, ALU.max).then_inc(*s.dve_chain.next())
                dve.wait_ge(s.dve_chain.handle, s.dve_chain.last())
                V.tensor_tensor(p, p, spread, ALU.subtract).then_inc(*self.shifted.next())
                dve.wait_ge(self.shifted.handle, self.shifted.last())
            else:
                V.tensor_reduce(mx, sc, AX.X, ALU.max).then_inc(*s.dve_chain.next())
                dve.wait_ge(s.dve_chain.handle, s.dve_chain.last())
                V.tensor_tensor(p, sc, spread, ALU.subtract).then_inc(*self.shifted.next())
                dve.wait_ge(self.shifted.handle, self.shifted.last())
            dve.wait_ge(self.exped.handle, self.exped.at(g + 1))
            rs = self.rs[:, :, g, :, :].rearrange("p i e j -> p i (e j)")
            V.tensor_reduce(rs, p, AX.X, ALU.add).then_inc(*s.dve_chain.next())
            dve.wait_ge(s.dve_chain.handle, s.dve_chain.last())
            V.reciprocal(rs, rs).then_inc(*self.summed.next())
            dve.wait_ge(self.summed.handle, self.summed.last())
        dve.wait_ge(self.ctx_mm.handle, self.ctx_mm.at(self.nm))
        for j in range(J):
            for k in range(KT):
                r = self.rs[:].rearrange("p i q e j -> p i (q e) j")[:, :, k * self.nm:(k + 1) * self.nm, j:j + 1]
                o = self.ctx[:, j, k * 128:(k + 1) * 128].rearrange("p (i m d) -> p i m d", i=4, m=self.nm)
                src = c.ps[:, j % 2, (j // 2) * D + k * 128:(j // 2) * D + (k + 1) * 128]
                V.tensor_tensor(o, src.rearrange("p (i m d) -> p i m d", i=4, m=self.nm),
                                     r.broadcast_to([128, 4, self.nm, self.hd]), ALU.mult).then_inc(*self.ctx_in.next())
                dve.wait_ge(self.ctx_in.handle, self.ctx_in.last())

    def scalar(self, act):
        c, s, A = self.c, self.s, self.c.nc.scalar
        for g in range(self.nm):
            act.wait_ge(self.shifted.handle, self.shifted.at(g + 1))
            p = self.p[:, :, :, 0:T].rearrange("p i e t -> p (i e) t")
            A.activation(p, p, ACT.Exp, scale=self.scale).then_inc(*self.exped.next())
            act.wait_ge(self.exped.handle, self.exped.last())
            for i in range(4):
                act.wait_ge(self.turned.handle, self.turned.at(4 * g + i + 1))
                if g > 0:
                    act.wait_ge(self.ctx_mm.handle, self.ctx_mm.at(g))
                A.copy(self.pT[:, i].rearrange("p e g q -> p (e g q)"), c.ps[:, 6 + i % 2, :]).then_inc(*self.t_act.next())
                act.wait_ge(self.t_act.handle, self.t_act.last())
        for k in range(KT):
            act.wait_ge(self.ctx_t.handle, self.ctx_t.at(k + 1))
            A.copy(self.ctxT[:, k, :, :], c.ps[:, 6 + k, :].rearrange("p (b t) -> p b t", b=B)).then_inc(*self.ctxT_in.next())
            act.wait_ge(self.ctxT_in.handle, self.ctxT_in.last())


def value_tile(c, out, x, g, weights):
    b = 4 * (g // 2) + g % 2
    for k, w in enumerate(weights):
        for r in range(2):
            m = c.nc.tensor.matmul(out[r * TP:(r + 1) * TP], x[k][:, b + 2 * r, :], w,
                                   start=(k == 0), stop=(k == len(weights) - 1), skip_group_check=True)
    return m



CH, CL = NT // 32, 32
MAGIC = 12582912.0


def L1_ATTN_LOADS(c):
    return [("L1a_W", c.at(0, 2048)), ("L1a_WT", c.at(2048, 2048)), ("L1a_bias", c.at(15360, 8)),
            ("L1a_ob", c.at(15368, D))]


def quantise(c, s, dve, tm_in, tmax_in, src, res, tmp, cb, small, done):
    V = c.nc.vector
    r3 = res.rearrange("p (n l) -> p n l", l=CL)
    s3 = src.rearrange("p (n l) -> p n l", l=CL)
    N = KT * CH
    f = lambda i: small[:, i * N:(i + 1) * N]
    mx, mn, cmax, t1, thr, fac, sc, inv = (f(i) for i in range(8))
    tm, tmax = small[:, 8 * N:8 * N + CH], small[:, 8 * N + CH:8 * N + 2 * CH]
    spread = lambda ap: ap.unsqueeze(2).broadcast_to([128, N, CL])
    V.tensor_reduce(mx, s3, AX.X, ALU.max).then_inc(*s.dve_chain.next())
    dve.wait_ge(s.dve_chain.handle, s.dve_chain.last())
    V.tensor_reduce(mn, s3, AX.X, ALU.min).then_inc(*s.dve_chain.next())
    dve.wait_ge(s.dve_chain.handle, s.dve_chain.last())
    V.tensor_tensor(cb, mx, mn, ALU.add).then_inc(*s.dve_chain.next())
    dve.wait_ge(s.dve_chain.handle, s.dve_chain.last())
    V.tensor_scalar(cb, cb, 0.5, None, ALU.mult).then_inc(*s.dve_chain.next())
    dve.wait_ge(s.dve_chain.handle, s.dve_chain.last())
    V.tensor_tensor(r3, s3, spread(cb), ALU.subtract).then_inc(*s.dve_chain.next())
    dve.wait_ge(s.dve_chain.handle, s.dve_chain.last())
    V.tensor_tensor(mx, mx, cb, ALU.subtract).then_inc(*s.dve_chain.next())
    dve.wait_ge(s.dve_chain.handle, s.dve_chain.last())
    V.tensor_tensor(mn, cb, mn, ALU.subtract).then_inc(*s.dve_chain.next())
    dve.wait_ge(s.dve_chain.handle, s.dve_chain.last())
    V.tensor_tensor(cmax, mx, mn, ALU.max).then_inc(*s.dve_chain.next())
    dve.wait_ge(s.dve_chain.handle, s.dve_chain.last())
    V.tensor_tensor(tm, cmax[:, 0:CH], cmax[:, CH:N], ALU.max).then_inc(*tm_in.next())
    dve.wait_ge(tm_in.handle, tm_in.last())
    if tm_in.n > 0:
        dve.wait_ge(tmax_in.handle, tmax_in.at(tm_in.n))
    for k in range(KT):
        V.tensor_copy(t1[:, k * CH:(k + 1) * CH], tmax).then_inc(*s.dve_chain.next())
        dve.wait_ge(s.dve_chain.handle, s.dve_chain.last())
    V.memset(fac, 2.0 ** -7).then_inc(*s.dve_chain.next())
    dve.wait_ge(s.dve_chain.handle, s.dve_chain.last())
    for m in range(7):
        V.scalar_tensor_tensor(out=thr, in0=t1, scalar=2.0 ** (m - 7), in1=cmax, op0=ALU.mult, op1=ALU.is_lt).then_inc(*s.dve_chain.next())
        dve.wait_ge(s.dve_chain.handle, s.dve_chain.last())
        V.scalar_tensor_tensor(out=fac, in0=thr, scalar=1.0, in1=fac, op0=ALU.add, op1=ALU.mult).then_inc(*s.dve_chain.next())
        dve.wait_ge(s.dve_chain.handle, s.dve_chain.last())
    V.tensor_tensor(sc, t1, fac, ALU.mult).then_inc(*s.dve_chain.next())
    dve.wait_ge(s.dve_chain.handle, s.dve_chain.last())
    V.tensor_scalar(sc, sc, 1.0 / 7.0, 1e-9, ALU.mult, ALU.max).then_inc(*s.dve_chain.next())
    dve.wait_ge(s.dve_chain.handle, s.dve_chain.last())
    V.reciprocal(inv, sc).then_inc(*s.dve_chain.next())
    dve.wait_ge(s.dve_chain.handle, s.dve_chain.last())
    V.tensor_tensor(r3, r3, spread(inv), ALU.mult).then_inc(*s.dve_chain.next())
    dve.wait_ge(s.dve_chain.handle, s.dve_chain.last())
    V.tensor_scalar(res, res, MAGIC, MAGIC, ALU.add, ALU.subtract).then_inc(*s.dve_chain.next())
    dve.wait_ge(s.dve_chain.handle, s.dve_chain.last())
    V.tensor_scalar(res, res, 7.0, -8.0, ALU.min, ALU.max).then_inc(*s.dve_chain.next())
    dve.wait_ge(s.dve_chain.handle, s.dve_chain.last())
    V.tensor_tensor(r3, r3, spread(sc), ALU.mult).then_inc(*s.dve_chain.next())
    dve.wait_ge(s.dve_chain.handle, s.dve_chain.last())
    V.tensor_copy(tmp.rearrange("p (n l) -> p n l", l=CL), spread(cb)).then_inc(*done.next())
    dve.wait_ge(done.handle, done.last())


def l1_attention(c, now, prefetch):
    nc, s = c.nc, Stage(c, "L1_attn")
    w = c.at(0, 2048).rearrange("p (w n) -> p w n", n=D)
    wT = c.at(2048, 2048).rearrange("p (w k n) -> p w k n", w=4, k=KT)
    bias = c.at(15360, 8)
    ob = c.at(15368, D)
    W = 15700
    wq4 = c.at(W, 2048).rearrange("p (w n) -> p w n", n=D)
    wqT = c.at(W + 2048, 2048).rearrange("p (w k n) -> p w k n", w=4, k=KT)
    W += 4096
    src, res, cbx = (c.at(W + i * 2 * NT, 2 * NT) for i in range(3))
    W += 6 * NT
    small = c.at(W, 320)
    cb = c.at(W + 320, 28)
    wsc = c.at(W + 352, 16)
    W += 376
    vT = c.at(W, 1024).rearrange("p (k b t) -> p k b t", k=KT, b=B)
    W += 1024
    at = SmallHeads(c, s, W, 8, 8 ** -0.5, None)
    resP = at.p.rearrange("p i e t -> p (i e t)")[:, 0:1024].rearrange("p (k b t) -> p k b t", k=KT, b=B)
    cbP = at.p.rearrange("p i e t -> p (i e t)")[:, 1024:2048].rearrange("p (k b t) -> p k b t", k=KT, b=B)
    tm_in, tmax_in, quant, wq_in, wt_mm, wt_in, proj, got, vt_in, v_mm, resp_in = (
        s.sem(x) for x in ("tm_in", "tmax_in", "quant", "wq_in", "wt_mm", "wt_in", "proj", "got", "vt_in", "v_mm",
                           "resp_in"))
    small_at = 8 * KT * CH
    tm, tmax = small[:, small_at:small_at + CH], small[:, small_at + CH:small_at + 2 * CH]

    def project(pe, bank, w_, m_):
        for k in range(KT):
            nc.tensor.matmul(c.ps[:, bank, 0:NT], wqT[:, w_, k, m_ * 128:(m_ + 1) * 128],
                             res[:, k * NT:(k + 1) * NT], start=(k == 0), stop=False)
        for k in range(KT):
            m = nc.tensor.matmul(c.ps[:, bank, 0:NT], wT[:, w_, k, m_ * 128:(m_ + 1) * 128],
                                 cbx[:, k * NT:(k + 1) * NT], start=False, stop=(k == KT - 1))
        return m

    with nc.Block(no_gpsimd_drain=True) as block:
        @block.sync
        def _(sp):
            c.load(sp, "L1_attn", now)
            prefetch(sp)

        @block.gpsimd
        def _(pool):
            at.pool(pool)
            nc.gpsimd.memset(vT[:, :, :, T:TP], 0.0).then_inc(*at.padded.next())
            pool.wait_ge(at.padded.handle, at.padded.at(at.padded.n))
            for n in range(2):
                pool.wait_ge(tm_in.handle, tm_in.at(n + 1))
                nc.gpsimd.partition_all_reduce(tmax, tm, 128, bass.bass_isa.ReduceOp.max).then_inc(*tmax_in.next())
                pool.wait_ge(tmax_in.handle, tmax_in.at(n + 1))

        @block.tensor
        def _(pe):
            pe.wait_ge(c.loaded["L1_attn"].handle, 16 * c.expect["L1_attn"])
            pe.wait_ge(wq_in.handle, wq_in.at(1))
            for w_ in range(4):
                for k in range(KT):
                    for o in range(2):
                        t = nc.tensor.transpose(c.ps[:, 2 + w_, k * D + o * 128:k * D + (o + 1) * 128],
                                                wq4[:, 2 * w_ + o, k * 128:(k + 1) * 128], c.ident[:])
                t.then_inc(*wt_mm.next())
            pe.wait_ge(wt_in.handle, wt_in.at(4))
            pe.wait_ge(quant.handle, quant.at(1))
            for n in range(6):
                project(pe, 2 + n, n // 2, n % 2).then_inc(*proj.next())
            pe.wait_ge(vt_in.handle, vt_in.at(4))
            pe.wait_ge(at.padded.handle, at.padded.at(at.nm + 2))
            for g in range(4):
                for k in range(KT):
                    t = nc.tensor.transpose(c.ps[:, g // 2, (g % 2) * D + k * 128:(g % 2) * D + (k + 1) * 128],
                                            vT[:, k, 2 * g:2 * g + 2, :], c.ident[:])
            t.then_inc(*v_mm.next())
            at.tensor(pe, 2 * at.nm, 2, 2)
            pe.wait_ge(resp_in.handle, resp_in.at(2))
            for k in range(KT):
                for j in range(J):
                    project_out(c, pe, j, k, resP[:, k, 2 * j:2 * j + 2, :], wqT[:, 3, k, :], k == 0, False)
                    m = project_out(c, pe, j, k, cbP[:, k, 2 * j:2 * j + 2, :], wT[:, 3, k, :], False, k == KT - 1)
            m.then_inc(*s.y_done.next())
            norm_tensor(c, s, pe, False)

        @block.scalar
        def _(act):
            for w_ in range(4):
                act.wait_ge(wt_mm.handle, wt_mm.at(w_ + 1))
                nc.scalar.copy(wqT[:, w_].rearrange("p k n -> p (k n)"), c.ps[:, 2 + w_, :]).then_inc(*wt_in.next())
                act.wait_ge(wt_in.handle, wt_in.last())
            act.wait_ge(at.padded.handle, at.padded.at(at.nm + 2))
            for k in range(KT):
                act.wait_ge(proj.handle, proj.at(2 + k + 1))
                nc.scalar.activation(at.k[:, k, :, 0:T], valid(c.ps[:, 4 + k, 0:NT]), ACT.Identity,
                                          bias=bias[:, 2 + k:3 + k]).then_inc(*at.k_in.next())
                act.wait_ge(at.k_in.handle, at.k_in.last())
            for k in range(KT):
                act.wait_ge(proj.handle, proj.at(4 + k + 1))
                for r in range(2):
                    nc.scalar.activation(
                        vT[:, k].rearrange("p (a e r) t -> p r a e t", e=2, r=2)[:, r, :, :, 0:T],
                        c.ps[:, 6 + k, 0:NT].rearrange("p (a r e t) -> p r a e t", a=2, r=2, e=2)[:, r],
                        ACT.Identity, bias=bias[:, 4 + k:5 + k]).then_inc(*vt_in.next())
                    act.wait_ge(vt_in.handle, vt_in.last())
            act.wait_ge(v_mm.handle, v_mm.at(1))
            for i in range(2):
                nc.scalar.copy(at.v[:, 2 * i:2 * i + 2, :].rearrange("p g n -> p (g n)"), c.ps[:, i, :]).then_inc(*at.v_in.next())
                act.wait_ge(at.v_in.handle, at.v_in.last())
            at.scalar(act)
            norm_scalar(c, s, act, False)

        @block.vector
        def _(dve):
            V = nc.vector

            dve.wait_ge(c.loaded["L1_attn"].handle, 16 * c.expect["L1_attn"])
            V.tensor_reduce(wsc[:, 0:8], w, AX.X, ALU.max, apply_absolute_value=True).then_inc(*s.dve_chain.next())
            dve.wait_ge(s.dve_chain.handle, s.dve_chain.last())
            V.tensor_scalar(wsc[:, 0:8], wsc[:, 0:8], 1.0 / 7.0, 1e-9, ALU.mult, ALU.max).then_inc(*s.dve_chain.next())
            dve.wait_ge(s.dve_chain.handle, s.dve_chain.last())
            V.reciprocal(wsc[:, 8:16], wsc[:, 0:8]).then_inc(*s.dve_chain.next())
            dve.wait_ge(s.dve_chain.handle, s.dve_chain.last())
            V.tensor_tensor(wq4, w, wsc[:, 8:16].unsqueeze(2).broadcast_to([128, 8, D]), ALU.mult).then_inc(*s.dve_chain.next())
            dve.wait_ge(s.dve_chain.handle, s.dve_chain.last())
            V.tensor_scalar(wq4, wq4, MAGIC, MAGIC, ALU.add, ALU.subtract).then_inc(*s.dve_chain.next())
            dve.wait_ge(s.dve_chain.handle, s.dve_chain.last())
            V.tensor_scalar(wq4, wq4, 7.0, -8.0, ALU.min, ALU.max).then_inc(*s.dve_chain.next())
            dve.wait_ge(s.dve_chain.handle, s.dve_chain.last())
            V.tensor_tensor(wq4, wq4, wsc[:, 0:8].unsqueeze(2).broadcast_to([128, 8, D]), ALU.mult).then_inc(*wq_in.next())
            dve.wait_ge(wq_in.handle, wq_in.last())
            for k in range(KT):
                V.tensor_copy(valid(src[:, k * NT:(k + 1) * NT]), c.x_feat[:, k, :, 0:T]).then_inc(*s.dve_chain.next())
                dve.wait_ge(s.dve_chain.handle, s.dve_chain.last())
            quantise(c, s, dve, tm_in, tmax_in, src, res, cbx, cb, small, quant)
            V.tensor_tensor(c.x_tok[:], c.x_tok[:], ob.unsqueeze(1).broadcast_to([128, J, D]), ALU.add).then_inc(*s.dve_chain.next())
            dve.wait_ge(s.dve_chain.handle, s.dve_chain.last())
            dve.wait_ge(at.padded.handle, at.padded.at(at.nm + 2))
            for k in range(KT):
                dve.wait_ge(proj.handle, proj.at(k + 1))
                for m in range(at.nm):
                    V.tensor_scalar(at.q[:, m, k, :, 0:T], valid(c.ps[:, 2 + k, 0:NT]), bias[:, k:k + 1],
                                         c.heads8[:, m:m + 1], ALU.add, ALU.mult).then_inc(*at.q_in.next())
                    dve.wait_ge(at.q_in.handle, at.q_in.last())
            at.vector(dve)
            for k in range(KT):
                dve.wait_ge(at.ctxT_in.handle, at.ctxT_in.at(k + 1))
                V.tensor_copy(valid(src[:, k * NT:(k + 1) * NT]), at.ctxT[:, k, :, 0:T]).then_inc(*s.dve_chain.next())
                dve.wait_ge(s.dve_chain.handle, s.dve_chain.last())
            quantise(c, s, dve, tm_in, tmax_in, src, res, cbx, cb, small, quant)
            V.memset(resP[:, :, :, T:TP], 0.0).then_inc(*s.dve_chain.next())
            dve.wait_ge(s.dve_chain.handle, s.dve_chain.last())
            V.memset(cbP[:, :, :, T:TP], 0.0).then_inc(*s.dve_chain.next())
            dve.wait_ge(s.dve_chain.handle, s.dve_chain.last())
            V.tensor_copy(resP[:, :, :, 0:T].rearrange("p k b t -> p (k b) t"),
                               res.rearrange("p (a t) -> p a t", t=T)).then_inc(*resp_in.next())
            dve.wait_ge(resp_in.handle, resp_in.last())
            V.tensor_copy(cbP[:, :, :, 0:T].rearrange("p k b t -> p (k b) t"),
                               cbx.rearrange("p (a t) -> p a t", t=T)).then_inc(*resp_in.next())
            dve.wait_ge(resp_in.handle, resp_in.last())
            norm_vector(c, s, dve, False)



def L1_X_LOADS(c):
    return [("L1x_Wq", c.at(4096, 512)), ("L1x_Wkv", c.at(4608, 512, 64)), ("L1x_Wout", c.at(5120, 512)),
            ("L1x_lat", c.at(5632, 512, 64)), ("causal_add", c.at(37700, T))]


def output_of(c, s, at, pe, wo):
    pe.wait_ge(at.ctxT_in.handle, at.ctxT_in.at(KT))
    for k in range(KT):
        for j in range(J):
            m = project_out(c, pe, j, k, at.ctxT[:, k, 2 * j:2 * j + 2, :], wo[:, k, :], k == 0, k == KT - 1)
    m.then_inc(*s.y_done.next())


def l1_cross(c, now, prefetch):
    nc, s = c.nc, Stage(c, "L1_xattn")
    wq = c.at(4096, 512).rearrange("p (k n) -> p k n", k=KT)
    wkv = c.at(4608, 512, 64)
    wo = c.at(5120, 512).rearrange("p (k n) -> p k n", k=KT)
    lat = c.at(5632, 512, 64).rearrange("p (b t) -> p b t", b=B)
    mask = c.at(37700, T)
    at = SmallHeads(c, s, 15360, 16, 0.25, mask)
    proj = s.sem("proj")

    with nc.Block(no_gpsimd_drain=True) as block:
        @block.sync
        def _(sp):
            c.load(sp, "L1_xattn", now)
            prefetch(sp)

        @block.gpsimd
        def _(pool):
            at.pool(pool)

        @block.tensor
        def _(pe):
            pe.wait_ge(c.loaded["L1_xattn"].handle, 16 * c.expect["L1_xattn"])
            for m_ in range(2):
                for k in range(KT):
                    m = nc.tensor.matmul(c.ps[:, 2 + m_, 0:NT], wq[:, k, m_ * 128:(m_ + 1) * 128],
                                         c.x_feat[:, k, :, 0:T], start=(k == 0), stop=(k == KT - 1))
                m.then_inc(*proj.next())
            for m_ in range(2):
                m = nc.tensor.matmul(c.ps[:, 4 + m_, 0:NT], wkv[:, m_ * 128:(m_ + 1) * 128], lat[:, :, 0:T],
                                     start=True, stop=True)
                m.then_inc(*proj.next())
            for g in range(4):
                m = value_tile(c, c.ps[:, 6 + g // 2, (g % 2) * D:(g % 2 + 1) * D], [lat], g, [wkv[:, D:2 * D]])
            m.then_inc(*proj.next())
            at.tensor(pe, 2 * at.nm, 2, 2)
            output_of(c, s, at, pe, wo)
            norm_tensor(c, s, pe, False)

        @block.scalar
        def _(act):
            act.wait_ge(at.padded.handle, at.padded.at(at.nm + 1))
            for k in range(KT):
                act.wait_ge(proj.handle, proj.at(k + 1))
                for m in range(at.nm):
                    nc.scalar.activation(at.q[:, m, k, :, 0:T], valid(c.ps[:, 2 + k, 0:NT]), ACT.Copy,
                                              scale=c.heads16[:, m:m + 1]).then_inc(*at.q_in.next())
                    act.wait_ge(at.q_in.handle, at.q_in.last())
            for k in range(KT):
                act.wait_ge(proj.handle, proj.at(2 + k + 1))
                nc.scalar.copy(at.k[:, k, :, 0:T], valid(c.ps[:, 4 + k, 0:NT])).then_inc(*at.k_in.next())
                act.wait_ge(at.k_in.handle, at.k_in.last())
            at.scalar(act)
            norm_scalar(c, s, act, False)

        @block.vector
        def _(dve):
            dve.wait_ge(c.loaded["L1_xattn"].handle, 16 * c.expect["L1_xattn"])
            dve.wait_ge(proj.handle, proj.at(5))
            for i in range(2):
                nc.vector.tensor_copy(at.v[:, 2 * i:2 * i + 2, :].rearrange("p g n -> p (g n)"), c.ps[:, 6 + i, :]).then_inc(*at.v_in.next())
                dve.wait_ge(at.v_in.handle, at.v_in.last())
            at.vector(dve)
            norm_vector(c, s, dve, False)



def L2_ATTN_LOADS(c):
    return [("L2a_W", c.at(32500, 5 * 512)), ("L2a_Wo", c.at(35060, 512)), ("L2a_rope", c.at(35572, 2 * T)),
            ("causal_add2", c.at(35684, T))]


def l2_attention(c, now, prefetch):
    nc, s = c.nc, Stage(c, "L2_attn")
    w = c.at(32500, 5 * 512).rearrange("p (w k n) -> p w k n", w=5, k=KT)
    wo = c.at(35060, 512).rearrange("p (k n) -> p k n", k=KT)
    tab = c.at(35572, 2 * T).rearrange("p (i t) -> p i t", i=2)
    mask = c.at(35684, T)
    at = SmallHeads(c, s, 16384, 16, 0.25, mask)
    prod = [c.at(at.end + i * NT, NT) for i in range(2)]
    turned_q = [c.at(at.end + (2 + i) * NT, NT) for i in range(2)]
    proj, rotated = s.sem("proj"), s.sem("rotated")

    with nc.Block(no_gpsimd_drain=True) as block:
        @block.sync
        def _(sp):
            c.load(sp, "L2_attn", now)
            prefetch(sp)

        @block.gpsimd
        def _(pool):
            at.pool(pool)

        @block.tensor
        def _(pe):
            pe.wait_ge(c.loaded["L2_attn"].handle, 16 * c.expect["L2_attn"])
            for n in range(8):
                w_, m_ = n // 4 * 2 + n % 2, n // 2 % 2
                for k in range(KT):
                    m = nc.tensor.matmul(c.ps[:, n, 0:NT], w[:, w_, k, m_ * 128:(m_ + 1) * 128],
                                         c.x_feat[:, k, :, 0:T], start=(k == 0), stop=(k == KT - 1))
                m.then_inc(*proj.next())
            pe.wait_ge(rotated.handle, rotated.at(2))
            for g in range(4):
                m = value_tile(c, c.ps[:, g // 2, (g % 2) * D:(g % 2 + 1) * D], [c.x_feat[:, k] for k in range(KT)],
                               g, [w[:, 4, k, :] for k in range(KT)])
            m.then_inc(*proj.next())
            at.tensor(pe, 2 * at.nm, 2, 2)
            output_of(c, s, at, pe, wo)
            norm_tensor(c, s, pe, False)

        @block.scalar
        def _(act):
            act.wait_ge(at.padded.handle, at.padded.at(at.nm + 1))
            for k in range(KT):
                act.wait_ge(rotated.handle, rotated.at(k + 1))
                for m in range(at.nm):
                    nc.scalar.activation(at.q[:, m, k, :, 0:T], valid(turned_q[k]), ACT.Copy,
                                              scale=c.heads16[:, m:m + 1]).then_inc(*at.q_in.next())
                    act.wait_ge(at.q_in.handle, at.q_in.last())
            act.wait_ge(proj.handle, proj.at(9))
            for i in range(2):
                nc.scalar.copy(at.v[:, 2 * i:2 * i + 2, :].rearrange("p g n -> p (g n)"), c.ps[:, i, :]).then_inc(*at.v_in.next())
                act.wait_ge(at.v_in.handle, at.v_in.last())
            at.scalar(act)
            norm_scalar(c, s, act, False)

        @block.vector
        def _(dve):
            V = nc.vector
            dve.wait_ge(c.loaded["L2_attn"].handle, 16 * c.expect["L2_attn"])
            for n in range(4):
                dve.wait_ge(proj.handle, proj.at(2 * n + 2))
                for i in range(2):
                    V.tensor_tensor(valid(prod[i]), valid(c.ps[:, 2 * n + i, 0:NT]),
                                         tab[:, i, :].unsqueeze(1).broadcast_to([128, B, T]), ALU.mult).then_inc(*s.dve_chain.next())
                    dve.wait_ge(s.dve_chain.handle, s.dve_chain.last())
                if n < 2:
                    V.tensor_tensor(turned_q[n], prod[0], prod[1], ALU.add).then_inc(*rotated.next())
                    dve.wait_ge(rotated.handle, rotated.last())
                else:
                    V.tensor_tensor(at.k[:, n - 2, :, 0:T], valid(prod[0]), valid(prod[1]), ALU.add).then_inc(*at.k_in.next())
                    dve.wait_ge(at.k_in.handle, at.k_in.last())
            at.vector(dve)
            norm_vector(c, s, dve, False)



def L3_ATTN_LOADS(c):
    return [("L3a_wq", c.at(0, 4096)), ("L3a_wk", c.at(4096, 4096)), ("L3a_wv", c.at(8192, 4096)),
            ("L3a_wo", c.at(12288, 4096)), ("L3a_B", c.at(24100, 2048)), ("L3a_A", c.at(26148, 768)),
            ("L3a_oB", c.at(26916, 256))]


def L3_ATTN_SMALL(c):
    return [("L3a_norm", c.at(23900, 2)), ("L3a_rope", c.at(23902, 2 * T)), ("causal_add3", c.at(24014, T))]


def l3_attention(c, now, prefetch):
    nc, s = c.nc, Stage(c, "L3_attn")
    w = [c.at(4096 * i, 4096) for i in range(4)]
    Bm = c.at(24100, 2048)
    Am = c.at(26148, 768).rearrange("p (i n) -> p i n", i=3)
    oB = c.at(26916, 256)
    normw = c.at(23900, 2)
    tab = c.at(23902, 2 * T).rearrange("p (i t) -> p i t", i=2)
    mask = c.at(24014, T)
    v = c.at(27200, 8192).rearrange("p (g n) -> p g n", g=4)
    W = 16384
    hf = c.at(W, 1024).rearrange("p (k b t) -> p k b t", k=KT, b=B)
    hx = c.at(W + 1024, 1024).rearrange("p (j n) -> p j n", j=J)
    q = [c.at(W + 2048 + 512 * i, 512).rearrange("p (b t) -> p b t", b=B) for i in range(2)]
    kk = [c.at(W + 3072 + NT * i, NT).rearrange("p (b t) -> p b t", b=B) for i in range(2)]
    prod = [c.at(W + 3968 + NT * i, NT) for i in range(4)]
    p = [c.at(W + 5760 + 256 * i, 256).rearrange("p (j t) -> p j t", j=J) for i in range(2)]
    pT = [c.at(W + 6272 + 256 * i, 256).rearrange("p (g q) -> p g q", g=2) for i in range(2)]
    small = c.at(W + 6784, 64)
    yT = [c.at(35400 + 512 * i, 512).rearrange("p (b t) -> p b t", b=B) for i in range(2)]
    ms_in, rms_in, h_in, h_t, hf_in, padded = (s.sem(x) for x in ("ms_in", "rms_in", "h_in", "h_t", "hf_in", "padded"))
    lora_mm, lora_in, v_mm, v_act, v_dve = (s.sem(x) for x in ("lora_mm", "lora_in", "v_mm", "v_act", "v_dve"))
    q_mm, k_mm, prod_in, qk_in, scored, shifted, exped, p_in, turned, pt_in, y_mm, y_in, out_mm = (
        s.sem(x) for x in ("q_mm", "k_mm", "prod_in", "qk_in", "scored", "shifted", "exped", "p_in", "turned",
                           "pt_in", "y_mm", "y_in", "out_mm"))
    NL = 32

    def lora_target(n):
        i, r = n // 8, n % 8
        if i < 3:
            return w[i].rearrange("p (k n) -> p k n", k=KT)[:, r // 4, (r % 4) * 512:(r % 4 + 1) * 512]
        return w[3][:, r * 512:(r + 1) * 512]

    with nc.Block(no_gpsimd_drain=True) as block:
        @block.sync
        def _(sp):
            c.load(sp, "L3_small", L3_ATTN_SMALL(c))
            c.load(sp, "L3_attn", now)
            sp.wait_ge(v_mm.handle, v_mm.at(16))
            sp.wait_ge(lora_mm.handle, lora_mm.at(NL))
            sp.wait_ge(lora_in.handle, lora_in.at(NL))
            prefetch(sp)

        @block.gpsimd
        def _(pool):
            for i in range(2):
                nc.gpsimd.memset(q[i][:, :, T:TP], 0.0).then_inc(*padded.next())
                nc.gpsimd.memset(yT[i][:, :, T:TP], 0.0).then_inc(*padded.next())
                nc.gpsimd.memset(p[i][:, :, T:TP], 0.0).then_inc(*padded.next())
            pool.wait_ge(padded.handle, padded.at(6))
            for n in range(2 * NH):
                pool.wait_ge(prod_in.handle, prod_in.at(n + 1))
                h = n // 2
                if h - 1 > 0:
                    pool.wait_ge(scored.handle, scored.at(h - 1))
                a, b = prod[2 * (n % 2)], prod[2 * (n % 2) + 1]
                dst = q[h % 2][:, :, 0:T] if n % 2 == 0 else kk[h % 2]
                nc.gpsimd.tensor_tensor(dst, valid(a), valid(b), ALU.add).then_inc(*qk_in.next())
                pool.wait_ge(qk_in.handle, qk_in.at(n + 1))

        @block.tensor
        def _(pe):
            pe.wait_ge(c.loaded["L3_attn"].handle, 16 * c.expect["L3_attn"])
            for n in range(NL):
                if n - 5 > 0:
                    pe.wait_ge(lora_in.handle, lora_in.at(n - 5))
                i, r = n // 8, n % 8
                bank = c.ps[:, 2 + n % 6, :]
                if i < 3:
                    m = nc.tensor.matmul(bank, Am[:, i, (r // 4) * 128:(r // 4 + 1) * 128],
                                         Bm[:, (r % 4) * 512:(r % 4 + 1) * 512], start=True, stop=True)
                else:
                    for e in range(2):
                        m = nc.tensor.matmul(bank[:, e * D:(e + 1) * D],
                                             Bm[:, (2 * r + e) * 128:(2 * r + e + 1) * 128], oB, start=True, stop=True)
                m.then_inc(*lora_mm.next())
            for j in range(J):
                pe.wait_ge(h_in.handle, h_in.at(j + 1))
                for k in range(KT):
                    t = nc.tensor.transpose(c.ps[:, k, j * 128:(j + 1) * 128], hx[:, j, k * 128:(k + 1) * 128],
                                            c.ident[:])
            t.then_inc(*h_t.next())
            pe.wait_ge(hf_in.handle, hf_in.at(2))
            pe.wait_ge(lora_in.handle, lora_in.at(NL))
            wv = w[2].rearrange("p (k n) -> p k n", k=KT)
            for n in range(16):
                g, r = n // 4, n % 4
                if n >= 6:
                    done = v_dve if n % 2 else v_act
                    if (n - 6) // 2 + 1 > 0:
                        pe.wait_ge(done.handle, done.at((n - 6) // 2 + 1))
                m = value_tile(c, c.ps[:, 2 + n % 6, :], [hf[:, k] for k in range(KT)], g,
                               [wv[:, k, r * 512:(r + 1) * 512] for k in range(KT)])
                m.then_inc(*v_mm.next())
            pe.wait_ge(v_act.handle, v_act.at(8))
            pe.wait_ge(v_dve.handle, v_dve.at(8))
            pe.wait_ge(padded.handle, padded.at(6))
            wq, wk = (w[i].rearrange("p (k n) -> p k n", k=KT) for i in range(2))

            def qk(h):
                if 2 * h > 0:
                    pe.wait_ge(prod_in.handle, prod_in.at(2 * h))
                for k in range(KT):
                    m = nc.tensor.matmul(c.ps[:, 2, 0:NT], wq[:, k, h * HD:(h + 1) * HD], hf[:, k, :, 0:T],
                                         start=(k == 0), stop=(k == KT - 1))
                m.then_inc(*q_mm.next())
                for k in range(KT):
                    m = nc.tensor.matmul(c.ps[:, 3, 0:NT], wk[:, k, h * HD:(h + 1) * HD], hf[:, k, :, 0:T],
                                         start=(k == 0), stop=(k == KT - 1))
                m.then_inc(*k_mm.next())

            def scores(h):
                pe.wait_ge(qk_in.handle, qk_in.at(2 * h + 2))
                if h > 0:
                    pe.wait_ge(shifted.handle, shifted.at(h))
                for b in range(B):
                    m = nc.tensor.matmul(c.ps[(b % 2) * TP:(b % 2 + 1) * TP, 4, (b // 2) * T:(b // 2 + 1) * T],
                                         q[h % 2][:, b, :], kk[h % 2][:, b, :], start=True, stop=True)
                m.then_inc(*scored.next())

            def context(h):
                pe.wait_ge(p_in.handle, p_in.at(h + 1))
                if h > 0:
                    pe.wait_ge(pt_in.handle, pt_in.at(h))
                for g in range(2):
                    t = nc.tensor.transpose(c.ps[:, 5, g * 128:(g + 1) * 128], p[h % 2][:, 2 * g:2 * g + 2, :], c.ident[:])
                t.then_inc(*turned.next())
                pe.wait_ge(pt_in.handle, pt_in.at(h + 1))
                if 2 * h > 0:
                    pe.wait_ge(y_in.handle, y_in.at(2 * h))
                for g in range(4):
                    for r in range(2):
                        m = nc.tensor.matmul(c.ps[:, 6 + r, g * T:(g + 1) * T],
                                             v[r * TP:r * TP + T, g, h * HD:(h + 1) * HD],
                                             pT[h % 2][r * TP:r * TP + T, g // 2, (g % 2) * TP:(g % 2) * TP + T],
                                             start=True, stop=True)
                m.then_inc(*y_mm.next())

            def out(h):
                pe.wait_ge(y_in.handle, y_in.at(2 * (h + 1)))
                for j in range(J):
                    m = project_out(c, pe, j, h, yT[h % 2][:, 2 * j:2 * j + 2, :],
                                    w[3].rearrange("p (h n) -> p h n", h=NH)[:, h, :], h == 0, h == NH - 1)
                m.then_inc(*out_mm.next())

            for h in range(NH + 3):
                if h < NH:
                    qk(h)
                if 1 <= h <= NH:
                    scores(h - 1)
                if 2 <= h <= NH + 1:
                    context(h - 2)
                if h >= 3:
                    out(h - 3)
            pe.wait_ge(out_mm.handle, out_mm.at(NH))
            pe.sem_inc(*s.y_done.next())
            norm_tensor(c, s, pe, False)

        @block.scalar
        def _(act):
            act.wait_ge(ms_in.handle, ms_in.at(1))
            nc.scalar.activation(small[:, 4:8], small[:, 4:8], ACT.Sqrt).then_inc(*rms_in.next())
            act.wait_ge(rms_in.handle, rms_in.last())
            act.wait_ge(h_t.handle, h_t.at(1))
            act.wait_ge(c.loaded["L3_small"].handle, 16 * 3)
            for k in range(KT):
                nc.scalar.activation(hf[:, k, :, :], c.ps[:, k, :].rearrange("p (b t) -> p b t", b=B), ACT.Copy,
                                          scale=normw[:, k:k + 1]).then_inc(*hf_in.next())
                act.wait_ge(hf_in.handle, hf_in.last())
            for n in range(0, 16, 2):
                act.wait_ge(v_mm.handle, v_mm.at(n + 1))
                nc.scalar.copy(v[:, n // 4, (n % 4) * 512:(n % 4 + 1) * 512], c.ps[:, 2 + n % 6, :]).then_inc(*v_act.next())
                act.wait_ge(v_act.handle, v_act.last())
            for h in range(NH + 1):
                if h < NH:
                    act.wait_ge(shifted.handle, shifted.at(h + 1))
                    nc.scalar.activation(p[h % 2][:, :, 0:T], p[h % 2][:, :, 0:T], ACT.Exp, scale=HD ** -0.5).then_inc(*exped.next())
                    act.wait_ge(exped.handle, exped.last())
                    act.wait_ge(turned.handle, turned.at(h + 1))
                    if h - 1 > 0:
                        act.wait_ge(y_mm.handle, y_mm.at(h - 1))
                    nc.scalar.copy(pT[h % 2].rearrange("p g q -> p (g q)"), c.ps[:, 5, 0:256]).then_inc(*pt_in.next())
                    act.wait_ge(pt_in.handle, pt_in.last())
                    act.wait_ge(y_mm.handle, y_mm.at(h + 1))
                    if h - 1 > 0:
                        act.wait_ge(out_mm.handle, out_mm.at(h - 1))
                    for r in range(2):
                        nc.scalar.copy(yT[h % 2].rearrange("p (a r e) t -> p r a e t", r=2, e=2)[:, r, :, :, 0:T],
                                            c.ps[:, 6 + r, 0:4 * T].rearrange("p (a e t) -> p a e t", a=2, e=2)).then_inc(*y_in.next())
                        act.wait_ge(y_in.handle, y_in.last())
            norm_scalar(c, s, act, False)

        @block.vector
        def _(dve):
            V = nc.vector
            for j in range(J):
                V.tensor_tensor(hx[:, j, :], c.x_tok[:, j, :], c.x_tok[:, j, :], ALU.mult).then_inc(*s.dve_chain.next())
                dve.wait_ge(s.dve_chain.handle, s.dve_chain.last())
                V.tensor_reduce(small[:, j:j + 1], hx[:, j, :], AX.X, ALU.add).then_inc(*s.dve_chain.next())
                dve.wait_ge(s.dve_chain.handle, s.dve_chain.last())
            V.tensor_scalar(small[:, 4:8], small[:, 0:4], 1.0 / D, 1e-6, ALU.mult, ALU.add).then_inc(*ms_in.next())
            dve.wait_ge(ms_in.handle, ms_in.last())
            dve.wait_ge(rms_in.handle, rms_in.at(1))
            V.reciprocal(small[:, 8:12], small[:, 4:8]).then_inc(*s.dve_chain.next())
            dve.wait_ge(s.dve_chain.handle, s.dve_chain.last())
            for j in range(J):
                V.tensor_scalar(hx[:, j, :], c.x_tok[:, j, :], small[:, 8 + j:9 + j], None, ALU.mult).then_inc(*h_in.next())
                dve.wait_ge(h_in.handle, h_in.last())
            V.tensor_scalar(c.x_tok[:], c.x_tok[:], 2.0, None, ALU.mult).then_inc(*s.dve_chain.next())
            dve.wait_ge(s.dve_chain.handle, s.dve_chain.last())
            dve.wait_ge(c.loaded["L3_attn"].handle, 16 * c.expect["L3_attn"])
            dve.wait_ge(c.loaded["L3_small"].handle, 16 * 3)
            for n in range(NL):
                dve.wait_ge(lora_mm.handle, lora_mm.at(n + 1))
                t = lora_target(n)
                V.scalar_tensor_tensor(out=t, in0=c.ps[:, 2 + n % 6, :], scalar=1.0 / 16, in1=t,
                                            op0=ALU.mult, op1=ALU.add).then_inc(*lora_in.next())
                dve.wait_ge(lora_in.handle, lora_in.last())
            for n in range(1, 16, 2):
                dve.wait_ge(v_mm.handle, v_mm.at(n + 1))
                V.tensor_copy(v[:, n // 4, (n % 4) * 512:(n % 4 + 1) * 512], c.ps[:, 2 + n % 6, :]).then_inc(*v_dve.next())
                dve.wait_ge(v_dve.handle, v_dve.last())
            dve.wait_ge(padded.handle, padded.at(6))

            def rotate(n):
                h, i = n // 2, n % 2
                done = k_mm if i else q_mm
                dve.wait_ge(done.handle, done.at(h + 1))
                if n - 1 > 0:
                    dve.wait_ge(qk_in.handle, qk_in.at(n - 1))
                b = c.ps[:, 2 + i, 0:NT]
                V.tensor_tensor(valid(prod[2 * i]), valid(b), tab[:, 0, :].unsqueeze(1).broadcast_to([128, B, T]),
                                       ALU.mult).then_inc(*s.dve_chain.next())
                for e in range(2):
                    lo, hi = e * 64, (1 - e) * 64
                    ins = V.tensor_tensor(valid(prod[2 * i + 1])[lo:lo + 64], valid(b)[hi:hi + 64],
                                          tab[hi:hi + 64, 1, :].unsqueeze(1).broadcast_to([64, B, T]), ALU.mult)
                    if e:
                        ins.then_inc(*prod_in.next())
                        dve.wait_ge(prod_in.handle, prod_in.last())
                    else:
                        ins.then_inc(*s.dve_chain.next())

            def shift(h):
                dve.wait_ge(scored.handle, scored.at(h + 1))
                if h - 1 > 0:
                    dve.wait_ge(turned.handle, turned.at(h - 1))
                r = p[h % 2][:, :, 0:T]
                V.tensor_tensor(r, c.ps[:, 4, 0:4 * T].rearrange("p (j t) -> p j t", j=J),
                                     mask.unsqueeze(1).broadcast_to([128, J, T]), ALU.add).then_inc(*s.dve_chain.next())
                dve.wait_ge(s.dve_chain.handle, s.dve_chain.last())
                V.tensor_reduce(small[:, 16:20], r, AX.X, ALU.max).then_inc(*s.dve_chain.next())
                dve.wait_ge(s.dve_chain.handle, s.dve_chain.last())
                V.tensor_tensor(r, r, small[:, 16:20].unsqueeze(2).broadcast_to([128, J, T]), ALU.subtract).then_inc(*shifted.next())
                dve.wait_ge(shifted.handle, shifted.last())

            def divide(h):
                dve.wait_ge(exped.handle, exped.at(h + 1))
                r = p[h % 2][:, :, 0:T]
                V.tensor_reduce(small[:, 20:24], r, AX.X, ALU.add).then_inc(*s.dve_chain.next())
                dve.wait_ge(s.dve_chain.handle, s.dve_chain.last())
                V.reciprocal(small[:, 24:28], small[:, 20:24]).then_inc(*s.dve_chain.next())
                dve.wait_ge(s.dve_chain.handle, s.dve_chain.last())
                V.tensor_tensor(r, r, small[:, 24:28].unsqueeze(2).broadcast_to([128, J, T]), ALU.mult).then_inc(*p_in.next())
                dve.wait_ge(p_in.handle, p_in.last())

            for h in range(NH + 1):
                if h < NH:
                    rotate(2 * h)
                    rotate(2 * h + 1)
                if h >= 1:
                    shift(h - 1)
                    divide(h - 1)
            norm_vector(c, s, dve, False)



def ffn_specs():
    sh = lambda n, w=128: (w, n, None)
    return {
        "L0_ffn": Experts(128, 128, 4, [sh(0), sh(1)] + [(128, 2, k) for k in range(8)], 1280,
                          29696, 32256, 34816, 3, 35584, 22000, 35840),
        "L1_ffn": Experts(16, 16, 2, [sh(0), sh(1)] + [(128, 2 + e, e) for e in range(16)], 2304,
                          6144, 10752, 25780, 18, 32448, 30400, 32480),
        "L2_ffn": Experts(9, 8, 2, [(128, n, n) for n in range(10)], 1280,
                          29696, 32256, 34816, 10, 37376, 22000, 37400),
        "L3_ffn": Experts(8, 8, 2, [sh(0), sh(1), sh(2, 96)] + [(128, 3 + n, n) for n in range(11)], 1792,
                          29696, 33280, 0, 14, 24048, 22000, 24064),
    }


def ffn_loads(c, name, f):
    tag = name[:2] + "f"
    d = {"gate": (tag + "_gate", c.at(f.gate, KT * f.hidden)), "up": (tag + "_up", c.at(f.up, KT * f.hidden)),
         "down": (tag + "_down", c.at(f.down, f.downs * D)), "router": (tag + "_router", c.at(f.router, KT * f.cols))}
    if name != "L0_ffn":
        n = {"L1_ffn": 16, "L2_ffn": 10, "L3_ffn": 11}[name]
        d["spread"] = (tag + "_spread", c.at(f.spread, n * 128))
    if name == "L0_ffn":
        d["extra"] = (tag + "_mix", c.at(f.extra, 17))
    if name == "L1_ffn":
        d["extra"] = (tag + "_bias", c.at(f.extra, 16))
    return d


def decoder_program(nc, dram, out):
    with ExitStack() as ctx:
        c = Core(nc, ctx, dram)
        c.sb_small = ctx.enter_context(nc.sbuf_tensor("softmax_stats", [128, 12], F32))
        spec = ffn_specs()
        fl = {n: ffn_loads(c, n, spec[n]) for n in spec}
        x0, x2, x3 = X_WEIGHTS(c, X_AT, "L0x"), X_WEIGHTS(c, X_AT, "L2x"), X_WEIGHTS(c, X3_AT, "L3x")
        pick = lambda d, *keys: [d[k] for k in keys]
        c.expect = {"L0_xattn": 7, "L2_xattn": 7, "L3_xattn": 6, "L0_ffn": 5, "L1_ffn": 6, "L2_ffn": 5, "L3_ffn": 5,
                    "L1_attn": 4, "L1_xattn": 5, "L2_attn": 4, "L3_attn": 7}
        nothing = lambda sp: None

        def stage_l0_attn():
            l0_attention(c, lambda sp: c.load(sp, "L0_xattn", pick(x0, "Wq", "kcq")))

        def stage_l0_x():
            cross_attention(c, "L0_xattn", X_AT, True, pick(x0, "Wqr", "Wkr", "rope", "kckv", "Wo"),
                            lambda sp: c.load(sp, "L0_ffn", list(fl["L0_ffn"].values())))

        def stage_l0_ffn():
            def ahead(sp):
                c.load(sp, "L1_attn", L1_ATTN_LOADS(c))
                c.load(sp, "L1_xattn", L1_X_LOADS(c)[0:4])
                c.load(sp, "L1_ffn", pick(fl["L1_ffn"], "gate", "up"))
            feed_forward(c, "L0_ffn", spec["L0_ffn"], [], ahead)

        def stage_l1_attn():
            l1_attention(c, [], nothing)

        def stage_l1_x():
            l1_cross(c, L1_X_LOADS(c)[4:], lambda sp: c.load(sp, "L1_ffn", pick(
                fl["L1_ffn"], "down", "router", "spread", "extra")))

        def stage_l1_ffn():
            feed_forward(c, "L1_ffn", spec["L1_ffn"], [], lambda sp: c.load(sp, "L2_attn", L2_ATTN_LOADS(c)))

        def stage_l2_attn():
            l2_attention(c, [], lambda sp: c.load(sp, "L2_xattn", pick(
                x2, "Wqr", "Wkr", "rope", "Wq", "kcq", "kckv", "Wo")))

        def stage_l2_x():
            cross_attention(c, "L2_xattn", X_AT, True, [], lambda sp: c.load(sp, "L2_ffn", pick(
                fl["L2_ffn"], "gate", "up", "down", "router")))

        def stage_l2_ffn():
            feed_forward(c, "L2_ffn", spec["L2_ffn"], pick(fl["L2_ffn"], "spread"),
                         lambda sp: c.load(sp, "L3_attn", L3_ATTN_LOADS(c)))

        def stage_l3_attn():
            l3_attention(c, [], lambda sp: c.load(sp, "L3_xattn", pick(x3, "Wq")))

        def stage_l3_x():
            cross_attention(c, "L3_xattn", X3_AT, False, pick(x3, "Wqr", "Wkr", "kcq", "kckv", "Wo"),
                            lambda sp: c.load(sp, "L3_ffn", pick(fl["L3_ffn"], "gate", "up")))

        def stage_l3_ffn():
            feed_forward(c, "L3_ffn", spec["L3_ffn"], pick(fl["L3_ffn"], "router", "spread", "down"), nothing, out)

        context_stage(c)
        for run in (stage_l0_attn, stage_l0_x, stage_l0_ffn, stage_l1_attn, stage_l1_x, stage_l1_ffn,
                    stage_l2_attn, stage_l2_x, stage_l2_ffn, stage_l3_attn, stage_l3_x, stage_l3_ffn):
            run()



def lay_out(i, np):
    f = lambda n: np.asarray(i[n])
    out = {}

    def tiles(w):
        w = np.asarray(w)
        return np.ascontiguousarray(w.reshape(-1, 128, w.shape[-1]).transpose(1, 0, 2).reshape(128, -1))

    def rows(w, n=128):
        return np.ascontiguousarray(np.broadcast_to(np.asarray(w).reshape(1, -1), (n, np.asarray(w).size)))

    x = f("x")
    xt = np.zeros((2, TP, J, D), np.float32)
    xt[:, :T] = x.reshape(J, 2, T, D).transpose(1, 2, 0, 3)
    out["x_tok"] = xt.reshape(128, J * D)
    xf = np.zeros((128, KT, B, TP), np.float32)
    xf[..., :T] = x.reshape(B, T, KT, 128).transpose(3, 2, 0, 1)
    out["x_feat"] = xf.reshape(128, -1)
    ctx = f("ctx_512")
    out["ctx"] = np.ascontiguousarray(ctx.reshape(J, 2, LP, LT, LC).transpose(2, 0, 3, 1, 4).reshape(LP, -1))
    out["ident"] = np.eye(128, dtype=np.float32)
    pp = np.arange(128)
    out["heads8"] = (pp[:, None] // 8 % 4 == np.arange(4)).astype(np.float32)
    out["heads16"] = (pp[:, None] // 16 % 2 == np.arange(2)).astype(np.float32)

    def rope(length, dim):
        inv = np.float32(1.0) / (np.float32(10000.0) ** (np.arange(0, dim, 2, dtype=np.float32) / np.float32(dim)))
        a = np.arange(length, dtype=np.float32)[:, None] * inv.astype(np.float32)[None, :]
        return np.cos(a).astype(np.float32), np.sin(a).astype(np.float32)

    co, si = (np.repeat(a, 2, axis=1) for a in rope(L, LC))
    sgn = np.where(np.arange(LC) < LC // 2, -1.0, 1.0).astype(np.float32)
    out["ctx_cos"] = np.ascontiguousarray(co.reshape(LP, LT * LC))
    out["ctx_sin"] = np.ascontiguousarray((si * sgn).reshape(LP, LT * LC))
    co, si = (np.repeat(a, 2, axis=1).T for a in rope(T, DQ))
    out["q_rope"] = np.ascontiguousarray(np.concatenate([co[:DH], -si[:DH], co[DH:], si[DH:]], axis=1))
    out["L0a_Wq"], out["L0a_Wk"], out["L0a_Wv"] = tiles(f("L0_attn_Wq")), tiles(f("L0_attn_Wk")), tiles(f("L0_attn_Wv"))
    out["L0a_Wg"], out["L0a_Wc"] = tiles(f("L0_attn_Wg")), tiles(f("L0_attn_Wc"))
    out["L0a_bc"] = rows(f("L0_attn_bc"))
    hh, tt = pp // TP, pp % TP
    real = tt < T
    out["L0a_after"] = ((hh[:, None] == hh) & (tt[:, None] > tt) & real[:, None]).astype(np.float32)
    out["L0a_half"] = np.concatenate([np.repeat(((hh == h) & real)[:, None], 128, 1) for h in range(2)], 1).astype(np.float32)
    out["L0a_tri"] = (tt[:, None] <= np.arange(T)).astype(np.float32)
    out["L0a_causal"] = ((tt[:, None] <= np.arange(T)) & real[:, None]).astype(np.float32)
    add = np.where(np.arange(T)[None, :] > tt[:, None], -3.0e38, 0.0).astype(np.float32)
    out["causal_add"] = out["causal_add2"] = out["causal_add3"] = add
    for l in "023":
        g = lambda n: f(f"L{l}_xattn_{n}")
        t = f"L{l}x_"
        if l == "3":
            out[t + "Wq"] = tiles(g("Wq"))
            out[t + "kcqT"] = np.ascontiguousarray(g("w_kc_q").transpose(2, 0, 1).reshape(2, DH, -1).transpose(1, 0, 2).reshape(DH, -1))
        else:
            out[t + "Wq"] = tiles(g("Wq").T)
            out[t + "kcq"] = np.ascontiguousarray(g("w_kc_q").transpose(1, 0, 2).reshape(128, -1))
        out[t + "kckv"] = np.ascontiguousarray(g("w_kc_kv").transpose(1, 0, 2).reshape(128, -1))
        out[t + "Wqr"] = np.ascontiguousarray(g("W_qr").transpose(2, 0, 1).reshape(64, -1))
        out[t + "Wkr"] = np.ascontiguousarray(g("W_kr").transpose(2, 0, 1).reshape(64, -1))
        out[t + "Wo"] = tiles(g("Wo").T)
    cat = lambda parts: tiles(np.concatenate(parts, axis=1))
    out["L0f_gate"] = cat([f("L0_ffn_shared_w_gate"), f("L0_ffn_w_gate")])
    out["L0f_up"] = cat([f("L0_ffn_shared_w_up"), f("L0_ffn_w_up")])
    out["L0f_down"] = tiles(np.concatenate([f("L0_ffn_shared_w_down"), f("L0_ffn_w_down")], 0))
    out["L0f_router"] = tiles(f("L0_ffn_w_router"))
    out["L0f_mix"] = np.concatenate([f("L0_ffn_amplitudes").reshape(128, 16), f("L0_ffn_expert_scale")[:, None]], 1)
    ecat = lambda w: np.asarray(w).transpose(1, 0, 2).reshape(D, -1)
    out["L1f_gate"] = cat([f("L1_ffn_Su")[0], ecat(f("L1_ffn_Wu"))])
    out["L1f_up"] = cat([f("L1_ffn_Sg")[0], ecat(f("L1_ffn_Wg"))])
    out["L1f_down"] = tiles(np.concatenate([f("L1_ffn_Sd")[0], f("L1_ffn_Wd").reshape(-1, D)], 0))
    out["L1f_router"] = tiles(f("L1_ffn_router_w").T)
    out["L1f_bias"] = rows(f("L1_ffn_router_bias"))

    def spread(e, hidden, width):
        return (np.minimum(np.arange(hidden) // width, e - 1)[None, :] == pp[:, None]).astype(np.float32)

    out["L1f_spread"] = spread(16, 2048, 128)
    out["L2f_gate"] = cat([f("L2_ffn_w_gate").reshape(-1, D).T, f("L2_ffn_sh_gate").T])
    out["L2f_up"] = cat([f("L2_ffn_w_up").reshape(-1, D).T, f("L2_ffn_sh_up").T])
    out["L2f_down"] = tiles(np.concatenate([f("L2_ffn_w_down").transpose(0, 2, 1).reshape(-1, D), f("L2_ffn_sh_down").T], 0))
    out["L2f_router"] = tiles(np.concatenate([f("L2_ffn_gate_w"), f("L2_ffn_se_gate_w")], 0).T)
    out["L2f_spread"] = spread(9, 1280, 128)
    pad = lambda w, n: np.concatenate([w, np.zeros((w.shape[0], n), np.float32)], 1)
    out["L3f_gate"] = cat([pad(f("L3_ffn_sg"), 32), ecat(f("L3_ffn_wg"))])
    out["L3f_up"] = cat([pad(f("L3_ffn_su"), 32), ecat(f("L3_ffn_wu"))])
    out["L3f_down"] = tiles(np.concatenate([f("L3_ffn_sd"), np.zeros((32, D), np.float32),
                                            f("L3_ffn_wd").reshape(-1, D)], 0))
    out["L3f_router"] = tiles(f("L3_ffn_router_w").T)
    out["L3f_spread"] = spread(8, 1408, 176)
    ws = [f(f"L1_attn_{n}_weight") for n in "qkvo"]
    out["L1a_W"] = np.concatenate([tiles(w) for w in ws], 1)
    out["L1a_WT"] = np.concatenate([tiles(w.T) for w in ws], 1)
    out["L1a_bias"] = np.concatenate([f(f"L1_attn_{n}_bias").reshape(2, 128).T for n in "qkv"]
                                     + [np.zeros((128, 2), np.float32)], 1)
    out["L1a_ob"] = rows(f("L1_attn_o_bias"))
    out["L1x_Wq"], out["L1x_Wout"] = tiles(f("L1_xattn_Wq").T), tiles(f("L1_xattn_Wout").T)
    out["L1x_Wkv"] = np.ascontiguousarray(f("L1_xattn_Wkv_expand").T)
    lat = np.zeros((LC, B, TP), np.float32)
    lat[:, :, :T] = ctx[:, :T].transpose(2, 0, 1)
    out["L1x_lat"] = lat.reshape(LC, -1)
    qw, kvw = f("L2_attn_q_w"), f("L2_attn_kv_w")
    rep = lambda w: np.repeat(w.reshape(4, 1, 16, D), 4, axis=1).reshape(256, D)
    kw, vw = rep(kvw[:64]), rep(kvw[64:])
    swap = lambda w: w.reshape(128, 2, D)[:, ::-1].reshape(256, D)
    out["L2a_W"] = np.concatenate([tiles(w.T) for w in (qw, swap(qw), kw, swap(kw), vw)], 1)
    out["L2a_Wo"] = tiles(f("L2_attn_c_w").T)
    co, si = rope(T, 16)
    d = pp % 16
    sg = np.where(d % 2 == 0, -1.0, 1.0).astype(np.float32)[:, None]
    out["L2a_rope"] = np.ascontiguousarray(np.concatenate([co.T[d // 2], si.T[d // 2] * sg], 1))
    out["L3a_wq"], out["L3a_wk"], out["L3a_wv"] = (tiles(f(f"L3_attn_w{n}").T) for n in "qkv")
    out["L3a_wo"] = tiles(f("L3_attn_wo").T)
    bm = np.zeros((128, 2048), np.float32)
    am = np.zeros((128, 3, D), np.float32)
    for n, q in enumerate("qkv"):
        bm[32 * n:32 * n + 16] = f(f"L3_attn_{q}B").T
        am[32 * n:32 * n + 16, n] = f(f"L3_attn_{q}A")
    bm[96:112] = f("L3_attn_oA")
    ob = np.zeros((128, D), np.float32)
    ob[96:112] = f("L3_attn_oB").T
    out["L3a_B"], out["L3a_A"], out["L3a_oB"] = bm, am.reshape(128, -1), ob
    out["L3a_norm"] = np.ascontiguousarray(f("L3_attn_norm_w").reshape(2, 128).T)
    co, si = rope(T, 128)
    sg = np.where(pp < 64, 1.0, -1.0).astype(np.float32)[:, None]
    out["L3a_rope"] = np.ascontiguousarray(np.concatenate([co.T[pp % 64], si.T[pp % 64] * sg], 1))
    return out


def kernel(**inputs):
    import numpy as _np
    import concourse.bacc as _bacc
    from concourse.bass_utils import run_bass_kernel_spmd as _run

    nc = _bacc.Bacc("TRN2", target_bir_lowering=False, num_devices=1)
    arrays, dram = {}, {}
    for name, a in lay_out(inputs, _np).items():
        a = _np.ascontiguousarray(a)
        arrays["in_" + name] = a
        dram[name] = nc.dram_tensor("in_" + name, a.shape, mybir.dt.from_np(a.dtype), kind="ExternalInput").ap()
    out = nc.dram_tensor("out_0", (B, T, D), F32, kind="ExternalOutput").ap()
    decoder_program(nc, dram, out)
    r = _run(nc, [arrays], core_ids=[0])
    return r.results[0]["out_0"]
```

```python
import concourse.bass as bass
from concourse import mybir
from contextlib import ExitStack

F32 = mybir.dt.float32
ALU = mybir.AluOpType
ACT = mybir.ActivationFunctionType
AX = mybir.AxisListType

B, T, D = 8, 56, 256
TP = 64
NT = B * T
J = B // 2
KT = D // 128
L, LC, LT = 1500, 64, 12
LP = L // LT
ARENA = 37800


class Sem:

    def __init__(self, handle):
        self.handle = handle
        self.base = 0
        self.n = 0

    def next(self):
        self.n += 1
        return self.handle, 1

    def at(self, k):
        return self.base + k

    def last(self):
        return self.base + self.n


class Core:

    def __init__(self, nc, ctx, dram):
        self.nc, self.ctx, self.dram = nc, ctx, dram
        sb = lambda name, shape: ctx.enter_context(nc.sbuf_tensor(name, shape, F32))
        self.arena = sb("arena", [128, ARENA])
        self.x_tok = sb("x_tok", [128, J, D])
        self.x_feat = sb("x_feat", [128, KT, B, TP])
        self.ctx_pos = sb("ctx_pos", [LP, J, LT, 2, LC])
        self.ctx_feat = sb("ctx_feat", [128, J, L])
        self.ident = sb("ident", [128, 128])
        self.heads8 = sb("heads8", [128, 4])
        self.heads16 = sb("heads16", [128, 2])
        self.stats = sb("stats", [128, J, 6])
        self.mv = sb("mv", [128, J, 2])
        self.eps = sb("eps", [128, 1])
        self.warm = sb("warm", [128, 1])
        self.std = sb("std", [128, J])
        self.rstd = sb("rstd", [128, J])
        self.ps = ctx.enter_context(nc.psum_tensor("ps", [128, 8, 512], F32))
        self.loaded = {}
        self.shared, self.taken = [], 0

    def at(self, off, n, parts=128):
        assert off + n <= ARENA, (off, n)
        return self.arena[0:parts, off:off + n]

    def sem(self, name):
        return Sem(self.ctx.enter_context(self.nc.semaphore(name)))

    def stage_sem(self):
        if self.taken == len(self.shared):
            self.shared.append(self.sem("stage_%d" % self.taken))
        self.taken += 1
        sem = self.shared[self.taken - 1]
        sem.base, sem.n = sem.base + sem.n, 0
        return sem

    def load(self, eng, group, items):
        if group not in self.loaded:
            self.loaded[group] = self.sem("load_" + group)
        for name, dst in items:
            eng.dma_start(dst, self.dram[name]).then_inc(self.loaded[group].handle, 16)
            self.loaded[group].n += 16


class Stage:

    def __init__(self, c, name):
        self.c, self.name = c, name
        c.taken = 0
        self.dve_chain = c.stage_sem()
        self.act_chain = c.stage_sem()
        self.y_done = c.stage_sem()
        self.var_ready = c.stage_sem()
        self.std_ready = c.stage_sem()
        self.x_normed = c.stage_sem()
        self.x_turned = c.stage_sem()

    def sem(self, what):
        return self.c.stage_sem()



def norm_vector(c, s, dve, last):
    x2 = c.x_tok[:].rearrange("p (a b) d -> p a (b d)", a=2)
    for a in range(2):
        dve.wait_ge(s.y_done.handle, s.y_done.at(a + 1))
        c.nc.vector.tensor_tensor(x2[:, a], c.ps[:, a, :], x2[:, a], ALU.add).then_inc(*s.dve_chain.next())
        dve.wait_ge(s.dve_chain.handle, s.dve_chain.last())
        for j in (2 * a, 2 * a + 1):
            c.nc.vector.bn_stats(c.stats[:, j, :], c.x_tok[:, j, :]).then_inc(*s.dve_chain.next())
    dve.wait_ge(s.dve_chain.handle, s.dve_chain.last())
    for j in range(J):
        c.nc.vector.bn_aggr(c.mv[:, j, :], c.stats[:, j, :]).then_inc(*s.var_ready.next())
    dve.wait_ge(s.std_ready.handle, s.std_ready.at(1))
    c.nc.vector.reciprocal(c.rstd[:], c.std[:]).then_inc(*s.dve_chain.next())
    dve.wait_ge(s.dve_chain.handle, s.dve_chain.last())
    for j in range(J):
        c.nc.vector.tensor_scalar(c.x_tok[:, j, :], c.x_tok[:, j, :], c.mv[:, j, 0:1], c.rstd[:, j:j + 1],
                                       ALU.subtract, ALU.mult).then_inc(*s.x_normed.next())
    if not last:
        dve.wait_ge(s.x_turned.handle, s.x_turned.at(1))
        c.nc.vector.tensor_copy(c.x_feat[:, 1, :, :], c.ps[:, 3, :].rearrange("p (b t) -> p b t", b=B)).then_inc(*s.dve_chain.next())
        dve.wait_ge(s.dve_chain.handle, s.dve_chain.last())


def norm_scalar(c, s, act, last):
    c.nc.scalar.activation(c.warm[:], c.eps[:], ACT.Sqrt).then_inc(*s.act_chain.next())
    act.wait_ge(s.var_ready.handle, s.var_ready.at(J))
    c.nc.scalar.activation(c.std[:], c.mv[:, :, 1], ACT.Sqrt, bias=c.eps[:]).then_inc(*s.std_ready.next())
    act.wait_ge(s.std_ready.handle, s.std_ready.last())
    if not last:
        act.wait_ge(s.x_turned.handle, s.x_turned.at(1))
        c.nc.scalar.copy(c.x_feat[:, 0, :, :], c.ps[:, 2, :].rearrange("p (b t) -> p b t", b=B)).then_inc(*s.act_chain.next())
        act.wait_ge(s.act_chain.handle, s.act_chain.last())


def norm_tensor(c, s, pe, last):
    if last:
        return
    for j in range(J):
        pe.wait_ge(s.x_normed.handle, s.x_normed.at(j + 1))
        for k in range(KT):
            t = c.nc.tensor.transpose(c.ps[:, 2 + k, j * 128:(j + 1) * 128],
                                      c.x_tok[:, j, k * 128:(k + 1) * 128], c.ident[:])
    t.then_inc(*s.x_turned.next())


def norm_store(c, s, sp, out):
    rows = out.rearrange("(j h) t d -> h t j d", h=2)
    sp.wait_ge(s.x_normed.handle, s.x_normed.at(J))
    stored = s.sem("stored")
    for h in range(2):
        sp.dma_start(rows[h], c.x_tok[h * TP:h * TP + T, :, :]).then_inc(stored.handle, 16)
    sp.wait_ge(stored.handle, stored.at(32))


def valid(ap):
    return ap.rearrange("p (b t) -> p b t", b=B)


def project_out(c, pe, j, k, lhsT, rhs, first, last):
    return c.nc.tensor.matmul(c.ps[:, j // 2, (j % 2) * D:(j % 2 + 1) * D], lhsT, rhs,
                              start=first and j % 2 == 0, stop=last, skip_group_check=True)




GH, HD = 8, 128


def L0_LOADS(c):
    flat = lambda a: a.rearrange("p a b n -> p (a b n)")
    return [("L0_start", [("x_feat", flat(c.x_feat[:])), ("L0a_Wk", c.at(4096, 2048)), ("L0a_Wg", c.at(12288, 16)),
                          ("L0a_after", c.at(12304, 128)), ("L0a_tri", c.at(12688, T))]),
            ("L0_queries", [("L0a_Wq", c.at(0, 4096))]),
            ("context", [("ctx", c.ctx_pos[:].rearrange("p j l h d -> p (j l h d)")),
                         ("ctx_cos", c.at(32256, LT * LC, LP)), ("ctx_sin", c.at(32256 + LT * LC, LT * LC, LP))]),
            ("L0_values", [("L0a_Wv", c.at(6144, 2048))]),
            ("L0_rest", [("ident", c.ident[:]), ("L0a_half", c.at(12432, 256)), ("L0a_causal", c.at(12744, T)),
                         ("L0a_bc", c.at(12800, D)), ("x_tok", c.x_tok[:].rearrange("p j d -> p (j d)")),
                         ("L0a_Wc", c.at(8192, 4096)), ("heads8", c.heads8[:]), ("heads16", c.heads16[:])])]


def l0_attention(c, prefetch):
    nc, s = c.nc, Stage(c, "L0_attn")
    wq = c.at(0, 4096).rearrange("p (k n) -> p k n", k=KT)
    wk = c.at(4096, 2048).rearrange("p (k n) -> p k n", k=KT)
    wv = c.at(6144, 2048).rearrange("p (k n) -> p k n", k=KT)
    wc = c.at(8192, 4096).rearrange("p (h n) -> p h n", h=2 * GH)
    wg = c.at(12288, 16).rearrange("p (k n) -> p k n", k=KT)
    later = c.at(12304, 128)
    half = c.at(12432, 256).rearrange("p (h m) -> p h m", h=2)
    tri = c.at(12688, T)
    causal = c.at(12744, T)
    bias = c.at(12800, D)
    kT = c.at(13312, 4096).rearrange("p (g b t) -> p g b t", g=GH, b=B)
    qT = c.at(17408, 7168).rearrange("p (h b t) -> p h b t", h=2 * GH, b=B)
    v = c.at(24576, 4096).rearrange("p (j n) -> p j n", j=J)
    masked = c.at(28672, 1792).rearrange("p (g j t) -> p g j t", g=GH, j=J)
    gate = c.at(30464, 1792)
    square = [c.at(32256 + 448 * i, NT) for i in range(2)]
    a = [c.at(33152 + 448 * i, NT) for i in range(2)]
    yT = [c.at(34048 + 1024 * i, 1024).rearrange("p (r b t) -> p r b t", r=2, b=B) for i in range(2)]
    rnorm = c.at(36096, 896).rearrange("p (h n) -> p h n", h=2)
    ones = c.at(37088, 128, 2 * T)
    rsum = c.at(37216, 8, 2 * T).rearrange("p (j h) -> p j h", j=J)
    diag = [c.at(28672 + 896 * i, 896, 2 * T).rearrange("p (h j n) -> p h j n", h=2, j=J) for i in range(2)]
    lg = c.at(36992, 32).rearrange("p (j g) -> p j g", j=J)
    lg2 = c.at(37024, 32).rearrange("p (j g) -> p j g", j=J)
    lg3 = c.at(37056, 32).rearrange("p (j g) -> p j g", j=J)
    cos, sin = c.at(32256, LT * LC, LP), c.at(32256 + LT * LC, LT * LC, LP)
    flipped = c.at(32256 + 2 * LT * LC, LT * 2 * LC, LP).rearrange("p (l h d) -> p l h d", l=LT, h=2)
    rotated = s.sem("rotated")
    projected = s.sem("projected")
    out_act = s.sem("copied_act")
    out_dve = s.sem("copied_dve")
    padded = s.sem("padded")
    gates_in, lg_exp, lg_in, lg_ln, masked_in = (s.sem(x) for x in ("gates", "lg_exp", "lg_in", "lg_ln", "masked"))
    diffs, gate_exp, gate_in = s.sem("diffs"), s.sem("gate_exp"), s.sem("gate_in")
    scored, squared, a_in, summed, rs_in, diag_in, spread_mm, rn_in, weighed, y_in, projected_y = (
        s.sem(x) for x in ("scored", "squared", "a_in", "summed", "rs_in", "diag_in", "spread_mm", "rn_in",
                           "weighed", "y_in", "projected_y"))
    banks = [("k", g) for g in range(GH)] + [("q", h) for h in range(2 * GH)] + [("v", i) for i in range(2 * J)]
    banks += [("context", i) for i in range(J * LT // 4)]
    NB = len(banks)
    GATES_AT = (7, 15)
    ROTATE_AT = (16, 20, 24, 28)

    def copied(eng, n):
        if n >= 0:
            done = out_act if n % 2 else out_dve
            eng.wait_ge(done.handle, done.at(n // 2 + 1))

    def copy_out(n):
        kind, i = banks[n]
        bank = c.ps[:, 2 + n % 6, :]
        if kind == "k":
            return kT[:, i, :, 0:T], valid(bank[:, 0:NT])
        if kind == "q":
            return qT[:, i, :, :], valid(bank[:, 0:NT])
        if kind == "context":
            j, g = i // (LT // 4), i % (LT // 4)
            return c.ctx_feat[:, j, g * 4 * LP:(g + 1) * 4 * LP], bank[:, 0:4 * LP]
        return v[:, i // 2, (i % 2) * 512:(i % 2 + 1) * 512], bank

    with nc.Block(no_gpsimd_drain=True) as block:
        @block.sync
        def _(sp):
            for group, items in L0_LOADS(c):
                c.load(sp, group, items)
            sp.wait_ge(projected.handle, projected.at(NB))
            prefetch(sp)

        @block.gpsimd
        def _(pool):
            nc.gpsimd.memset(kT[:, :, :, T:TP], 0.0).then_inc(*padded.next())
            pool.wait_ge(rotated.handle, rotated.at(J))
            for i in range(2):
                nc.gpsimd.memset(yT[i][:, :, :, T:TP], 0.0).then_inc(*padded.next())
            nc.gpsimd.memset(ones, 1.0).then_inc(*padded.next())
            pool.wait_ge(padded.handle, padded.at(4))
            pool.wait_ge(diffs.handle, diffs.at(2))
            pool.wait_ge(c.loaded["L0_rest"].handle, c.loaded["L0_rest"].n)
            for g in range(GH):
                pool.wait_ge(rs_in.handle, rs_in.at(g + 1))
                if g >= 2:
                    pool.wait_ge(spread_mm.handle, spread_mm.at(g - 1))
                for h in range(2):
                    nc.gpsimd.tensor_tensor(diag[g % 2][:, h], c.ident[0:2 * T, 0:2 * T].unsqueeze(1).broadcast_to([2 * T, J, 2 * T]),
                                            rsum[:, :, h].unsqueeze(2).broadcast_to([2 * T, J, 2 * T]), ALU.mult).then_inc(*diag_in.next())

        @block.tensor
        def _(pe):
            pe.wait_ge(c.loaded["L0_start"].handle, c.loaded["L0_start"].n)
            for j in range(J):
                for k in range(KT):
                    m = nc.tensor.matmul(c.ps[:, 0, j * GH:(j + 1) * GH], c.x_feat[:, k, 2 * j:2 * j + 2, :],
                                         wg[:, k, :], start=(k == 0), stop=(k == KT - 1))
            m.then_inc(*gates_in.next())
            for n, (kind, i) in enumerate(banks):
                copied(pe, n - 6)
                if i == 0 and kind != "k":
                    needs = {"q": "L0_queries", "v": "L0_values", "context": "L0_rest"}[kind]
                    pe.wait_ge(c.loaded[needs].handle, c.loaded[needs].n)
                if kind == "context":
                    pe.wait_ge(rotated.handle, rotated.at(i // (LT // 4) + 1))
                    for l in range(4):
                        m = nc.tensor.transpose(c.ps[:, 2 + n % 6, l * LP:(l + 1) * LP],
                                                c.ctx_pos[:, i // (LT // 4), i % (LT // 4) * 4 + l, :, :], c.ident[0:LP, 0:LP])
                    m.then_inc(*projected.next())
                    continue
                for k in range(KT):
                    if kind == "v":
                        m = nc.tensor.matmul(c.ps[:, 2 + n % 6, :], c.x_feat[:, k, i // 2 * 2:i // 2 * 2 + 2, :],
                                             wv[:, k, (i % 2) * 512:(i % 2 + 1) * 512],
                                             start=(k == 0), stop=(k == KT - 1))
                    else:
                        w = wk if kind == "k" else wq
                        m = nc.tensor.matmul(c.ps[:, 2 + n % 6, 0:NT], w[:, k, i * HD:(i + 1) * HD],
                                             c.x_feat[:, k, :, 0:T], start=(k == 0), stop=(k == KT - 1))
                m.then_inc(*projected.next())
                if n in GATES_AT:
                    i = GATES_AT.index(n)
                    pe.wait_ge(masked_in.handle, masked_in.at(1))
                    if i > 0:
                        pe.wait_ge(gate_exp.handle, gate_exp.at(2))
                    for g in range(4 * i, 4 * i + 4):
                        m = nc.tensor.matmul(c.ps[:, g // 2 % 2, (g % 2) * 224:(g % 2 + 1) * 224], later, masked[:, g, :, :],
                                             start=True, stop=True)
                    m.then_inc(*diffs.next())
            copied(pe, NB - 2)
            copied(pe, NB - 1)
            pe.wait_ge(padded.handle, padded.at(4))
            pe.wait_ge(gate_exp.handle, gate_exp.at(4))

            def scores(g):
                if g >= 2:
                    pe.wait_ge(rs_in.handle, rs_in.at(g - 1))
                for b in range(B):
                    m = nc.tensor.matmul(c.ps[(b % 2) * TP:(b % 2 + 1) * TP, 6 + g % 2,
                                              (b // 2) * 2 * T:(b // 2 + 1) * 2 * T],
                                         kT[:, g, b, :], qT[:, 2 * g:2 * g + 2, b, :], start=True, stop=True)
                m.then_inc(*scored.next())

            def sums(g):
                pe.wait_ge(a_in.handle, a_in.at(g + 1))
                for j in range(J):
                    m = nc.tensor.matmul(c.ps[0:2 * T, 6 + g % 2, NT + 2 * j:NT + 2 * j + 2],
                                         a[g % 2][:, j * 2 * T:(j + 1) * 2 * T], half[:, :, 0], start=True, stop=True)
                m.then_inc(*summed.next())

            def spread(g):
                for h in range(2):
                    pe.wait_ge(diag_in.handle, diag_in.at(2 * g + h + 1))
                    if g > 0:
                        pe.wait_ge(rn_in.handle, rn_in.at(2 * g - 1 + h))
                    m = nc.tensor.matmul(c.ps[:, 4 + h, 0:NT], ones, diag[g % 2][:, h], start=True, stop=True)
                m.then_inc(*spread_mm.next())

            def weigh(g):
                if g > 0:
                    pe.wait_ge(y_in.handle, y_in.at(2 * g))
                for b in range(B):
                    h, j = b % 2, b // 2
                    m = nc.tensor.matmul(c.ps[:, 2 + h, j * 2 * T:(j + 1) * 2 * T],
                                         v[h * TP:h * TP + T, j, g * HD:(g + 1) * HD],
                                         a[g % 2][h * TP:h * TP + T, j * 2 * T:(j + 1) * 2 * T], start=True, stop=True)
                m.then_inc(*weighed.next())

            def out(g):
                pe.wait_ge(y_in.handle, y_in.at(2 * (g + 1)))
                for r in range(2):
                    for j in range(J):
                        m = project_out(c, pe, j, r, yT[g % 2][:, r, 2 * j:2 * j + 2, :], wc[:, 2 * g + r, :],
                                        g == 0 and r == 0, g == GH - 1 and r == 1)
                        if g == GH - 1 and r == 1 and j % 2 == 1:
                            m.then_inc(*s.y_done.next())
                if g < GH - 1:
                    m.then_inc(*projected_y.next())

            scores(0)
            for g in range(GH + 2):
                if g < GH:
                    sums(g)
                if 1 <= g <= GH:
                    weigh(g - 1)
                if g + 1 < GH:
                    scores(g + 1)
                if g >= 2:
                    out(g - 2)
                if g < GH:
                    spread(g)
            norm_tensor(c, s, pe, False)

        @block.scalar
        def _(act):
            act.wait_ge(lg_in.handle, lg_in.at(1))
            nc.scalar.activation(lg2, lg2, ACT.Exp, scale=-1.0).then_inc(*lg_exp.next())
            act.wait_ge(lg_exp.handle, lg_exp.last())
            act.wait_ge(lg_in.handle, lg_in.at(2))
            nc.scalar.activation(lg2, lg2, ACT.Ln).then_inc(*lg_ln.next())
            act.wait_ge(lg_ln.handle, lg_ln.last())
            for n in range(1, NB, 2):
                act.wait_ge(projected.handle, projected.at(n + 1))
                nc.scalar.copy(*copy_out(n)).then_inc(*out_act.next())
                if n in GATES_AT:
                    i = GATES_AT.index(n)
                    act.wait_ge(diffs.handle, diffs.at(i + 1))
                    for e in range(2):
                        nc.scalar.activation(gate[:, (2 * i + e) * 448:(2 * i + e + 1) * 448], c.ps[:, e, 0:448],
                                             ACT.Exp).then_inc(*gate_exp.next())
            def squares(g):
                act.wait_ge(scored.handle, scored.at(g + 1))
                if g >= 2:
                    act.wait_ge(a_in.handle, a_in.at(g - 1))
                nc.scalar.activation(square[g % 2], c.ps[:, 6 + g % 2, 0:NT], ACT.Square, scale=HD ** -0.5).then_inc(*squared.next())

            squares(0)
            for g in range(GH):
                if g + 1 < GH:
                    squares(g + 1)
                act.wait_ge(spread_mm.handle, spread_mm.at(g + 1))
                for h in range(2):
                    if g > 0:
                        act.wait_ge(y_in.handle, y_in.at(2 * g - 1 + h))
                    nc.scalar.copy(rnorm[:, h], c.ps[:, 4 + h, 0:NT]).then_inc(*rn_in.next())
            norm_scalar(c, s, act, False)

        @block.vector
        def _(dve):
            nc.vector.memset(c.eps[:], 1e-5).then_inc(*s.dve_chain.next())
            dve.wait_ge(gates_in.handle, gates_in.at(1))
            nc.vector.tensor_scalar(lg, c.ps[:, 0, 0:J * GH].rearrange("p (j g) -> p j g", j=J), 6.906768, None,
                                         ALU.add).then_inc(*s.dve_chain.next())
            dve.wait_ge(s.dve_chain.handle, s.dve_chain.last())
            nc.vector.tensor_scalar(lg3, lg, 0.0, None, ALU.min).then_inc(*s.dve_chain.next())
            dve.wait_ge(s.dve_chain.handle, s.dve_chain.last())
            nc.vector.scalar_tensor_tensor(out=lg2, in0=lg3, scalar=-2.0, in1=lg, op0=ALU.mult, op1=ALU.add).then_inc(*lg_in.next())
            dve.wait_ge(lg_in.handle, lg_in.last())
            dve.wait_ge(lg_exp.handle, lg_exp.at(1))
            nc.vector.tensor_scalar(lg2, lg2, 1.0, None, ALU.add).then_inc(*lg_in.next())
            dve.wait_ge(lg_in.handle, lg_in.last())
            dve.wait_ge(lg_ln.handle, lg_ln.at(1))
            nc.vector.tensor_tensor(lg, lg3, lg2, ALU.subtract).then_inc(*s.dve_chain.next())
            dve.wait_ge(s.dve_chain.handle, s.dve_chain.last())
            nc.vector.tensor_tensor(masked, lg.rearrange("p j g -> p g j").unsqueeze(3).broadcast_to([128, GH, J, T]),
                                         tri.rearrange("p (a b t) -> p a b t", a=1, b=1).broadcast_to([128, GH, J, T]),
                                         ALU.mult).then_inc(*masked_in.next())
            dve.wait_ge(masked_in.handle, masked_in.last())
            for n in range(0, NB, 2):
                dve.wait_ge(projected.handle, projected.at(n + 1))
                nc.vector.tensor_copy(*copy_out(n)).then_inc(*out_dve.next())
                if n in ROTATE_AT:
                    j = ROTATE_AT.index(n)
                    dve.wait_ge(c.loaded["context"].handle, c.loaded["context"].n)
                    if j > 0:
                        dve.wait_ge(rotated.handle, rotated.at(j))
                    x = c.ctx_pos[:, j]
                    co = cos.rearrange("p (l o d) -> p l o d", l=LT, o=1).broadcast_to([LP, LT, 2, LC])
                    sn = sin.rearrange("p (l o d) -> p l o d", l=LT, o=1).broadcast_to([LP, LT, 2, LC])
                    for lo, hi in ((0, LC // 2), (LC // 2, 0)):
                        nc.vector.tensor_tensor(flipped[:, :, :, lo:lo + LC // 2], x[:, :, :, hi:hi + LC // 2],
                                                sn[:, :, :, lo:lo + LC // 2], ALU.mult).then_inc(*s.dve_chain.next())
                    dve.wait_ge(s.dve_chain.handle, s.dve_chain.last())
                    nc.vector.tensor_tensor(x, x, co, ALU.mult).then_inc(*s.dve_chain.next())
                    dve.wait_ge(s.dve_chain.handle, s.dve_chain.last())
                    nc.vector.tensor_tensor(x, x, flipped, ALU.add).then_inc(*rotated.next())
            dve.wait_ge(c.loaded["L0_rest"].handle, c.loaded["L0_rest"].n)
            nc.vector.tensor_tensor(c.x_tok[:], c.x_tok[:], bias.unsqueeze(1).broadcast_to([128, J, D]), ALU.add).then_inc(*s.dve_chain.next())
            dve.wait_ge(s.dve_chain.handle, s.dve_chain.last())
            dve.wait_ge(gate_exp.handle, gate_exp.at(4))
            g3 = gate.rearrange("p (a t) -> p a t", t=T)
            nc.vector.tensor_tensor(g3, g3, causal.unsqueeze(1).broadcast_to([128, GH * J, T]), ALU.mult).then_inc(*s.dve_chain.next())
            dve.wait_ge(s.dve_chain.handle, s.dve_chain.last())
            g4 = gate.rearrange("p (g j o t) -> p g j o t", g=GH, j=J, o=1)

            def weights(g):
                dve.wait_ge(squared.handle, squared.at(g + 1))
                if g >= 2:
                    dve.wait_ge(weighed.handle, weighed.at(g - 1))
                nc.vector.tensor_tensor(a[g % 2].rearrange("p (j r t) -> p j r t", j=J, r=2),
                                             square[g % 2].rearrange("p (j r t) -> p j r t", j=J, r=2),
                                             g4[:, g].broadcast_to([128, J, 2, T]), ALU.mult).then_inc(*a_in.next())

            def invert(g):
                dve.wait_ge(summed.handle, summed.at(g + 1))
                if g > 0:
                    dve.wait_ge(diag_in.handle, diag_in.at(2 * g))
                r = rsum.rearrange("p j h -> p (j h)")
                nc.vector.tensor_scalar(r, c.ps[0:2 * T, 6 + g % 2, NT:NT + 8], 1e-6, None, ALU.add).then_inc(*s.dve_chain.next())
                dve.wait_ge(s.dve_chain.handle, s.dve_chain.last())
                nc.vector.reciprocal(r, r).then_inc(*rs_in.next())

            def divide(g):
                dve.wait_ge(weighed.handle, weighed.at(g + 1))
                if g >= 2:
                    dve.wait_ge(projected_y.handle, projected_y.at(g - 1))
                for h in range(2):
                    dve.wait_ge(rn_in.handle, rn_in.at(2 * g + h + 1))
                    nc.vector.tensor_tensor(
                        yT[g % 2].rearrange("p r (j h) t -> p h j r t", h=2)[:, h, :, :, 0:T],
                        c.ps[:, 2 + h, 0:NT].rearrange("p (j r t) -> p j r t", j=J, r=2),
                        rnorm[:, h].rearrange("p (j r t) -> p j r t", j=J, r=2), ALU.mult).then_inc(*y_in.next())

            dve.wait_ge(padded.handle, padded.at(4))
            weights(0)
            for g in range(GH + 1):
                if g < GH:
                    invert(g)
                if g >= 1:
                    divide(g - 1)
                if g + 1 < GH:
                    weights(g + 1)
            norm_vector(c, s, dve, False)



NH, DQ, DH = 16, 192, 96
UNITS = NH * T // 128


def X_WEIGHTS(c, o, tag):
    if "rope" in o:
        q = {"kcq": (tag + "_kcq", c.at(o["kcq"], 3072)), "rope": ("q_rope", c.at(o["rope"], 4 * T, DH))}
    else:
        q = {"kcq": (tag + "_kcqT", c.at(o["kcq"], 4096, DH))}
    return {**q, "Wq": (tag + "_Wq", c.at(o["Wq"], 4096)),
            "Wqr": (tag + "_Wqr", c.at(o["Wqr"], 3072, 64)), "Wkr": (tag + "_Wkr", c.at(o["Wkr"], 1024, 64)),
            "kckv": (tag + "_kckv", c.at(o["kckv"], 1024)), "Wo": (tag + "_Wo", c.at(o["Wo"], 4096))}


X_AT = {"Wqr": 0, "Wkr": 3072, "Wq": 4096, "kcq": 8192, "kckv": 11264, "Wo": 12288, "QZ": 16384, "C": 23552,
        "Z": 25600, "buf": 27648, "rope": 36000, "CT": 25600, "PT": 0, "P": 10752}
X3_AT = {"Wq": 4096, "kcq": 8192, "Wqr": 24100, "Wkr": 36424, "kckv": 0, "Wo": 12288, "QZ": 16384, "C": 27648,
         "Z": 1024, "buf": 29696, "CT": 23552, "PT": 0, "P": 10752}


def cross_attention(c, name, o, rope, now, prefetch):
    nc, s = c.nc, Stage(c, name)
    if rope:
        wq = c.at(o["Wq"], 4096).rearrange("p (k h m) -> p k h m", k=KT, h=NH)
        kcq = c.at(o["kcq"], 3072).rearrange("p (h q) -> p h q", h=NH)
        tab = c.at(o["rope"], 4 * T, DH).rearrange("p (i t) -> p i t", i=4)
    else:
        wqT = c.at(o["Wq"], 4096).rearrange("p (h n) -> p h n", h=NH)
        kcqT = c.at(o["kcq"], 4096, DH).rearrange("p (e h m) -> p e h m", e=2, h=NH)
    wqr = c.at(o["Wqr"], 3072, 64).rearrange("p (h q) -> p h q", h=NH)
    wkr = c.at(o["Wkr"], 1024, 64).rearrange("p (h d) -> p h d", h=NH)
    kckv = c.at(o["kckv"], 1024).rearrange("p (h d) -> p h d", h=NH)
    wo = c.at(o["Wo"], 4096).rearrange("p (h n) -> p h n", h=NH)
    qz = c.at(o["QZ"], 7168).rearrange("p (b h t) -> p b h t", b=B, h=NH)
    cm = c.at(o["C"], 2048).rearrange("p (h n) -> p h n", h=8)
    z = c.at(o["Z"], 2048, DH).rearrange("p (h e d) -> p h e d", h=NH, e=2)
    buf = o["buf"]
    qhk = [c.at(buf + i * NT, NT) for i in range(2)]
    prod = [[c.at(buf + (2 + 4 * n + i) * NT, NT, DH) for i in range(4)] for n in range(2)]
    rot = [[c.at(buf + (10 + 2 * n + i) * NT, NT, DH) for i in range(2)] for n in range(4)]
    kz = [c.at(buf + 256 * i, 256).rearrange("p (h d) -> p h d", h=4) for i in range(2)]
    fold = [c.at(buf + 512 + 512 * i, 512).rearrange("p (k h d) -> p k h d", k=KT, h=4) for i in range(2)]
    ctxT = c.at(o["CT"], 4096).rearrange("p (h b t) -> p h b t", h=8, b=B)
    pT = c.at(o["PT"], LT * NH * T, LP).rearrange("p (l q) -> p l q", l=LT)
    probs = [c.at(o["P"] + i * L, L) for i in range(3)]
    stat = c.sb_small
    wide_mm, wide_in = s.sem("wide_mm"), s.sem("wide_in")
    kz_mm, kz_in, fold_mm, fold_in = s.sem("kz_mm"), s.sem("kz_in"), s.sem("fold_mm"), s.sem("fold_in")
    zeroed, hk_mm, hk_in, big_mm, prod_in, rot_in, lat_mm, lat_in = (
        s.sem(x) for x in ("zeroed", "hk_mm", "hk_in", "big_mm", "prod_in", "rot_in", "lat_mm", "lat_in"))
    scored, maxed, exped, recip, normed, turned, t_in, pv_mm, ct_in = (
        s.sem(x) for x in ("scored", "maxed", "exped", "recip", "normed", "turned", "t_in", "pv_mm", "ct_in"))
    padded = s.sem("padded")
    NU = B * UNITS
    steps = ([("Z", 0), ("Z", 1), ("C", 0), ("Z", 2), ("C", 1), ("Z", 3), ("C", 2), ("C", 3)] if rope else
             [("Z", 0), ("Z", 1), ("Z", 2), ("Z", 3), ("C", 0), ("C", 1), ("C", 2), ("C", 3)])

    def z_step(h):
        return steps.index(("Z", h // 4)) + 1

    TURNS = 3 * UNITS + 1

    def slot(i):
        return 3 * (i % 2)

    def turn_bank(i, k):
        return 6 + (i // UNITS * TURNS + 3 * (i % UNITS) + k) % 2

    with nc.Block(no_gpsimd_drain=True) as block:
        @block.sync
        def _(sp):
            for group, items in now:
                c.load(sp, group, items)
            sp.wait_ge(wide_in.handle, wide_in.at(8))
            sp.wait_ge(lat_in.handle, lat_in.at(4 * NH // 2))
            prefetch(sp)

        @block.gpsimd
        def _(pool):
            nc.gpsimd.memset(qz[64:128, 0::2, :, :], 0.0).then_inc(*zeroed.next())
            nc.gpsimd.memset(qz[0:64, 1::2, :, :], 0.0).then_inc(*zeroed.next())
            pool.wait_ge(zeroed.handle, zeroed.at(2))
            if rope:
                for h in range(NH):
                    if h >= 4:
                        pool.wait_ge(lat_mm.handle, lat_mm.at((h - 2) // 2))
                    for e in range(2):
                        pool.wait_ge(prod_in.handle, prod_in.at(4 * h + 3 + e))
                        nc.gpsimd.tensor_tensor(rot[h % 4][e], prod[h % 2][2 * e], prod[h % 2][2 * e + 1],
                                                ALU.add).then_inc(*rot_in.next())
            pool.wait_ge(lat_in.handle, lat_in.at(4 * NH // 2))
            nc.gpsimd.memset(ctxT[:, :, :, T:TP], 0.0).then_inc(*padded.next())
            pool.wait_ge(padded.handle, padded.at(1))

        @block.tensor
        def _(pe):
            def arrived(group):
                pe.wait_ge(c.loaded[name + group].handle, 16 * c.expect[name + group])

            arrived("_first")
            def wide(n):
                kind, g = steps[n]
                if n >= 2:
                    pe.wait_ge(wide_in.handle, wide_in.at(n - 1))
                if kind == "Z":
                    for h in range(4 * g, 4 * g + 4):
                        for e in range(2):
                            m = nc.tensor.matmul(c.ps[0:DH, n % 2, ((h % 4) * 2 + e) * 64:((h % 4) * 2 + e + 1) * 64],
                                                 wqr[:, h, e * DH:(e + 1) * DH], wkr[:, h, :], start=True, stop=True)
                else:
                    for i in range(2):
                        for e in range(2):
                            h = 2 * g + i + 8 * e
                            m = nc.tensor.matmul(c.ps[e * 64:(e + 1) * 64, n % 2, i * D:(i + 1) * D], kckv[:, h, :],
                                                 wo[:, h, :], start=True, stop=True)
                m.then_inc(*wide_mm.next())

            def first(h):
                if h >= 2:
                    pe.wait_ge(hk_in.handle, hk_in.at(h - 1))
                for k in range(KT):
                    m = nc.tensor.matmul(c.ps[:, 2 + h % 2, 0:NT], wq[:, k, h, :], c.x_feat[:, k, :, 0:T],
                                         start=(k == 0), stop=(k == KT - 1))
                m.then_inc(*hk_mm.next())

            def second(h):
                pe.wait_ge(hk_in.handle, hk_in.at(h + 1))
                for e in range(2):
                    if h > 0:
                        pe.wait_ge(prod_in.handle, prod_in.at(4 * (h - 1) + 2 * (e + 1)))
                    m = nc.tensor.matmul(c.ps[0:DH, 4 + e, 0:NT], kcq[:, h, e * DH:(e + 1) * DH], qhk[h % 2],
                                         start=True, stop=True)
                    m.then_inc(*big_mm.next())

            def third(p):
                pe.wait_ge(rot_in.handle, rot_in.at(4 * p + 4))
                pe.wait_ge(wide_in.handle, wide_in.at(z_step(2 * p)))
                if p >= 2:
                    pe.wait_ge(lat_in.handle, lat_in.at(4 * (p - 1)))
                for e in range(2):
                    for r in range(2):
                        h = 2 * p + r
                        m = nc.tensor.matmul(c.ps[r * 64:(r + 1) * 64, 6 + p % 2, 0:NT], z[:, h, e, :], rot[h % 4][e],
                                             start=(e == 0), stop=(e == 1), skip_group_check=True)
                m.then_inc(*lat_mm.next())

            def fold_kz(g):
                pe.wait_ge(wide_in.handle, wide_in.at(z_step(4 * g)))
                if g >= 2:
                    pe.wait_ge(kz_in.handle, kz_in.at(g - 1))
                for h in range(4 * g, 4 * g + 4):
                    for e in range(2):
                        m = nc.tensor.matmul(c.ps[:, 2 + g % 2, (h % 4) * 64:(h % 4 + 1) * 64], kcqT[:, e, h, :],
                                             z[:, h, e, :], start=(e == 0), stop=(e == 1))
                m.then_inc(*kz_mm.next())

            def fold_wq(g):
                pe.wait_ge(kz_in.handle, kz_in.at(g + 1))
                if g >= 2:
                    pe.wait_ge(fold_in.handle, fold_in.at(g - 1))
                for k in range(KT):
                    for h in range(4 * g, 4 * g + 4):
                        at = k * 256 + (h % 4) * 64
                        m = nc.tensor.matmul(c.ps[:, 4 + g % 2, at:at + 64], wqT[:, h, k * 128:(k + 1) * 128],
                                             kz[g % 2][:, h % 4, :], start=True, stop=True)
                m.then_inc(*fold_mm.next())

            def folded(p):
                pe.wait_ge(fold_in.handle, fold_in.at(p // 2 + 1))
                if p >= 2:
                    pe.wait_ge(lat_in.handle, lat_in.at(4 * (p - 1)))
                for k in range(KT):
                    m = nc.tensor.matmul(c.ps[:, 6 + p % 2, 0:NT], fold[p // 2 % 2][:, k, 2 * (p % 2):2 * (p % 2) + 2, :],
                                         c.x_feat[:, k, :, 0:T], start=(k == 0), stop=(k == KT - 1))
                m.then_inc(*lat_mm.next())

            def scores(i, k):
                if k == 0 and i >= 2:
                    pe.wait_ge(exped.handle, exped.at(i - 1))
                q = qz[:, i // UNITS, :, :].rearrange("p h t -> p (h t)")[:, i % UNITS * 128:(i % UNITS + 1) * 128]
                m = nc.tensor.matmul(c.ps[:, slot(i) + k, 0:4 * LP], q,
                                     c.ctx_feat[:, i // UNITS // 2, k * 4 * LP:(k + 1) * 4 * LP], start=True, stop=True)
                if k == 2:
                    m.then_inc(*scored.next())

            if rope:
                wide(0)
                for h in range(NH + 2):
                    if h < NH:
                        first(h)
                    if h % 2 == 1 and h < 15:
                        if h == 3:
                            arrived("_last")
                        wide(h // 2 + 1)
                    if h == 1:
                        arrived("_next")
                    if 1 <= h <= NH:
                        second(h - 1)
                    if h == NH:
                        pe.wait_ge(wide_in.handle, wide_in.at(8))
                        pe.wait_ge(zeroed.handle, zeroed.at(2))
                        pe.wait_ge(lat_in.handle, lat_in.at(4 * 2))
                        for k in range(3):
                            scores(0, k)
                    if h % 2 == 1 and h >= 3:
                        third(h // 2 - 1)
            else:
                for t in range(8):
                    if t == 4:
                        arrived("_last")
                    wide(t)
                    if 1 <= t <= 4:
                        fold_kz(t - 1)
                    if t == 2:
                        arrived("_next")
                    if 2 <= t <= 5:
                        fold_wq(t - 2)
                    if 3 <= t <= 6:
                        folded(2 * (t - 3))
                        folded(2 * (t - 3) + 1)
            pe.wait_ge(wide_in.handle, wide_in.at(8))
            pe.wait_ge(lat_in.handle, lat_in.at(4 * NH // 2))
            pe.wait_ge(zeroed.handle, zeroed.at(2))

            def turn(i, k):
                if k == 0:
                    pe.wait_ge(normed.handle, normed.at(i + 1))
                if i % UNITS == 0 and k == 1 and i > 0:
                    pe.wait_ge(ct_in.handle, ct_in.at(i // UNITS))
                elif i % UNITS == 0 and k == 0 and i > 0:
                    pe.wait_ge(t_in.handle, t_in.at(3 * i))
                elif 3 * i + k - 1 > 0:
                    pe.wait_ge(t_in.handle, t_in.at(3 * i + k - 1))
                for l in range(4):
                    m = nc.tensor.transpose(
                        c.ps[0:LP, turn_bank(i, k), l * 128:(l + 1) * 128],
                        probs[i % 3].rearrange("p (k l) -> p k l", l=LP)[:, 4 * k + l, :], c.ident[:])
                m.then_inc(*turned.next())

            def weigh(b):
                pe.wait_ge(t_in.handle, t_in.at(3 * UNITS * (b + 1)))
                for l in range(LT):
                    for e in range(2):
                        m = nc.tensor.matmul(c.ps[e * 64:(e + 1) * 64, turn_bank(b * UNITS + UNITS - 1, 3), 0:NT],
                                             c.ctx_pos[:, b // 2, l, b % 2, :], pT[:, l, e * NT:(e + 1) * NT],
                                             start=(l == 0), stop=(l == LT - 1), skip_group_check=True)
                m.then_inc(*pv_mm.next())

            def project(j):
                pe.wait_ge(exped.handle, exped.at(NU - 1))
                pe.wait_ge(ct_in.handle, ct_in.at(2 * j + 2))
                pe.wait_ge(padded.handle, padded.at(1))
                for h in range(8):
                    m = project_out(c, pe, j, h, ctxT[:, h, 2 * j:2 * j + 2, :], cm[:, h, :], h == 0, h == 7)
                if j % 2 == 1:
                    m.then_inc(*s.y_done.next())

            for i in range(NU + 2):
                ended = i > 2 and (i - 2) % UNITS == 0
                for k in range(3):
                    if i < NU and not (rope and i == 0):
                        scores(i, k)
                    if i >= 2 and not ended:
                        turn(i - 2, k)
                    if i >= NU and k == 0:
                        project(i - NU)
                if ended:
                    weigh((i - 2) // UNITS - 1)
                    for k in range(3):
                        turn(i - 2, k)
            project(2)
            weigh(B - 1)
            project(3)
            norm_tensor(c, s, pe, False)

        @block.scalar
        def _(act):
            def place(p):
                act.wait_ge(lat_mm.handle, lat_mm.at(p + 1))
                if p == 0:
                    act.wait_ge(zeroed.handle, zeroed.at(2))
                for r in range(2):
                    for e in range(2):
                        nc.scalar.copy(qz[e * 64:(e + 1) * 64, e::2, 2 * p + r, :],
                                       valid(c.ps[r * 64:(r + 1) * 64, 6 + p % 2, 0:NT])[:, e::2, :]).then_inc(*lat_in.next())

            if rope:
                for h in range(NH + 2):
                    if h < NH:
                        act.wait_ge(hk_mm.handle, hk_mm.at(h + 1))
                        if h >= 2:
                            act.wait_ge(big_mm.handle, big_mm.at(2 * (h - 1)))
                        nc.scalar.copy(qhk[h % 2], c.ps[:, 2 + h % 2, 0:NT]).then_inc(*hk_in.next())
                    if h % 2 == 1 and h >= 3:
                        place(h // 2 - 1)
            else:
                for t in range(6):
                    if t < 4:
                        act.wait_ge(kz_mm.handle, kz_mm.at(t + 1))
                        if t >= 2:
                            act.wait_ge(fold_mm.handle, fold_mm.at(t - 1))
                        nc.scalar.copy(kz[t % 2].rearrange("p h d -> p (h d)"), c.ps[:, 2 + t % 2, 0:256]).then_inc(*kz_in.next())
                    if t >= 2:
                        place(2 * (t - 2))
                        place(2 * (t - 2) + 1)
            for i in range(NU):
                act.wait_ge(maxed.handle, maxed.at(i + 1))
                if 3 * (i - 2) > 0:
                    act.wait_ge(turned.handle, turned.at(3 * (i - 2)))
                p = probs[i % 3]
                if i == 0:
                    act.wait_ge(wide_in.handle, wide_in.at(8))
                nc.scalar.activation(p.rearrange("p (k l) -> p k l", k=3), c.ps[:, slot(i):slot(i) + 3, 0:4 * LP],
                                          ACT.Exp, bias=stat[:, i % 4:i % 4 + 1],
                                          accum_out=stat[:, 4 + i % 4:5 + i % 4]).then_inc(*exped.next())
                act.wait_ge(exped.handle, exped.last())
                act.wait_ge(recip.handle, recip.at(i + 1))
                nc.scalar.activation(p, p, ACT.Copy, scale=stat[:, 8 + i % 4:9 + i % 4]).then_inc(*normed.next())
                act.wait_ge(normed.handle, normed.last())
            norm_scalar(c, s, act, False)

        @block.vector
        def _(dve):
            def wide_out(n):
                dve.wait_ge(wide_mm.handle, wide_mm.at(n + 1))
                kind, g = steps[n]
                if kind == "Z":
                    nc.vector.tensor_copy(z[:, 4 * g:4 * g + 4, :, :].rearrange("p h e d -> p (h e d)"),
                                          c.ps[0:DH, n % 2, :]).then_inc(*wide_in.next())
                else:
                    nc.vector.tensor_copy(cm[:, 2 * g:2 * g + 2, :].rearrange("p h n -> p (h n)"),
                                          c.ps[:, n % 2, :]).then_inc(*wide_in.next())

            if rope:
                wide_out(0)
                for h in range(NH):
                    if h % 2 == 0 and h < 14:
                        wide_out(h // 2 + 1)
                    if h >= 2:
                        dve.wait_ge(rot_in.handle, rot_in.at(2 * (h - 1)))
                    for e, f in ((0, 0), (1, 1), (0, 1), (1, 0)):
                        src = e if f == 0 else 1 - e
                        dve.wait_ge(big_mm.handle, big_mm.at(2 * h + 1 + src))
                        nc.vector.tensor_tensor(valid(prod[h % 2][2 * e + f]), valid(c.ps[0:DH, 4 + src, 0:NT]),
                                                tab[:, 2 * e + f, :].unsqueeze(1).broadcast_to([DH, B, T]),
                                                ALU.mult).then_inc(*prod_in.next())
            else:
                for t in range(8):
                    wide_out(t)
                    if 2 <= t <= 5:
                        g = t - 2
                        dve.wait_ge(fold_mm.handle, fold_mm.at(g + 1))
                        if g >= 2:
                            dve.wait_ge(lat_mm.handle, lat_mm.at(2 * (g - 1)))
                        nc.vector.tensor_copy(fold[g % 2].rearrange("p k h d -> p (k h d)"), c.ps[:, 4 + g % 2, :]).then_inc(*fold_in.next())

            def rowmax(i):
                dve.wait_ge(scored.handle, scored.at(i + 1))
                if i - 3 > 0:
                    dve.wait_ge(exped.handle, exped.at(i - 3))
                b0 = slot(i)
                nc.vector.tensor_reduce(stat[:, i % 4:i % 4 + 1], c.ps[:, b0:b0 + 3, 0:4 * LP], AX.XY, ALU.max,
                                             negate=True).then_inc(*maxed.next())
                dve.wait_ge(maxed.handle, maxed.last())

            def recips(i):
                dve.wait_ge(exped.handle, exped.at(i + 1))
                nc.vector.reciprocal(stat[:, 8 + i % 4:9 + i % 4], stat[:, 4 + i % 4:5 + i % 4]).then_inc(*recip.next())
                dve.wait_ge(recip.handle, recip.last())

            def copy_turned(i, k):
                if i % UNITS == 0 and k == 0 and i > 0:
                    dve.wait_ge(pv_mm.handle, pv_mm.at(i // UNITS))
                dve.wait_ge(turned.handle, turned.at(3 * i + k + 1))
                u = i % UNITS
                nc.vector.tensor_copy(pT[:, 4 * k:4 * k + 4, u * 128:(u + 1) * 128],
                                      c.ps[0:LP, turn_bank(i, k), :].rearrange("p (l q) -> p l q", l=4)).then_inc(*t_in.next())

            def keep(b):
                dve.wait_ge(pv_mm.handle, pv_mm.at(b + 1))
                dve.wait_ge(padded.handle, padded.at(1))
                nc.vector.tensor_copy(ctxT[:, :, b, 0:T], c.ps[:, turn_bank(b * UNITS + UNITS - 1, 3), 0:NT]
                                           .rearrange("p (h t) -> p h t", h=8)).then_inc(*ct_in.next())

            rowmax(0)
            for i in range(NU + 2):
                turned_too, kept = i >= 1 and i - 1 < NU, i >= UNITS + 1 and i % UNITS == 1
                if turned_too and not kept:
                    copy_turned(i - 1, 0)
                if i < NU:
                    recips(i)
                if turned_too and not kept:
                    copy_turned(i - 1, 1)
                if i + 1 < NU:
                    rowmax(i + 1)
                if turned_too and not kept:
                    copy_turned(i - 1, 2)
                if kept:
                    keep(i // UNITS - 1)
                if turned_too and kept:
                    for k in range(3):
                        copy_turned(i - 1, k)
            dve.wait_ge(t_in.handle, t_in.last())
            dve.wait_ge(ct_in.handle, ct_in.last())
            norm_vector(c, s, dve, False)



class Experts:

    def __init__(self, cols, experts, top, chunks, gate_tiles, gate, up, down, downs, router, spread, extra):
        self.cols, self.experts, self.top, self.chunks = cols, experts, top, chunks
        self.hidden, self.gate, self.up, self.down, self.downs = gate_tiles, gate, up, down, downs
        self.router, self.spread, self.extra = router, spread, extra


def feed_forward(c, name, f, now, prefetch, store=None, meanwhile=None):
    nc, s = c.nc, Stage(c, name)
    kind, E, last = name[:2], f.experts, store is not None
    wg = c.at(f.gate, KT * f.hidden).rearrange("p (k n) -> p k n", k=KT)
    wu = c.at(f.up, KT * f.hidden).rearrange("p (k n) -> p k n", k=KT)
    wd = c.at(f.down, f.downs * D).rearrange("p (h n) -> p h n", n=D)
    wr = c.at(f.router, KT * f.cols).rearrange("p (k n) -> p k n", k=KT)
    W = 16384
    hid = [c.at(W + 512 * i, 512).rearrange("p (b t) -> p b t", b=B) for i in range(2)]
    silu = [c.at(W + 1024 + NT * i, NT) for i in range(2)]
    comb = c.at(W + 1920, 512).rearrange("p (j e) -> p j e", j=J)
    combT = c.at(W + 2432, NT)
    cand = c.at(W + 2880, J * (E + 8)).rearrange("p (j e) -> p j e", j=J)
    left = c.at(W + 3424, J * (E + 8)).rearrange("p (j e) -> p j e", j=J)
    ex = c.at(W + 3968, J * E).rearrange("p (j e) -> p j e", j=J)
    top8 = c.at(W + 4480, J * 8).rearrange("p (j e) -> p j e", j=J)
    small = c.at(W + 4512, 32)
    mix = c.at(W + 4544, 32)
    spread = c.at(f.spread, 2048).rearrange("p (h m) -> p h m", m=128)[:, 0:16, :]
    logits, expin, exped, comb_in, comb_t, combT_in = (
        s.sem(x) for x in ("logits", "expin", "exped", "comb_in", "comb_t", "combT_in"))
    gu_mm, bc_mm, silu_in, hid_in, down_mm, padded = (
        s.sem(x) for x in ("gu_mm", "bc_mm", "silu_in", "hid_in", "down_mm", "padded"))
    N = len(f.chunks)
    weighted = [n for n, ch in enumerate(f.chunks) if ch[2] is not None]
    mixing = kind == "L0"

    def bank(n):
        return 2 + 3 * (n % 2)

    with nc.Block(no_gpsimd_drain=True) as block:
        @block.sync
        def _(sp):
            if now:
                c.load(sp, name + "_late", now)
            prefetch(sp)
            if last:
                norm_store(c, s, sp, store)

        @block.gpsimd
        def _(pool):
            for i in range(2):
                nc.gpsimd.memset(hid[i][:, :, T:TP], 0.0).then_inc(*padded.next())
            nc.gpsimd.memset(comb, 0.0).then_inc(*padded.next())
            nc.gpsimd.memset(cand[:, :, E:E + 8], -3.0e38).then_inc(*padded.next())
            nc.gpsimd.memset(top8, -3.0e38).then_inc(*padded.next())
            pool.wait_ge(padded.handle, padded.at(5))

        @block.tensor
        def _(pe):
            pe.wait_ge(c.loaded[name].handle, 16 * c.expect[name])
            for j in range(J):
                for k in range(KT):
                    m = nc.tensor.matmul(c.ps[:, 7, j * f.cols:(j + 1) * f.cols], c.x_feat[:, k, 2 * j:2 * j + 2, :],
                                         wr[:, k, :], start=(k == 0), stop=(k == KT - 1))
            m.then_inc(*logits.next())

            def arrived_late():
                if now:
                    pe.wait_ge(c.loaded[name + "_late"].handle, 16 * c.expect[name + "_late"])

            def gate_up(n):
                if n - 1 > 0:
                    pe.wait_ge(hid_in.handle, hid_in.at(n - 1))
                m_ = f.chunks[n][0]
                for i, w in enumerate((wg, wu)):
                    for k in range(KT):
                        m = nc.tensor.matmul(c.ps[0:m_, bank(n) + i, 0:NT], w[:, k, n * 128:n * 128 + m_],
                                             c.x_feat[:, k, :, 0:T], start=(k == 0), stop=(k == KT - 1))
                m.then_inc(*gu_mm.next())

            def weights(n):
                if n in weighted:
                    pe.wait_ge(combT_in.handle, combT_in.at(1))
                    m = nc.tensor.matmul(c.ps[:, bank(n) + 2, 0:NT], spread[:, f.chunks[n][2], :], combT,
                                         start=True, stop=True)
                    m.then_inc(*bc_mm.next())

            def down(n):
                pe.wait_ge(hid_in.handle, hid_in.at(n + 1))
                m_, t = f.chunks[n][0], f.chunks[n][1]
                for j in range(J):
                    m = project_out(c, pe, j, n, hid[n % 2][0:m_, 2 * j:2 * j + 2, :], wd[0:m_, t, :],
                                    n == 0, n == N - 1)
                    if n == N - 1 and j % 2 == 1:
                        m.then_inc(*s.y_done.next())
                if n < N - 1:
                    m.then_inc(*down_mm.next())

            gate_up(0)
            gate_up(1)
            if mixing:
                down(0)
                gate_up(2)
            pe.wait_ge(comb_in.handle, comb_in.at(1))
            for j in range(J):
                t = nc.tensor.transpose(c.ps[:, 7, j * 128:(j + 1) * 128], comb[:, j, :], c.ident[:])
            t.then_inc(*comb_t.next())
            arrived_late()
            weights(0)
            weights(1)
            for n in range(N):
                if n > 0 or not mixing:
                    down(n)
                if n + 2 < N:
                    if n > 0 or not mixing:
                        gate_up(n + 2)
                    weights(n + 2)
            norm_tensor(c, s, pe, last)

        @block.scalar
        def _(act):
            act.wait_ge(expin.handle, expin.at(1))
            nc.scalar.activation(ex, ex, ACT.Exp).then_inc(*exped.next())
            act.wait_ge(exped.handle, exped.last())
            if f.cols > E:
                act.wait_ge(expin.handle, expin.at(2))
                nc.scalar.activation(small[:, 24:28].rearrange("p (j o) -> p j o", j=J),
                                          c.ps[:, 7, 0:J * f.cols].rearrange("p (j e) -> p j e", j=J)[:, :, E:E + 1],
                                          ACT.Exp, scale=-1.0).then_inc(*exped.next())
                act.wait_ge(exped.handle, exped.last())
            for n in range(N):
                m_ = f.chunks[n][0]
                act.wait_ge(gu_mm.handle, gu_mm.at(n + 1))
                if n - 1 > 0:
                    act.wait_ge(hid_in.handle, hid_in.at(n - 1))
                nc.scalar.activation(silu[n % 2][0:m_], c.ps[0:m_, bank(n), 0:NT], ACT.Silu).then_inc(*silu_in.next())
                act.wait_ge(silu_in.handle, silu_in.last())
            norm_scalar(c, s, act, last)

        @block.vector
        def _(dve):
            V = nc.vector
            dve.wait_ge(c.loaded[name].handle, 16 * c.expect[name])
            dve.wait_ge(padded.handle, padded.at(5))
            spr = lambda ap: ap.unsqueeze(2).broadcast_to([128, J, E])
            if mixing:
                amp = c.at(f.extra, 16)
                scale = c.at(f.extra + 16, 1)
                V.tensor_tensor(amp, amp, amp, ALU.mult).then_inc(*s.dve_chain.next())
                dve.wait_ge(s.dve_chain.handle, s.dve_chain.last())
                V.tensor_reduce(mix[:, 0:8], amp.rearrange("p (k two) -> p k two", two=2), AX.X, ALU.add).then_inc(*s.dve_chain.next())
                dve.wait_ge(s.dve_chain.handle, s.dve_chain.last())
                V.tensor_reduce(mix[:, 8:9], mix[:, 0:8], AX.X, ALU.add).then_inc(*s.dve_chain.next())
                dve.wait_ge(s.dve_chain.handle, s.dve_chain.last())
                V.tensor_scalar(mix[:, 8:9], mix[:, 8:9], 1e-8, None, ALU.add).then_inc(*s.dve_chain.next())
                dve.wait_ge(s.dve_chain.handle, s.dve_chain.last())
                V.reciprocal(mix[:, 8:9], mix[:, 8:9]).then_inc(*s.dve_chain.next())
                dve.wait_ge(s.dve_chain.handle, s.dve_chain.last())
                V.tensor_scalar(mix[:, 0:8], mix[:, 0:8], mix[:, 8:9], scale, ALU.mult, ALU.mult).then_inc(*s.dve_chain.next())
                dve.wait_ge(s.dve_chain.handle, s.dve_chain.last())
                V.tensor_copy(spread[:, 0:8, :], mix[:, 0:8].unsqueeze(2).broadcast_to([128, 8, 128])).then_inc(*s.dve_chain.next())
                dve.wait_ge(s.dve_chain.handle, s.dve_chain.last())
            def gated(n):
                m_ = f.chunks[n][0]
                dve.wait_ge(silu_in.handle, silu_in.at(n + 1))
                if n - 1 > 0:
                    dve.wait_ge(down_mm.handle, down_mm.at(n - 1))
                up = c.ps[0:m_, bank(n) + 1, 0:NT]
                h = hid[n % 2][0:m_, :, 0:T]
                sl = silu[n % 2][0:m_]
                if n in weighted:
                    V.tensor_tensor(sl, up, sl, ALU.mult).then_inc(*s.dve_chain.next())
                    dve.wait_ge(s.dve_chain.handle, s.dve_chain.last())
                    dve.wait_ge(bc_mm.handle, bc_mm.at(weighted.index(n) + 1))
                    V.tensor_tensor(h, valid(c.ps[0:m_, bank(n) + 2, 0:NT]), valid(sl), ALU.mult).then_inc(*hid_in.next())
                else:
                    V.tensor_tensor(h, valid(up), valid(sl), ALU.mult).then_inc(*hid_in.next())
                if meanwhile is not None and n >= 2:
                    meanwhile(s, dve, n - 2)

            dve.wait_ge(logits.handle, logits.at(1))
            lg = c.ps[:, 7, 0:J * f.cols].rearrange("p (j e) -> p j e", j=J)[:, :, 0:E]
            V.tensor_reduce(small[:, 0:4], lg, AX.X, ALU.max).then_inc(*s.dve_chain.next())
            dve.wait_ge(s.dve_chain.handle, s.dve_chain.last())
            V.tensor_tensor(ex, lg, spr(small[:, 0:4]), ALU.subtract).then_inc(*expin.next())
            dve.wait_ge(expin.handle, expin.last())
            if kind == "L1":
                bias = c.at(f.extra, 16)
                V.tensor_tensor(cand[:, :, 0:E], lg, bias.unsqueeze(1).broadcast_to([128, J, E]), ALU.add).then_inc(*s.dve_chain.next())
                dve.wait_ge(s.dve_chain.handle, s.dve_chain.last())
            elif not mixing:
                V.tensor_copy(cand[:, :, 0:E], lg).then_inc(*expin.next())
                dve.wait_ge(expin.handle, expin.last())
            dve.wait_ge(exped.handle, exped.at(1))
            if mixing:
                V.tensor_reduce(small[:, 4:8], ex, AX.X, ALU.add).then_inc(*s.dve_chain.next())
                dve.wait_ge(s.dve_chain.handle, s.dve_chain.last())
                V.reciprocal(small[:, 4:8], small[:, 4:8]).then_inc(*s.dve_chain.next())
                dve.wait_ge(s.dve_chain.handle, s.dve_chain.last())
                V.tensor_tensor(ex, ex, spr(small[:, 4:8]), ALU.mult).then_inc(*s.dve_chain.next())
                dve.wait_ge(s.dve_chain.handle, s.dve_chain.last())
                V.tensor_copy(cand[:, :, 0:E], ex).then_inc(*s.dve_chain.next())
                dve.wait_ge(s.dve_chain.handle, s.dve_chain.last())
            if mixing:
                gated(0)
            for j in range(J):
                V.max(mix[:, 16:24], cand[:, j, 0:E]).then_inc(*s.dve_chain.next())
                dve.wait_ge(s.dve_chain.handle, s.dve_chain.last())
                V.tensor_copy(top8[:, j, 0:f.top], mix[:, 16:16 + f.top]).then_inc(*s.dve_chain.next())
                dve.wait_ge(s.dve_chain.handle, s.dve_chain.last())
                V.match_replace(left[:, j, :], top8[:, j, :], cand[:, j, :], 3.0e38).then_inc(*s.dve_chain.next())
                dve.wait_ge(s.dve_chain.handle, s.dve_chain.last())
            V.tensor_tensor(left[:, :, 0:E], left[:, :, 0:E], cand[:, :, 0:E], ALU.not_equal).then_inc(*s.dve_chain.next())
            dve.wait_ge(s.dve_chain.handle, s.dve_chain.last())
            V.tensor_tensor(ex, ex, left[:, :, 0:E], ALU.mult).then_inc(*s.dve_chain.next())
            dve.wait_ge(s.dve_chain.handle, s.dve_chain.last())
            V.tensor_reduce(small[:, 8:12], ex, AX.X, ALU.add).then_inc(*s.dve_chain.next())
            dve.wait_ge(s.dve_chain.handle, s.dve_chain.last())
            eps = {"L0": 1e-8, "L3": 1e-20}.get(kind, 0.0)
            if eps:
                V.tensor_scalar(small[:, 8:12], small[:, 8:12], eps, None, ALU.add).then_inc(*s.dve_chain.next())
                dve.wait_ge(s.dve_chain.handle, s.dve_chain.last())
            V.reciprocal(small[:, 12:16], small[:, 8:12]).then_inc(*s.dve_chain.next())
            dve.wait_ge(s.dve_chain.handle, s.dve_chain.last())
            if f.cols > E:
                dve.wait_ge(exped.handle, exped.at(2))
                V.tensor_scalar(small[:, 24:28], small[:, 24:28], 1.0, None, ALU.add).then_inc(*s.dve_chain.next())
                dve.wait_ge(s.dve_chain.handle, s.dve_chain.last())
                V.reciprocal(comb[:, :, E:E + 1], small[:, 24:28].rearrange("p (j o) -> p j o", j=J)).then_inc(*s.dve_chain.next())
                dve.wait_ge(s.dve_chain.handle, s.dve_chain.last())
            V.tensor_tensor(comb[:, :, 0:E], ex, spr(small[:, 12:16]), ALU.mult).then_inc(*comb_in.next())
            dve.wait_ge(comb_in.handle, comb_in.last())
            dve.wait_ge(comb_t.handle, comb_t.at(1))
            V.tensor_copy(combT.rearrange("p (b t) -> p b t", b=B),
                               c.ps[:, 7, :].rearrange("p (b t) -> p b t", b=B)[:, :, 0:T]).then_inc(*combT_in.next())
            dve.wait_ge(combT_in.handle, combT_in.last())
            for n in range(1 if mixing else 0, N):
                gated(n)
            norm_vector(c, s, dve, last)



class SmallHeads:

    def __init__(self, c, s, base, hd, scale, mask, v_at=None):
        self.c, self.s, self.hd, self.nm, self.scale, self.mask = c, s, hd, 32 // hd, scale, mask
        o = base
        self.q = c.at(o, 1024).rearrange("p (k b t) -> p k b t", k=KT, b=B)
        o += 1024
        self.k = c.at(o, self.nm * 1024).rearrange("p (m k b t) -> p m k b t", m=self.nm, k=KT, b=B)
        o += self.nm * 1024
        if v_at is None:
            v_at, o = o, o + 2048
        self.v = c.at(v_at, 2048).rearrange("p (g r n) -> p g r n", g=4, r=2)
        self.pads = 4
        o -= 2048
        self.p = c.at(o + 2048, 2048).rearrange("p (i e t) -> p i e t", i=4, e=8)
        self.pT = c.at(o + 4096, 2048).rearrange("p (i e g q) -> p i e g q", i=4, e=2, g=2)
        self.ctx = c.at(o + 6144, 1024).rearrange("p (j n) -> p j n", j=J)
        self.ctxT = c.at(o + 7168, 1024).rearrange("p (k b t) -> p k b t", k=KT, b=B)
        self.mx = c.at(o + 8192, 32)
        self.rs = c.at(o + 8224, 128).rearrange("p (i q e j) -> p i q e j", i=4, q=4, e=2)
        self.end = o + 8352
        (self.scored, self.shifted, self.exped, self.turned, self.t_act, self.ctx_mm, self.summed, self.ctx_in,
         self.ctx_t, self.ctxT_in, self.padded, self.q_in, self.k_in, self.v_in) = (s.sem(i) for i in range(14))

    def pool(self, pool):
        n = self.c.nc
        n.gpsimd.memset(self.q[:, :, :, T:TP], 0.0).then_inc(*self.padded.next())
        n.gpsimd.memset(self.p[:, :, :, T:TP], 0.0).then_inc(*self.padded.next())
        n.gpsimd.memset(self.v[0:TP, :, 1, :], 0.0).then_inc(*self.padded.next())
        pool.wait_ge(self.padded.handle, self.padded.at(self.padded.n))
        n.gpsimd.memset(self.v[TP:128, :, 0, :], 0.0).then_inc(*self.padded.next())
        pool.wait_ge(self.padded.handle, self.padded.at(self.padded.n))

    def tensor(self, pe, q_steps, k_steps, v_steps):
        c, nc = self.c, self.c.nc
        if q_steps > 0:
            pe.wait_ge(self.q_in.handle, self.q_in.at(q_steps))
        if k_steps > 0:
            pe.wait_ge(self.k_in.handle, self.k_in.at(k_steps))
        pe.wait_ge(self.padded.handle, self.padded.at(self.pads))

        def scores(g):
            if g > 0:
                pe.wait_ge(self.shifted.handle, self.shifted.at(2 * g))
            k, m_ = divmod(2 * g, self.nm)
            for b in range(B):
                for i in range(4):
                    m = nc.tensor.matmul(
                        c.ps[(b % 2) * TP:(b % 2 + 1) * TP, 2 + i, 0:NT]
                        .rearrange("p (e j t) -> p e j t", e=2, t=T)[:, :, b // 2, :],
                        self.q[32 * i:32 * i + 32, k, b, :], self.k[32 * i:32 * i + 32, m_:m_ + 2, k, b, 0:T],
                        start=True, stop=True)
            m.then_inc(*self.scored.next())

        def turn(g):
            for i in range(4):
                pe.wait_ge(self.exped.handle, self.exped.at(2 * g + i // 2 + 1))
                if 4 * g + i >= 2:
                    pe.wait_ge(self.t_act.handle, self.t_act.at(4 * g + i - 1))
                for e in range(2):
                    for h in range(2):
                        t = nc.tensor.transpose(c.ps[:, 6 + i % 2, (2 * e + h) * 128:(2 * e + h + 1) * 128],
                                                self.p[:, i, e * 4 + 2 * h:e * 4 + 2 * h + 2, :], c.ident[:])
                t.then_inc(*self.turned.next())

        def context(g):
            if g == 0:
                pe.wait_ge(self.v_in.handle, self.v_in.at(v_steps))
            for i in range(4):
                pe.wait_ge(self.t_act.handle, self.t_act.at(4 * g + i + 1))
                for e in range(2):
                    k, m_ = divmod(2 * g + e, self.nm)
                    f = k * 128 + 32 * i + m_ * self.hd
                    for a in range(2):
                        for h in range(2):
                            m = nc.tensor.matmul(
                                c.ps[h * TP:(h + 1) * TP, a, :].rearrange("p (r n) -> p r n", r=2)[:, :, f:f + self.hd],
                                self.pT[:, i, e, a, h * TP:(h + 1) * TP],
                                self.v[:, 2 * a + h, :, f:f + self.hd], start=True, stop=True,
                                skip_group_check=True)
            m.then_inc(*self.ctx_mm.next())

        scores(0)
        scores(1)
        for g in range(self.nm):
            turn(g)
            context(g)
            if g + 2 < self.nm:
                scores(g + 2)
        pe.wait_ge(self.ctx_in.handle, self.ctx_in.at(J * KT))
        for k in range(KT):
            for j in range(J):
                t = nc.tensor.transpose(c.ps[:, 6 + k, j * 128:(j + 1) * 128], self.ctx[:, j, k * 128:(k + 1) * 128],
                                        c.ident[:])
            t.then_inc(*self.ctx_t.next())

    def vector(self, dve):
        c, s, V = self.c, self.s, self.c.nc.vector
        dve.wait_ge(self.padded.handle, self.padded.at(self.pads))
        for g in range(self.nm):
            dve.wait_ge(self.scored.handle, self.scored.at(g + 1))
            for a in range(2):
                if g > 0:
                    dve.wait_ge(self.turned.handle, self.turned.at(4 * (g - 1) + 2 * a + 2))
                sc = c.ps[:, 2 + 2 * a:4 + 2 * a, 0:NT].rearrange("p i (e t) -> p i e t", t=T)
                p = self.p[:, 2 * a:2 * a + 2, :, 0:T]
                mx = self.mx.rearrange("p (i e) -> p i e", i=4)[:, 2 * a:2 * a + 2]
                spread = mx.unsqueeze(3).broadcast_to([128, 2, 8, T])
                if self.mask is not None:
                    V.tensor_tensor(p, sc, self.mask.rearrange("p (a b t) -> p a b t", a=1, b=1)
                                         .broadcast_to([128, 2, 8, T]), ALU.add).then_inc(*s.dve_chain.next())
                    dve.wait_ge(s.dve_chain.handle, s.dve_chain.last())
                    sc = p
                V.tensor_reduce(mx, sc, AX.X, ALU.max).then_inc(*s.dve_chain.next())
                dve.wait_ge(s.dve_chain.handle, s.dve_chain.last())
                V.tensor_tensor(p, sc, spread, ALU.subtract).then_inc(*self.shifted.next())
            for a in range(2):
                dve.wait_ge(self.exped.handle, self.exped.at(2 * g + a + 1))
                V.tensor_reduce(self.rs[:, 2 * a:2 * a + 2, g, :, :].rearrange("p i e j -> p i (e j)"),
                                self.p[:, 2 * a:2 * a + 2, :, 0:T], AX.X, ALU.add).then_inc(*s.dve_chain.next())
            dve.wait_ge(s.dve_chain.handle, s.dve_chain.last())
            rs = self.rs[:, :, g, :, :].rearrange("p i e j -> p i (e j)")
            V.reciprocal(rs, rs).then_inc(*self.summed.next())
        dve.wait_ge(self.summed.handle, self.summed.last())
        dve.wait_ge(self.ctx_mm.handle, self.ctx_mm.at(self.nm))
        for j in range(J):
            for k in range(KT):
                r = self.rs[:].rearrange("p i q e j -> p i (q e) j")[:, :, k * self.nm:(k + 1) * self.nm, j:j + 1]
                o = self.ctx[:, j, k * 128:(k + 1) * 128].rearrange("p (i m d) -> p i m d", i=4, m=self.nm)
                src = c.ps[:, j // 2, (j % 2) * D + k * 128:(j % 2) * D + (k + 1) * 128]
                V.tensor_tensor(o, src.rearrange("p (i m d) -> p i m d", i=4, m=self.nm),
                                     r.broadcast_to([128, 4, self.nm, self.hd]), ALU.mult).then_inc(*self.ctx_in.next())

    def scalar(self, act):
        c, s, A = self.c, self.s, self.c.nc.scalar
        for g in range(self.nm):
            for a in range(2):
                act.wait_ge(self.shifted.handle, self.shifted.at(2 * g + a + 1))
                p = self.p[:, 2 * a:2 * a + 2, :, 0:T].rearrange("p i e t -> p (i e) t")
                A.activation(p, p, ACT.Exp, scale=self.scale).then_inc(*self.exped.next())
            for i in range(4):
                act.wait_ge(self.turned.handle, self.turned.at(4 * g + i + 1))
                if g > 0:
                    act.wait_ge(self.ctx_mm.handle, self.ctx_mm.at(g))
                A.copy(self.pT[:, i].rearrange("p e g q -> p (e g q)"), c.ps[:, 6 + i % 2, :]).then_inc(*self.t_act.next())
        for k in range(KT):
            act.wait_ge(self.ctx_t.handle, self.ctx_t.at(k + 1))
            A.copy(self.ctxT[:, k, :, :], c.ps[:, 6 + k, :].rearrange("p (b t) -> p b t", b=B)).then_inc(*self.ctxT_in.next())


def value_tile(c, out, x, g, weights):
    b = 4 * (g // 2) + g % 2
    for k, w in enumerate(weights):
        for r in range(2):
            m = c.nc.tensor.matmul(out[r * TP:(r + 1) * TP], x[k][:, b + 2 * r, :], w,
                                   start=(k == 0), stop=(k == len(weights) - 1), skip_group_check=True)
    return m



CH, CL = NT // 32, 32
MAGIC = 12582912.0


def L1_ATTN_LOADS(c):
    return [("L1a_W", c.at(0, 2048)), ("L1a_WT", c.at(2048, 2048)), ("L1a_bias", c.at(15360, 8)),
            ("L1a_ob", c.at(15368, D))]


def quantise(c, s, dve, tm_in, tmax_in, src, res, cb, small, cb_in, done):
    V = c.nc.vector
    r3 = res.rearrange("p (n l) -> p n l", l=CL)
    s3 = src.rearrange("p (n l) -> p n l", l=CL)
    N = KT * CH
    f = lambda i: small[:, i * N:(i + 1) * N]
    mx, mn, cmax, t1, thr, fac, sc, inv = (f(i) for i in range(8))
    tm, tmax = small[:, 8 * N:8 * N + CH], small[:, 8 * N + CH:8 * N + 2 * CH]
    spread = lambda ap: ap.unsqueeze(2).broadcast_to([128, N, CL])
    V.tensor_reduce(mx, s3, AX.X, ALU.max).then_inc(*s.dve_chain.next())
    dve.wait_ge(s.dve_chain.handle, s.dve_chain.last())
    V.tensor_reduce(mn, s3, AX.X, ALU.min).then_inc(*s.dve_chain.next())
    dve.wait_ge(s.dve_chain.handle, s.dve_chain.last())
    V.tensor_tensor(cb, mx, mn, ALU.add).then_inc(*s.dve_chain.next())
    dve.wait_ge(s.dve_chain.handle, s.dve_chain.last())
    V.tensor_scalar(cb, cb, 0.5, None, ALU.mult).then_inc(*cb_in.next())
    dve.wait_ge(cb_in.handle, cb_in.last())
    V.tensor_tensor(r3, s3, spread(cb), ALU.subtract).then_inc(*s.dve_chain.next())
    dve.wait_ge(s.dve_chain.handle, s.dve_chain.last())
    V.tensor_tensor(mx, mx, cb, ALU.subtract).then_inc(*s.dve_chain.next())
    dve.wait_ge(s.dve_chain.handle, s.dve_chain.last())
    V.tensor_tensor(mn, cb, mn, ALU.subtract).then_inc(*s.dve_chain.next())
    dve.wait_ge(s.dve_chain.handle, s.dve_chain.last())
    V.tensor_tensor(cmax, mx, mn, ALU.max).then_inc(*s.dve_chain.next())
    dve.wait_ge(s.dve_chain.handle, s.dve_chain.last())
    V.tensor_tensor(tm, cmax[:, 0:CH], cmax[:, CH:N], ALU.max).then_inc(*tm_in.next())
    dve.wait_ge(tm_in.handle, tm_in.last())
    if tm_in.n > 0:
        dve.wait_ge(tmax_in.handle, tmax_in.at(tm_in.n))
    for k in range(KT):
        V.tensor_copy(t1[:, k * CH:(k + 1) * CH], tmax).then_inc(*s.dve_chain.next())
        dve.wait_ge(s.dve_chain.handle, s.dve_chain.last())
    V.memset(fac, 2.0 ** -7).then_inc(*s.dve_chain.next())
    dve.wait_ge(s.dve_chain.handle, s.dve_chain.last())
    for m in range(7):
        V.scalar_tensor_tensor(out=thr, in0=t1, scalar=2.0 ** (m - 7), in1=cmax, op0=ALU.mult, op1=ALU.is_lt).then_inc(*s.dve_chain.next())
        dve.wait_ge(s.dve_chain.handle, s.dve_chain.last())
        V.scalar_tensor_tensor(out=fac, in0=thr, scalar=1.0, in1=fac, op0=ALU.add, op1=ALU.mult).then_inc(*s.dve_chain.next())
        dve.wait_ge(s.dve_chain.handle, s.dve_chain.last())
    V.tensor_tensor(sc, t1, fac, ALU.mult).then_inc(*s.dve_chain.next())
    dve.wait_ge(s.dve_chain.handle, s.dve_chain.last())
    V.tensor_scalar(sc, sc, 1.0 / 7.0, 1e-9, ALU.mult, ALU.max).then_inc(*s.dve_chain.next())
    dve.wait_ge(s.dve_chain.handle, s.dve_chain.last())
    V.reciprocal(inv, sc).then_inc(*s.dve_chain.next())
    dve.wait_ge(s.dve_chain.handle, s.dve_chain.last())
    V.tensor_tensor(r3, r3, spread(inv), ALU.mult).then_inc(*s.dve_chain.next())
    dve.wait_ge(s.dve_chain.handle, s.dve_chain.last())
    V.tensor_scalar(res, res, MAGIC, MAGIC, ALU.add, ALU.subtract).then_inc(*s.dve_chain.next())
    dve.wait_ge(s.dve_chain.handle, s.dve_chain.last())
    V.tensor_scalar(res, res, 7.0, -8.0, ALU.min, ALU.max).then_inc(*s.dve_chain.next())
    dve.wait_ge(s.dve_chain.handle, s.dve_chain.last())
    V.tensor_tensor(r3, r3, spread(sc), ALU.mult).then_inc(*done.next())
    dve.wait_ge(done.handle, done.last())


WQ4_AT = 24908


def quantise_weights(c, s, dve, step):
    V = c.nc.vector
    w = c.at(0, 2048).rearrange("p (w n) -> p w n", n=D)
    wq4 = c.at(WQ4_AT, 2048).rearrange("p (w n) -> p w n", n=D)
    wsc = c.at(WQ4_AT + 2048, 16)
    if step == 0:
        dve.wait_ge(c.loaded["L1_attn"].handle, 16 * c.expect["L1_attn"])
        V.tensor_reduce(wsc[:, 0:8], w, AX.X, ALU.max, apply_absolute_value=True).then_inc(*s.dve_chain.next())
    elif step == 1:
        V.tensor_scalar(wsc[:, 0:8], wsc[:, 0:8], 1.0 / 7.0, 1e-9, ALU.mult, ALU.max).then_inc(*s.dve_chain.next())
        dve.wait_ge(s.dve_chain.handle, s.dve_chain.last())
        V.reciprocal(wsc[:, 8:16], wsc[:, 0:8]).then_inc(*s.dve_chain.next())
    elif step == 2:
        V.tensor_tensor(wq4, w, wsc[:, 8:16].unsqueeze(2).broadcast_to([128, 8, D]), ALU.mult).then_inc(*s.dve_chain.next())
    elif step == 3:
        V.tensor_scalar(wq4, wq4, MAGIC, MAGIC, ALU.add, ALU.subtract).then_inc(*s.dve_chain.next())
    elif step == 4:
        V.tensor_scalar(wq4, wq4, 7.0, -8.0, ALU.min, ALU.max).then_inc(*s.dve_chain.next())
    elif step == 5:
        V.tensor_tensor(wq4, wq4, wsc[:, 0:8].unsqueeze(2).broadcast_to([128, 8, D]), ALU.mult).then_inc(*s.dve_chain.next())
    dve.wait_ge(s.dve_chain.handle, s.dve_chain.last())


def l1_attention(c, now, prefetch):
    nc, s = c.nc, Stage(c, "L1_attn")
    wT = c.at(2048, 2048).rearrange("p (w k n) -> p w k n", w=4, k=KT)
    bias = c.at(15360, 8)
    ob = c.at(15368, D)
    W = 15700
    wq4 = c.at(WQ4_AT, 2048).rearrange("p (w n) -> p w n", n=D)
    wqT = c.at(W + 2048, 2048).rearrange("p (w k n) -> p w k n", w=4, k=KT)
    W += 4096
    src, res, cbx = (c.at(W + i * 2 * NT, 2 * NT) for i in range(3))
    W += 6 * NT
    small = c.at(W, 320)
    cb = c.at(W + 320, 28)
    W += 376
    vT = c.at(W, 1024).rearrange("p (k b t) -> p k b t", k=KT, b=B)
    W += 1024
    at = SmallHeads(c, s, W, 8, 8 ** -0.5, None)
    resP = at.p.rearrange("p i e t -> p (i e t)")[:, 0:1024].rearrange("p (k b t) -> p k b t", k=KT, b=B)
    cbP = at.p.rearrange("p i e t -> p (i e t)")[:, 1024:2048].rearrange("p (k b t) -> p k b t", k=KT, b=B)
    tm_in, tmax_in, cb_in, cbx_in, cbp_in, quant, wt_mm, wt_in, proj, got, vt_in, v_mm, resp_in = (
        s.sem(x) for x in ("tm_in", "tmax_in", "cb_in", "cbx_in", "cbp_in", "quant", "wt_mm", "wt_in", "proj", "got", "vt_in", "v_mm",
                           "resp_in"))
    small_at = 8 * KT * CH
    tm, tmax = small[:, small_at:small_at + CH], small[:, small_at + CH:small_at + 2 * CH]

    def spread_bias(act):
        nc.scalar.copy(cbx.rearrange("p (n l) -> p n l", l=CL),
                       cb.unsqueeze(2).broadcast_to([128, KT * CH, CL])).then_inc(*cbx_in.next())

    with nc.Block(no_gpsimd_drain=True) as block:
        @block.sync
        def _(sp):
            c.load(sp, "L1_attn", now)
            prefetch(sp)

        @block.gpsimd
        def _(pool):
            at.pool(pool)
            nc.gpsimd.memset(vT[:, :, :, T:TP], 0.0).then_inc(*at.padded.next())
            pool.wait_ge(at.padded.handle, at.padded.at(at.padded.n))
            for n in range(2):
                pool.wait_ge(tm_in.handle, tm_in.at(n + 1))
                nc.gpsimd.partition_all_reduce(tmax, tm, 128, bass.bass_isa.ReduceOp.max).then_inc(*tmax_in.next())
                pool.wait_ge(tmax_in.handle, tmax_in.at(n + 1))
                if n == 0:
                    pool.wait_ge(at.turned.handle, at.turned.at(4 * at.nm))
                    nc.gpsimd.memset(resP[:, :, :, T:TP], 0.0).then_inc(*at.padded.next())
                    nc.gpsimd.memset(cbP[:, :, :, T:TP], 0.0).then_inc(*at.padded.next())

        @block.tensor
        def _(pe):
            pe.wait_ge(c.loaded["L1_attn"].handle, 16 * c.expect["L1_attn"])
            for w_ in range(4):
                for k in range(KT):
                    for o in range(2):
                        t = nc.tensor.transpose(c.ps[:, 2 + w_, k * D + o * 128:k * D + (o + 1) * 128],
                                                wq4[:, 2 * w_ + o, k * 128:(k + 1) * 128], c.ident[:])
                t.then_inc(*wt_mm.next())
            pe.wait_ge(wt_in.handle, wt_in.at(4))
            pe.wait_ge(cbx_in.handle, cbx_in.at(1))
            for n in range(6):
                w_, m_ = (1, 0, 2)[n // 2], n % 2
                for k in range(KT):
                    nc.tensor.matmul(c.ps[:, 2 + n, 0:NT], wT[:, w_, k, m_ * 128:(m_ + 1) * 128],
                                     cbx[:, k * NT:(k + 1) * NT], start=(k == 0), stop=False)
            pe.wait_ge(quant.handle, quant.at(1))
            for n in range(6):
                w_, m_ = (1, 0, 2)[n // 2], n % 2
                for k in range(KT):
                    m = nc.tensor.matmul(c.ps[:, 2 + n, 0:NT], wqT[:, w_, k, m_ * 128:(m_ + 1) * 128],
                                         res[:, k * NT:(k + 1) * NT], start=False, stop=(k == KT - 1))
                m.then_inc(*proj.next())
            pe.wait_ge(vt_in.handle, vt_in.at(4))
            pe.wait_ge(at.padded.handle, at.padded.at(at.pads + 1))
            for g in range(4):
                for k in range(KT):
                    t = nc.tensor.transpose(c.ps[:, g // 2, (g % 2) * D + k * 128:(g % 2) * D + (k + 1) * 128],
                                            vT[:, k, 2 * g:2 * g + 2, :], c.ident[:])
            t.then_inc(*v_mm.next())
            at.tensor(pe, 2, 2 * at.nm, 4)
            pe.wait_ge(cbp_in.handle, cbp_in.at(1))
            pe.wait_ge(at.padded.handle, at.padded.at(at.pads + 3))
            pe.wait_ge(at.ctx_in.handle, at.ctx_in.at(J * KT))
            for k in range(KT):
                for j in range(J):
                    project_out(c, pe, j, k, cbP[:, k, 2 * j:2 * j + 2, :], wT[:, 3, k, :], k == 0, False)
            pe.wait_ge(resp_in.handle, resp_in.at(1))
            for k in range(KT):
                for j in range(J):
                    m = project_out(c, pe, j, k, resP[:, k, 2 * j:2 * j + 2, :], wqT[:, 3, k, :], False, k == KT - 1)
                    if k == KT - 1 and j % 2 == 1:
                        m.then_inc(*s.y_done.next())
            norm_tensor(c, s, pe, False)

        @block.scalar
        def _(act):
            for w_ in range(4):
                act.wait_ge(wt_mm.handle, wt_mm.at(w_ + 1))
                nc.scalar.copy(wqT[:, w_].rearrange("p k n -> p (k n)"), c.ps[:, 2 + w_, :]).then_inc(*wt_in.next())
            act.wait_ge(cb_in.handle, cb_in.at(1))
            spread_bias(act)
            act.wait_ge(at.padded.handle, at.padded.at(at.pads + 1))
            for k in range(KT):
                act.wait_ge(proj.handle, proj.at(2 + k + 1))
                nc.scalar.activation(at.q[:, k, :, 0:T], valid(c.ps[:, 4 + k, 0:NT]), ACT.Identity,
                                          bias=bias[:, k:k + 1]).then_inc(*at.q_in.next())
            for k in range(KT):
                act.wait_ge(proj.handle, proj.at(4 + k + 1))
                for r in range(2):
                    nc.scalar.activation(
                        vT[:, k].rearrange("p (a e r) t -> p r a e t", e=2, r=2)[:, r, :, :, 0:T],
                        c.ps[:, 6 + k, 0:NT].rearrange("p (a r e t) -> p r a e t", a=2, r=2, e=2)[:, r],
                        ACT.Identity, bias=bias[:, 4 + k:5 + k]).then_inc(*vt_in.next())
            act.wait_ge(v_mm.handle, v_mm.at(1))
            for i in range(2):
                for r in range(2):
                    nc.scalar.copy(at.v[r * TP:(r + 1) * TP, 2 * i:2 * i + 2, r, :],
                       c.ps[r * TP:(r + 1) * TP, i, :].rearrange("p (g n) -> p g n", g=2)).then_inc(*at.v_in.next())
            at.scalar(act)
            act.wait_ge(cb_in.handle, cb_in.at(2))
            spread_bias(act)
            act.wait_ge(cbx_in.handle, cbx_in.last())
            act.wait_ge(at.turned.handle, at.turned.at(4 * at.nm))
            nc.scalar.copy(cbP[:, :, :, 0:T].rearrange("p k b t -> p (k b) t"),
                           cbx.rearrange("p (a t) -> p a t", t=T)).then_inc(*cbp_in.next())
            norm_scalar(c, s, act, False)

        @block.vector
        def _(dve):
            V = nc.vector

            dve.wait_ge(c.loaded["L1_attn"].handle, 16 * c.expect["L1_attn"])
            for k in range(KT):
                V.tensor_copy(valid(src[:, k * NT:(k + 1) * NT]), c.x_feat[:, k, :, 0:T]).then_inc(*s.dve_chain.next())
                dve.wait_ge(s.dve_chain.handle, s.dve_chain.last())
            quantise(c, s, dve, tm_in, tmax_in, src, res, cb, small, cb_in, quant)
            V.tensor_tensor(c.x_tok[:], c.x_tok[:], ob.unsqueeze(1).broadcast_to([128, J, D]), ALU.add).then_inc(*s.dve_chain.next())
            dve.wait_ge(s.dve_chain.handle, s.dve_chain.last())
            dve.wait_ge(at.padded.handle, at.padded.at(at.pads + 1))
            for k in range(KT):
                dve.wait_ge(proj.handle, proj.at(k + 1))
                for m in range(at.nm):
                    V.tensor_scalar(at.k[:, m, k, :, 0:T], valid(c.ps[:, 2 + k, 0:NT]), bias[:, 2 + k:3 + k],
                                         c.heads8[:, m:m + 1], ALU.add, ALU.mult).then_inc(*at.k_in.next())
            at.vector(dve)
            for k in range(KT):
                dve.wait_ge(at.ctxT_in.handle, at.ctxT_in.at(k + 1))
                V.tensor_copy(valid(src[:, k * NT:(k + 1) * NT]), at.ctxT[:, k, :, 0:T]).then_inc(*s.dve_chain.next())
                dve.wait_ge(s.dve_chain.handle, s.dve_chain.last())
            quantise(c, s, dve, tm_in, tmax_in, src, res, cb, small, cb_in, quant)
            V.tensor_copy(resP[:, :, :, 0:T].rearrange("p k b t -> p (k b) t"),
                               res.rearrange("p (a t) -> p a t", t=T)).then_inc(*resp_in.next())
            norm_vector(c, s, dve, False)



def L1_X_LOADS(c):
    return [("L1x_Wq", c.at(4096, 512)), ("L1x_Wkv", c.at(4608, 512, 64)), ("L1x_Wout", c.at(5120, 512)),
            ("L1x_lat", c.at(5632, 512, 64)), ("causal_add", c.at(37700, T))]


def output_of(c, s, at, pe, wo):
    pe.wait_ge(at.ctxT_in.handle, at.ctxT_in.at(KT))
    for k in range(KT):
        for j in range(J):
            m = project_out(c, pe, j, k, at.ctxT[:, k, 2 * j:2 * j + 2, :], wo[:, k, :], k == 0, k == KT - 1)
            if k == KT - 1 and j % 2 == 1:
                m.then_inc(*s.y_done.next())


def l1_cross(c, now, prefetch):
    nc, s = c.nc, Stage(c, "L1_xattn")
    wq = c.at(4096, 512).rearrange("p (k n) -> p k n", k=KT)
    wkv = c.at(4608, 512, 64)
    wo = c.at(5120, 512).rearrange("p (k n) -> p k n", k=KT)
    lat = c.at(5632, 512, 64).rearrange("p (b t) -> p b t", b=B)
    mask = c.at(37700, T)
    at = SmallHeads(c, s, 15360, 16, 0.25, mask, 0)
    proj = s.sem("proj")

    with nc.Block(no_gpsimd_drain=True) as block:
        @block.sync
        def _(sp):
            c.load(sp, "L1_xattn", now)
            prefetch(sp)

        @block.gpsimd
        def _(pool):
            at.pool(pool)

        @block.tensor
        def _(pe):
            pe.wait_ge(c.loaded["L1_xattn"].handle, 16 * c.expect["L1_xattn"])
            for m_ in range(2):
                for k in range(KT):
                    m = nc.tensor.matmul(c.ps[:, 2 + m_, 0:NT], wq[:, k, m_ * 128:(m_ + 1) * 128],
                                         c.x_feat[:, k, :, 0:T], start=(k == 0), stop=(k == KT - 1))
                m.then_inc(*proj.next())
            for m_ in range(2):
                m = nc.tensor.matmul(c.ps[:, 4 + m_, 0:NT], wkv[:, m_ * 128:(m_ + 1) * 128], lat[:, :, 0:T],
                                     start=True, stop=True)
                m.then_inc(*proj.next())
            for g in range(4):
                m = value_tile(c, c.ps[:, 6 + g // 2, (g % 2) * D:(g % 2 + 1) * D], [lat], g, [wkv[:, D:2 * D]])
            m.then_inc(*proj.next())
            at.tensor(pe, 2, 2 * at.nm, 4)
            output_of(c, s, at, pe, wo)
            norm_tensor(c, s, pe, False)

        @block.scalar
        def _(act):
            act.wait_ge(at.padded.handle, at.padded.at(at.pads))
            for k in range(KT):
                act.wait_ge(proj.handle, proj.at(k + 1))
                nc.scalar.copy(at.q[:, k, :, 0:T], valid(c.ps[:, 2 + k, 0:NT])).then_inc(*at.q_in.next())
            for k in range(KT):
                act.wait_ge(proj.handle, proj.at(2 + k + 1))
                for m in range(at.nm):
                    nc.scalar.activation(at.k[:, m, k, :, 0:T], valid(c.ps[:, 4 + k, 0:NT]), ACT.Copy,
                                              scale=c.heads16[:, m:m + 1]).then_inc(*at.k_in.next())
            at.scalar(act)
            norm_scalar(c, s, act, False)

        @block.vector
        def _(dve):
            dve.wait_ge(c.loaded["L1_xattn"].handle, 16 * c.expect["L1_xattn"])
            dve.wait_ge(proj.handle, proj.at(5))
            for i in range(2):
                for r in range(2):
                    nc.vector.tensor_copy(at.v[r * TP:(r + 1) * TP, 2 * i:2 * i + 2, r, :],
                       c.ps[r * TP:(r + 1) * TP, 6 + i, :].rearrange("p (g n) -> p g n", g=2)).then_inc(*at.v_in.next())
            at.vector(dve)
            norm_vector(c, s, dve, False)



def L2_ATTN_LOADS(c):
    return [("L2a_W", c.at(32500, 5 * 512)), ("L2a_Wo", c.at(35060, 512)), ("L2a_rope", c.at(35572, 2 * T)),
            ("causal_add2", c.at(35684, T))]


def l2_attention(c, now, prefetch):
    nc, s = c.nc, Stage(c, "L2_attn")
    w = c.at(32500, 5 * 512).rearrange("p (w k n) -> p w k n", w=5, k=KT)
    wo = c.at(35060, 512).rearrange("p (k n) -> p k n", k=KT)
    tab = c.at(35572, 2 * T).rearrange("p (i t) -> p i t", i=2)
    mask = c.at(35684, T)
    at = SmallHeads(c, s, 16384, 16, 0.25, mask)
    prod = [c.at(at.end + i * NT, NT) for i in range(2)]
    turned_k = [c.at(at.end + (2 + i) * NT, NT) for i in range(2)]
    proj, rotated = s.sem("proj"), s.sem("rotated")

    with nc.Block(no_gpsimd_drain=True) as block:
        @block.sync
        def _(sp):
            c.load(sp, "L2_attn", now)
            prefetch(sp)

        @block.gpsimd
        def _(pool):
            at.pool(pool)

        @block.tensor
        def _(pe):
            pe.wait_ge(c.loaded["L2_attn"].handle, 16 * c.expect["L2_attn"])
            for n in range(8):
                w_, m_ = (1 - n // 4) * 2 + n % 2, n // 2 % 2
                for k in range(KT):
                    m = nc.tensor.matmul(c.ps[:, n, 0:NT], w[:, w_, k, m_ * 128:(m_ + 1) * 128],
                                         c.x_feat[:, k, :, 0:T], start=(k == 0), stop=(k == KT - 1))
                m.then_inc(*proj.next())
            pe.wait_ge(rotated.handle, rotated.at(2))
            for g in range(4):
                m = value_tile(c, c.ps[:, g // 2, (g % 2) * D:(g % 2 + 1) * D], [c.x_feat[:, k] for k in range(KT)],
                               g, [w[:, 4, k, :] for k in range(KT)])
            m.then_inc(*proj.next())
            at.tensor(pe, 2, 2 * at.nm, 4)
            output_of(c, s, at, pe, wo)
            norm_tensor(c, s, pe, False)

        @block.scalar
        def _(act):
            act.wait_ge(at.padded.handle, at.padded.at(at.pads))
            for k in range(KT):
                act.wait_ge(rotated.handle, rotated.at(k + 1))
                for m in range(at.nm):
                    nc.scalar.activation(at.k[:, m, k, :, 0:T], valid(turned_k[k]), ACT.Copy,
                                              scale=c.heads16[:, m:m + 1]).then_inc(*at.k_in.next())
            act.wait_ge(proj.handle, proj.at(9))
            for i in range(2):
                for r in range(2):
                    nc.scalar.copy(at.v[r * TP:(r + 1) * TP, 2 * i:2 * i + 2, r, :],
                       c.ps[r * TP:(r + 1) * TP, i, :].rearrange("p (g n) -> p g n", g=2)).then_inc(*at.v_in.next())
            at.scalar(act)
            norm_scalar(c, s, act, False)

        @block.vector
        def _(dve):
            V = nc.vector
            dve.wait_ge(c.loaded["L2_attn"].handle, 16 * c.expect["L2_attn"])
            for n in range(4):
                dve.wait_ge(proj.handle, proj.at(2 * n + 2))
                for i in range(2):
                    V.tensor_tensor(valid(prod[i]), valid(c.ps[:, 2 * n + i, 0:NT]),
                                         tab[:, i, :].unsqueeze(1).broadcast_to([128, B, T]), ALU.mult).then_inc(*s.dve_chain.next())
                    dve.wait_ge(s.dve_chain.handle, s.dve_chain.last())
                if n < 2:
                    V.tensor_tensor(turned_k[n], prod[0], prod[1], ALU.add).then_inc(*rotated.next())
                    dve.wait_ge(rotated.handle, rotated.last())
                else:
                    V.tensor_tensor(at.q[:, n - 2, :, 0:T], valid(prod[0]), valid(prod[1]), ALU.add).then_inc(*at.q_in.next())
                    dve.wait_ge(at.q_in.handle, at.q_in.last())
            at.vector(dve)
            norm_vector(c, s, dve, False)



def L3_ATTN_LOADS(c):
    return [("L3a_wq", c.at(0, 4096)), ("L3a_wk", c.at(4096, 4096)), ("L3a_wv", c.at(8192, 4096)),
            ("L3a_wo", c.at(12288, 4096)), ("L3a_B", c.at(24100, 2048)), ("L3a_A", c.at(26148, 768)),
            ("L3a_oB", c.at(26916, 256))]


def L3_ATTN_SMALL(c):
    return [("L3a_norm", c.at(23900, 2)), ("L3a_rope", c.at(23902, 2 * T)), ("causal_add3", c.at(24014, T))]


def l3_attention(c, now, prefetch):
    nc, s = c.nc, Stage(c, "L3_attn")
    w = [c.at(4096 * i, 4096) for i in range(4)]
    Bm = c.at(24100, 2048)
    Am = c.at(26148, 768).rearrange("p (i n) -> p i n", i=3)
    oB = c.at(26916, 256)
    normw = c.at(23900, 2)
    tab = c.at(23902, 2 * T).rearrange("p (i t) -> p i t", i=2)
    mask = c.at(24014, T)
    v = c.at(27200, 8192).rearrange("p (g n) -> p g n", g=4)
    W = 16384
    hf = c.at(W, 1024).rearrange("p (k b t) -> p k b t", k=KT, b=B)
    hx = c.at(W + 1024, 1024).rearrange("p (j n) -> p j n", j=J)
    q = [c.at(W + 2048 + 512 * i, 512).rearrange("p (b t) -> p b t", b=B) for i in range(2)]
    kk = [c.at(W + 3072 + NT * i, NT).rearrange("p (b t) -> p b t", b=B) for i in range(2)]
    prod = [c.at(W + 3968 + NT * i, NT) for i in range(4)]
    p = [c.at(W + 5760 + 256 * i, 256).rearrange("p (j t) -> p j t", j=J) for i in range(2)]
    pT = [c.at(W + 6272 + 256 * i, 256).rearrange("p (g q) -> p g q", g=2) for i in range(2)]
    small = c.at(W + 6784, 64)
    yT = [c.at(35400 + 512 * i, 512).rearrange("p (b t) -> p b t", b=B) for i in range(2)]
    ms_in, rms_in, h_in, h_t, hf_in, padded = (s.sem(x) for x in ("ms_in", "rms_in", "h_in", "h_t", "hf_in", "padded"))
    lora_mm, lora_in, v_mm, v_act, v_dve = (s.sem(x) for x in ("lora_mm", "lora_in", "v_mm", "v_act", "v_dve"))
    q_mm, k_mm, prod_in, qk_in, scored, shifted, exped, p_in, turned, pt_in, y_mm, y_in, out_mm = (
        s.sem(x) for x in ("q_mm", "k_mm", "prod_in", "qk_in", "scored", "shifted", "exped", "p_in", "turned",
                           "pt_in", "y_mm", "y_in", "out_mm"))
    NL = 32

    def lora_target(n):
        i, r = n // 8, n % 8
        if i < 3:
            return w[i].rearrange("p (k n) -> p k n", k=KT)[:, r // 4, (r % 4) * 512:(r % 4 + 1) * 512]
        return w[3][:, r * 512:(r + 1) * 512]

    with nc.Block(no_gpsimd_drain=True) as block:
        @block.sync
        def _(sp):
            c.load(sp, "L3_small", L3_ATTN_SMALL(c))
            c.load(sp, "L3_attn", now)
            sp.wait_ge(v_mm.handle, v_mm.at(16))
            sp.wait_ge(lora_mm.handle, lora_mm.at(NL))
            sp.wait_ge(lora_in.handle, lora_in.at(NL))
            prefetch(sp)

        @block.gpsimd
        def _(pool):
            for i in range(2):
                nc.gpsimd.memset(q[i][:, :, T:TP], 0.0).then_inc(*padded.next())
                nc.gpsimd.memset(yT[i][:, :, T:TP], 0.0).then_inc(*padded.next())
                nc.gpsimd.memset(p[i][:, :, T:TP], 0.0).then_inc(*padded.next())
            pool.wait_ge(padded.handle, padded.at(6))
            for n in range(2 * NH):
                pool.wait_ge(prod_in.handle, prod_in.at(n + 1))
                h = n // 2
                if h - 1 > 0:
                    pool.wait_ge(scored.handle, scored.at(h - 1))
                a, b = prod[2 * (n % 2)], prod[2 * (n % 2) + 1]
                dst = q[h % 2][:, :, 0:T] if n % 2 == 0 else kk[h % 2]
                nc.gpsimd.tensor_tensor(dst, valid(a), valid(b), ALU.add).then_inc(*qk_in.next())

        @block.tensor
        def _(pe):
            pe.wait_ge(c.loaded["L3_attn"].handle, 16 * c.expect["L3_attn"])
            for n in range(NL):
                if n - 5 > 0:
                    pe.wait_ge(lora_in.handle, lora_in.at(n - 5))
                i, r = n // 8, n % 8
                bank = c.ps[:, 2 + n % 6, :]
                if i < 3:
                    m = nc.tensor.matmul(bank, Am[:, i, (r // 4) * 128:(r // 4 + 1) * 128],
                                         Bm[:, (r % 4) * 512:(r % 4 + 1) * 512], start=True, stop=True)
                else:
                    for e in range(2):
                        m = nc.tensor.matmul(bank[:, e * D:(e + 1) * D],
                                             Bm[:, (2 * r + e) * 128:(2 * r + e + 1) * 128], oB, start=True, stop=True)
                m.then_inc(*lora_mm.next())
            for j in range(J):
                pe.wait_ge(h_in.handle, h_in.at(j + 1))
                for k in range(KT):
                    t = nc.tensor.transpose(c.ps[:, k, j * 128:(j + 1) * 128], hx[:, j, k * 128:(k + 1) * 128],
                                            c.ident[:])
            t.then_inc(*h_t.next())
            pe.wait_ge(hf_in.handle, hf_in.at(2))
            pe.wait_ge(lora_in.handle, lora_in.at(NL))
            wv = w[2].rearrange("p (k n) -> p k n", k=KT)
            for n in range(16):
                g, r = n // 4, n % 4
                if n >= 6:
                    done = v_dve if n % 2 else v_act
                    if (n - 6) // 2 + 1 > 0:
                        pe.wait_ge(done.handle, done.at((n - 6) // 2 + 1))
                m = value_tile(c, c.ps[:, 2 + n % 6, :], [hf[:, k] for k in range(KT)], g,
                               [wv[:, k, r * 512:(r + 1) * 512] for k in range(KT)])
                m.then_inc(*v_mm.next())
            pe.wait_ge(v_act.handle, v_act.at(8))
            pe.wait_ge(v_dve.handle, v_dve.at(8))
            pe.wait_ge(padded.handle, padded.at(6))
            wq, wk = (w[i].rearrange("p (k n) -> p k n", k=KT) for i in range(2))

            def qk(h):
                if 2 * h > 0:
                    pe.wait_ge(prod_in.handle, prod_in.at(2 * h))
                for k in range(KT):
                    m = nc.tensor.matmul(c.ps[:, 2, 0:NT], wq[:, k, h * HD:(h + 1) * HD], hf[:, k, :, 0:T],
                                         start=(k == 0), stop=(k == KT - 1))
                m.then_inc(*q_mm.next())
                for k in range(KT):
                    m = nc.tensor.matmul(c.ps[:, 3, 0:NT], wk[:, k, h * HD:(h + 1) * HD], hf[:, k, :, 0:T],
                                         start=(k == 0), stop=(k == KT - 1))
                m.then_inc(*k_mm.next())

            def scores(h):
                pe.wait_ge(qk_in.handle, qk_in.at(2 * h + 2))
                if h > 0:
                    pe.wait_ge(shifted.handle, shifted.at(h))
                for b in range(B):
                    m = nc.tensor.matmul(c.ps[(b % 2) * TP:(b % 2 + 1) * TP, 4, (b // 2) * T:(b // 2 + 1) * T],
                                         q[h % 2][:, b, :], kk[h % 2][:, b, :], start=True, stop=True)
                m.then_inc(*scored.next())

            def turn(h):
                pe.wait_ge(p_in.handle, p_in.at(h + 1))
                if h > 0:
                    pe.wait_ge(pt_in.handle, pt_in.at(h))
                for g in range(2):
                    t = nc.tensor.transpose(c.ps[:, 5, g * 128:(g + 1) * 128], p[h % 2][:, 2 * g:2 * g + 2, :], c.ident[:])
                t.then_inc(*turned.next())

            def context(h):
                pe.wait_ge(pt_in.handle, pt_in.at(h + 1))
                if 2 * h > 0:
                    pe.wait_ge(y_in.handle, y_in.at(2 * h))
                for g in range(4):
                    for r in range(2):
                        m = nc.tensor.matmul(c.ps[:, 6 + r, g * T:(g + 1) * T],
                                             v[r * TP:r * TP + T, g, h * HD:(h + 1) * HD],
                                             pT[h % 2][r * TP:r * TP + T, g // 2, (g % 2) * TP:(g % 2) * TP + T],
                                             start=True, stop=True)
                m.then_inc(*y_mm.next())

            def out(h):
                pe.wait_ge(y_in.handle, y_in.at(2 * (h + 1)))
                for j in range(J):
                    m = project_out(c, pe, j, h, yT[h % 2][:, 2 * j:2 * j + 2, :],
                                    w[3].rearrange("p (h n) -> p h n", h=NH)[:, h, :], h == 0, h == NH - 1)
                    if h == NH - 1 and j % 2 == 1:
                        m.then_inc(*s.y_done.next())
                if h < NH - 1:
                    m.then_inc(*out_mm.next())

            for h in range(NH + 3):
                if 2 <= h <= NH + 1:
                    turn(h - 2)
                if h < NH:
                    qk(h)
                if 1 <= h <= NH:
                    scores(h - 1)
                if 2 <= h <= NH + 1:
                    context(h - 2)
                if h >= 3:
                    out(h - 3)
            norm_tensor(c, s, pe, False)

        @block.scalar
        def _(act):
            act.wait_ge(ms_in.handle, ms_in.at(1))
            nc.scalar.activation(small[:, 4:8], small[:, 4:8], ACT.Sqrt).then_inc(*rms_in.next())
            act.wait_ge(rms_in.handle, rms_in.last())
            act.wait_ge(h_t.handle, h_t.at(1))
            act.wait_ge(c.loaded["L3_small"].handle, 16 * 3)
            for k in range(KT):
                nc.scalar.activation(hf[:, k, :, :], c.ps[:, k, :].rearrange("p (b t) -> p b t", b=B), ACT.Copy,
                                          scale=normw[:, k:k + 1]).then_inc(*hf_in.next())
            for n in range(0, 16, 2):
                act.wait_ge(v_mm.handle, v_mm.at(n + 1))
                nc.scalar.copy(v[:, n // 4, (n % 4) * 512:(n % 4 + 1) * 512], c.ps[:, 2 + n % 6, :]).then_inc(*v_act.next())
            for h in range(NH + 1):
                if h < NH:
                    act.wait_ge(shifted.handle, shifted.at(h + 1))
                    nc.scalar.activation(p[h % 2][:, :, 0:T], p[h % 2][:, :, 0:T], ACT.Exp, scale=HD ** -0.5).then_inc(*exped.next())
                if h >= 1:
                    g = h - 1
                    act.wait_ge(y_mm.handle, y_mm.at(g + 1))
                    if g >= 2:
                        act.wait_ge(out_mm.handle, out_mm.at(g - 1))
                    for r in range(2):
                        nc.scalar.copy(yT[g % 2].rearrange("p (a r e) t -> p r a e t", r=2, e=2)[:, r, :, :, 0:T],
                                            c.ps[:, 6 + r, 0:4 * T].rearrange("p (a e t) -> p a e t", a=2, e=2)).then_inc(*y_in.next())
                if h < NH:
                    act.wait_ge(turned.handle, turned.at(h + 1))
                    if h >= 2:
                        act.wait_ge(y_mm.handle, y_mm.at(h - 1))
                    nc.scalar.copy(pT[h % 2].rearrange("p g q -> p (g q)"), c.ps[:, 5, 0:256]).then_inc(*pt_in.next())
            norm_scalar(c, s, act, False)

        @block.vector
        def _(dve):
            V = nc.vector
            for j in range(J):
                V.tensor_tensor(hx[:, j, :], c.x_tok[:, j, :], c.x_tok[:, j, :], ALU.mult).then_inc(*s.dve_chain.next())
                dve.wait_ge(s.dve_chain.handle, s.dve_chain.last())
                V.tensor_reduce(small[:, j:j + 1], hx[:, j, :], AX.X, ALU.add).then_inc(*s.dve_chain.next())
                dve.wait_ge(s.dve_chain.handle, s.dve_chain.last())
            V.tensor_scalar(small[:, 4:8], small[:, 0:4], 1.0 / D, 1e-6, ALU.mult, ALU.add).then_inc(*ms_in.next())
            dve.wait_ge(ms_in.handle, ms_in.last())
            dve.wait_ge(rms_in.handle, rms_in.at(1))
            V.reciprocal(small[:, 8:12], small[:, 4:8]).then_inc(*s.dve_chain.next())
            dve.wait_ge(s.dve_chain.handle, s.dve_chain.last())
            for j in range(J):
                V.tensor_scalar(hx[:, j, :], c.x_tok[:, j, :], small[:, 8 + j:9 + j], None, ALU.mult).then_inc(*h_in.next())
            dve.wait_ge(h_in.handle, h_in.last())
            V.tensor_scalar(c.x_tok[:], c.x_tok[:], 2.0, None, ALU.mult).then_inc(*s.dve_chain.next())
            dve.wait_ge(s.dve_chain.handle, s.dve_chain.last())
            dve.wait_ge(c.loaded["L3_attn"].handle, 16 * c.expect["L3_attn"])
            dve.wait_ge(c.loaded["L3_small"].handle, 16 * 3)
            for n in range(NL):
                dve.wait_ge(lora_mm.handle, lora_mm.at(n + 1))
                t = lora_target(n)
                V.scalar_tensor_tensor(out=t, in0=c.ps[:, 2 + n % 6, :], scalar=1.0 / 16, in1=t,
                                            op0=ALU.mult, op1=ALU.add).then_inc(*lora_in.next())
            for n in range(1, 16, 2):
                dve.wait_ge(v_mm.handle, v_mm.at(n + 1))
                V.tensor_copy(v[:, n // 4, (n % 4) * 512:(n % 4 + 1) * 512], c.ps[:, 2 + n % 6, :]).then_inc(*v_dve.next())
            dve.wait_ge(padded.handle, padded.at(6))

            def rotate(n):
                h, i = n // 2, n % 2
                done = k_mm if i else q_mm
                dve.wait_ge(done.handle, done.at(h + 1))
                if n - 1 > 0:
                    dve.wait_ge(qk_in.handle, qk_in.at(n - 1))
                b = c.ps[:, 2 + i, 0:NT]
                V.tensor_tensor(valid(prod[2 * i]), valid(b), tab[:, 0, :].unsqueeze(1).broadcast_to([128, B, T]),
                                       ALU.mult).then_inc(*s.dve_chain.next())
                for e in range(2):
                    lo, hi = e * 64, (1 - e) * 64
                    ins = V.tensor_tensor(valid(prod[2 * i + 1])[lo:lo + 64], valid(b)[hi:hi + 64],
                                          tab[hi:hi + 64, 1, :].unsqueeze(1).broadcast_to([64, B, T]), ALU.mult)
                    if e:
                        ins.then_inc(*prod_in.next())
                    else:
                        ins.then_inc(*s.dve_chain.next())

            def shift(h):
                dve.wait_ge(scored.handle, scored.at(h + 1))
                if h - 1 > 0:
                    dve.wait_ge(turned.handle, turned.at(h - 1))
                r = p[h % 2][:, :, 0:T]
                V.tensor_tensor(r, c.ps[:, 4, 0:4 * T].rearrange("p (j t) -> p j t", j=J),
                                     mask.unsqueeze(1).broadcast_to([128, J, T]), ALU.add).then_inc(*s.dve_chain.next())
                dve.wait_ge(s.dve_chain.handle, s.dve_chain.last())
                V.tensor_reduce(small[:, 16:20], r, AX.X, ALU.max).then_inc(*s.dve_chain.next())
                dve.wait_ge(s.dve_chain.handle, s.dve_chain.last())
                V.tensor_tensor(r, r, small[:, 16:20].unsqueeze(2).broadcast_to([128, J, T]), ALU.subtract).then_inc(*shifted.next())

            def divide(h):
                dve.wait_ge(exped.handle, exped.at(h + 1))
                r = p[h % 2][:, :, 0:T]
                V.tensor_reduce(small[:, 20:24], r, AX.X, ALU.add).then_inc(*s.dve_chain.next())
                dve.wait_ge(s.dve_chain.handle, s.dve_chain.last())
                V.reciprocal(small[:, 24:28], small[:, 20:24]).then_inc(*s.dve_chain.next())
                dve.wait_ge(s.dve_chain.handle, s.dve_chain.last())
                V.tensor_tensor(r, r, small[:, 24:28].unsqueeze(2).broadcast_to([128, J, T]), ALU.mult).then_inc(*p_in.next())

            for h in range(NH + 1):
                if h < NH:
                    rotate(2 * h)
                    rotate(2 * h + 1)
                if h >= 1:
                    shift(h - 1)
                    divide(h - 1)
            norm_vector(c, s, dve, False)



def ffn_specs():
    sh = lambda n, w=128: (w, n, None)
    return {
        "L0_ffn": Experts(128, 128, 4, [sh(0), sh(1)] + [(128, 2, k) for k in range(8)], 1280,
                          29696, 32256, 34816, 3, 35584, 22000, 35840),
        "L1_ffn": Experts(16, 16, 2, [sh(0), sh(1)] + [(128, 2 + e, e) for e in range(16)], 2304,
                          6144, 10752, 25780, 18, 32448, 30400, 32480),
        "L2_ffn": Experts(9, 8, 2, [(128, n, n) for n in range(10)], 1280,
                          29696, 32256, 34816, 10, 37376, 22000, 37400),
        "L3_ffn": Experts(8, 8, 2, [sh(0), sh(1), sh(2, 96)] + [(128, 3 + n, n) for n in range(11)], 1792,
                          29696, 33280, 0, 14, 37448, 22000, 24064),
    }


def ffn_loads(c, name, f):
    tag = name[:2] + "f"
    d = {"gate": (tag + "_gate", c.at(f.gate, KT * f.hidden)), "up": (tag + "_up", c.at(f.up, KT * f.hidden)),
         "down": (tag + "_down", c.at(f.down, f.downs * D)), "router": (tag + "_router", c.at(f.router, KT * f.cols))}
    if name != "L0_ffn":
        n = {"L1_ffn": 16, "L2_ffn": 10, "L3_ffn": 11}[name]
        d["spread"] = (tag + "_spread", c.at(f.spread, n * 128))
    if name == "L0_ffn":
        d["extra"] = (tag + "_mix", c.at(f.extra, 17))
    if name == "L1_ffn":
        d["extra"] = (tag + "_bias", c.at(f.extra, 16))
    return d


def decoder_program(nc, dram, out):
    with ExitStack() as ctx:
        c = Core(nc, ctx, dram)
        c.sb_small = ctx.enter_context(nc.sbuf_tensor("softmax_stats", [128, 12], F32))
        spec = ffn_specs()
        fl = {n: ffn_loads(c, n, spec[n]) for n in spec}
        x0, x2, x3 = X_WEIGHTS(c, X_AT, "L0x"), X_WEIGHTS(c, X_AT, "L2x"), X_WEIGHTS(c, X3_AT, "L3x")
        pick = lambda d, *keys: [d[k] for k in keys]
        c.expect = {"L0_xattn_first": 3, "L0_xattn_next": 2, "L0_xattn_last": 2, "L2_xattn_first": 3, "L2_xattn_next": 2,
                    "L2_xattn_last": 2, "L3_xattn_first": 3, "L3_xattn_next": 1, "L3_xattn_last": 2,
                    "L0_ffn": 5, "L1_ffn": 6, "L2_ffn": 4, "L2_ffn_late": 1, "L3_ffn": 3, "L3_ffn_late": 2,
                    "L1_attn": 4, "L1_xattn": 5, "L2_attn": 4, "L3_attn": 7}
        nothing = lambda sp: None

        def stage_l0_attn():
            l0_attention(c, lambda sp: c.load(sp, "L0_xattn_first", pick(x0, "Wqr", "Wkr", "Wq")))

        def stage_l0_x():
            cross_attention(c, "L0_xattn", X_AT, True, [("L0_xattn_next", pick(x0, "kcq", "rope")),
                                                        ("L0_xattn_last", pick(x0, "kckv", "Wo"))],
                            lambda sp: c.load(sp, "L0_ffn", list(fl["L0_ffn"].values())))

        def stage_l0_ffn():
            def ahead(sp):
                c.load(sp, "L1_attn", L1_ATTN_LOADS(c))
                c.load(sp, "L1_xattn", L1_X_LOADS(c)[0:4])
                c.load(sp, "L1_ffn", pick(fl["L1_ffn"], "gate", "up"))
            feed_forward(c, "L0_ffn", spec["L0_ffn"], [], ahead, None, lambda s, dve, step: quantise_weights(c, s, dve, step))

        def stage_l1_attn():
            l1_attention(c, [], nothing)

        def stage_l1_x():
            l1_cross(c, L1_X_LOADS(c)[4:], lambda sp: c.load(sp, "L1_ffn", pick(
                fl["L1_ffn"], "down", "router", "spread", "extra")))

        def stage_l1_ffn():
            feed_forward(c, "L1_ffn", spec["L1_ffn"], [], lambda sp: c.load(sp, "L2_attn", L2_ATTN_LOADS(c)))

        def stage_l2_attn():
            def ahead(sp):
                c.load(sp, "L2_xattn_first", pick(x2, "Wqr", "Wkr", "Wq"))
                c.load(sp, "L2_xattn_next", pick(x2, "kcq", "rope"))
                c.load(sp, "L2_xattn_last", pick(x2, "kckv", "Wo"))
            l2_attention(c, [], ahead)

        def stage_l2_x():
            cross_attention(c, "L2_xattn", X_AT, True, [], lambda sp: c.load(sp, "L2_ffn", pick(
                fl["L2_ffn"], "gate", "up", "down", "router")))

        def stage_l2_ffn():
            feed_forward(c, "L2_ffn", spec["L2_ffn"], pick(fl["L2_ffn"], "spread"),
                         lambda sp: c.load(sp, "L3_attn", L3_ATTN_LOADS(c)))

        def stage_l3_attn():
            l3_attention(c, [], lambda sp: c.load(sp, "L3_xattn_first", pick(x3, "Wqr", "Wkr", "kcq")))

        def stage_l3_x():
            cross_attention(c, "L3_xattn", X3_AT, False, [("L3_xattn_next", pick(x3, "Wq")), ("L3_xattn_last", pick(x3, "kckv", "Wo"))],
                            lambda sp: c.load(sp, "L3_ffn", pick(fl["L3_ffn"], "router", "gate", "up")))

        def stage_l3_ffn():
            feed_forward(c, "L3_ffn", spec["L3_ffn"], pick(fl["L3_ffn"], "spread", "down"), nothing, out)

        for run in (stage_l0_attn, stage_l0_x, stage_l0_ffn, stage_l1_attn, stage_l1_x, stage_l1_ffn,
                    stage_l2_attn, stage_l2_x, stage_l2_ffn, stage_l3_attn, stage_l3_x, stage_l3_ffn):
            run()



def lay_out(i, np):
    f = lambda n: np.asarray(i[n])
    out = {}

    def tiles(w):
        w = np.asarray(w)
        return np.ascontiguousarray(w.reshape(-1, 128, w.shape[-1]).transpose(1, 0, 2).reshape(128, -1))

    def rows(w, n=128):
        return np.ascontiguousarray(np.broadcast_to(np.asarray(w).reshape(1, -1), (n, np.asarray(w).size)))

    x = f("x")
    xt = np.zeros((2, TP, J, D), np.float32)
    xt[:, :T] = x.reshape(J, 2, T, D).transpose(1, 2, 0, 3)
    out["x_tok"] = xt.reshape(128, J * D)
    xf = np.zeros((128, KT, B, TP), np.float32)
    xf[..., :T] = x.reshape(B, T, KT, 128).transpose(3, 2, 0, 1)
    out["x_feat"] = xf.reshape(128, -1)
    ctx = f("ctx_512")
    out["ctx"] = np.ascontiguousarray(ctx.reshape(J, 2, LP, LT, LC).transpose(2, 0, 3, 1, 4).reshape(LP, -1))
    out["ident"] = np.eye(128, dtype=np.float32)
    pp = np.arange(128)
    out["heads8"] = (pp[:, None] // 8 % 4 == np.arange(4)).astype(np.float32)
    out["heads16"] = (pp[:, None] // 16 % 2 == np.arange(2)).astype(np.float32)

    def rope(length, dim):
        inv = np.float32(1.0) / (np.float32(10000.0) ** (np.arange(0, dim, 2, dtype=np.float32) / np.float32(dim)))
        a = np.arange(length, dtype=np.float32)[:, None] * inv.astype(np.float32)[None, :]
        return np.cos(a).astype(np.float32), np.sin(a).astype(np.float32)

    co, si = (np.repeat(a, 2, axis=1) for a in rope(L, LC))
    sgn = np.where(np.arange(LC) < LC // 2, -1.0, 1.0).astype(np.float32)
    out["ctx_cos"] = np.ascontiguousarray(co.reshape(LP, LT * LC))
    out["ctx_sin"] = np.ascontiguousarray((si * sgn).reshape(LP, LT * LC))
    co, si = (np.repeat(a, 2, axis=1).T for a in rope(T, DQ))
    out["q_rope"] = np.ascontiguousarray(np.concatenate([co[:DH], -si[:DH], co[DH:], si[DH:]], axis=1))
    out["L0a_Wq"], out["L0a_Wk"], out["L0a_Wv"] = tiles(f("L0_attn_Wq")), tiles(f("L0_attn_Wk")), tiles(f("L0_attn_Wv"))
    out["L0a_Wg"], out["L0a_Wc"] = tiles(f("L0_attn_Wg")), tiles(f("L0_attn_Wc"))
    out["L0a_bc"] = rows(f("L0_attn_bc"))
    hh, tt = pp // TP, pp % TP
    real = tt < T
    out["L0a_after"] = ((hh[:, None] == hh) & (tt[:, None] > tt) & real[:, None]).astype(np.float32)
    out["L0a_half"] = np.concatenate([np.repeat(((hh == h) & real)[:, None], 128, 1) for h in range(2)], 1).astype(np.float32)
    out["L0a_tri"] = (tt[:, None] <= np.arange(T)).astype(np.float32)
    out["L0a_causal"] = ((tt[:, None] <= np.arange(T)) & real[:, None]).astype(np.float32)
    add = np.where(np.arange(T)[None, :] > tt[:, None], -3.0e38, 0.0).astype(np.float32)
    out["causal_add"] = out["causal_add2"] = out["causal_add3"] = add
    for l in "023":
        g = lambda n: f(f"L{l}_xattn_{n}")
        t = f"L{l}x_"
        if l == "3":
            out[t + "Wq"] = tiles(g("Wq"))
            out[t + "kcqT"] = np.ascontiguousarray(g("w_kc_q").transpose(2, 0, 1).reshape(2, DH, -1).transpose(1, 0, 2).reshape(DH, -1))
        else:
            out[t + "Wq"] = tiles(g("Wq").T)
            out[t + "kcq"] = np.ascontiguousarray(g("w_kc_q").transpose(1, 0, 2).reshape(128, -1))
        out[t + "kckv"] = np.ascontiguousarray(g("w_kc_kv").transpose(1, 0, 2).reshape(128, -1))
        out[t + "Wqr"] = np.ascontiguousarray(g("W_qr").transpose(2, 0, 1).reshape(64, -1))
        out[t + "Wkr"] = np.ascontiguousarray(g("W_kr").transpose(2, 0, 1).reshape(64, -1))
        out[t + "Wo"] = tiles(g("Wo").T)
    cat = lambda parts: tiles(np.concatenate(parts, axis=1))
    out["L0f_gate"] = cat([f("L0_ffn_shared_w_gate"), f("L0_ffn_w_gate")])
    out["L0f_up"] = cat([f("L0_ffn_shared_w_up"), f("L0_ffn_w_up")])
    out["L0f_down"] = tiles(np.concatenate([f("L0_ffn_shared_w_down"), f("L0_ffn_w_down")], 0))
    out["L0f_router"] = tiles(f("L0_ffn_w_router"))
    out["L0f_mix"] = np.concatenate([f("L0_ffn_amplitudes").reshape(128, 16), f("L0_ffn_expert_scale")[:, None]], 1)
    ecat = lambda w: np.asarray(w).transpose(1, 0, 2).reshape(D, -1)
    out["L1f_gate"] = cat([f("L1_ffn_Su")[0], ecat(f("L1_ffn_Wu"))])
    out["L1f_up"] = cat([f("L1_ffn_Sg")[0], ecat(f("L1_ffn_Wg"))])
    out["L1f_down"] = tiles(np.concatenate([f("L1_ffn_Sd")[0], f("L1_ffn_Wd").reshape(-1, D)], 0))
    out["L1f_router"] = tiles(f("L1_ffn_router_w").T)
    out["L1f_bias"] = rows(f("L1_ffn_router_bias"))

    def spread(e, hidden, width):
        return (np.minimum(np.arange(hidden) // width, e - 1)[None, :] == pp[:, None]).astype(np.float32)

    out["L1f_spread"] = spread(16, 2048, 128)
    out["L2f_gate"] = cat([f("L2_ffn_w_gate").reshape(-1, D).T, f("L2_ffn_sh_gate").T])
    out["L2f_up"] = cat([f("L2_ffn_w_up").reshape(-1, D).T, f("L2_ffn_sh_up").T])
    out["L2f_down"] = tiles(np.concatenate([f("L2_ffn_w_down").transpose(0, 2, 1).reshape(-1, D), f("L2_ffn_sh_down").T], 0))
    out["L2f_router"] = tiles(np.concatenate([f("L2_ffn_gate_w"), f("L2_ffn_se_gate_w")], 0).T)
    out["L2f_spread"] = spread(9, 1280, 128)
    pad = lambda w, n: np.concatenate([w, np.zeros((w.shape[0], n), np.float32)], 1)
    out["L3f_gate"] = cat([pad(f("L3_ffn_sg"), 32), ecat(f("L3_ffn_wg"))])
    out["L3f_up"] = cat([pad(f("L3_ffn_su"), 32), ecat(f("L3_ffn_wu"))])
    out["L3f_down"] = tiles(np.concatenate([f("L3_ffn_sd"), np.zeros((32, D), np.float32),
                                            f("L3_ffn_wd").reshape(-1, D)], 0))
    out["L3f_router"] = tiles(f("L3_ffn_router_w").T)
    out["L3f_spread"] = spread(8, 1408, 176)
    ws = [f(f"L1_attn_{n}_weight") for n in "qkvo"]
    out["L1a_W"] = np.concatenate([tiles(w) for w in ws], 1)
    out["L1a_WT"] = np.concatenate([tiles(w.T) for w in ws], 1)
    out["L1a_bias"] = np.concatenate([f(f"L1_attn_{n}_bias").reshape(2, 128).T for n in "qkv"]
                                     + [np.zeros((128, 2), np.float32)], 1)
    out["L1a_ob"] = rows(f("L1_attn_o_bias"))
    out["L1x_Wq"], out["L1x_Wout"] = tiles(f("L1_xattn_Wq").T), tiles(f("L1_xattn_Wout").T)
    out["L1x_Wkv"] = np.ascontiguousarray(f("L1_xattn_Wkv_expand").T)
    lat = np.zeros((LC, B, TP), np.float32)
    lat[:, :, :T] = ctx[:, :T].transpose(2, 0, 1)
    out["L1x_lat"] = lat.reshape(LC, -1)
    qw, kvw = f("L2_attn_q_w"), f("L2_attn_kv_w")
    rep = lambda w: np.repeat(w.reshape(4, 1, 16, D), 4, axis=1).reshape(256, D)
    kw, vw = rep(kvw[:64]), rep(kvw[64:])
    swap = lambda w: w.reshape(128, 2, D)[:, ::-1].reshape(256, D)
    out["L2a_W"] = np.concatenate([tiles(w.T) for w in (qw, swap(qw), kw, swap(kw), vw)], 1)
    out["L2a_Wo"] = tiles(f("L2_attn_c_w").T)
    co, si = rope(T, 16)
    d = pp % 16
    sg = np.where(d % 2 == 0, -1.0, 1.0).astype(np.float32)[:, None]
    out["L2a_rope"] = np.ascontiguousarray(np.concatenate([co.T[d // 2], si.T[d // 2] * sg], 1))
    out["L3a_wq"], out["L3a_wk"], out["L3a_wv"] = (tiles(f(f"L3_attn_w{n}").T) for n in "qkv")
    out["L3a_wo"] = tiles(f("L3_attn_wo").T)
    bm = np.zeros((128, 2048), np.float32)
    am = np.zeros((128, 3, D), np.float32)
    for n, q in enumerate("qkv"):
        bm[32 * n:32 * n + 16] = f(f"L3_attn_{q}B").T
        am[32 * n:32 * n + 16, n] = f(f"L3_attn_{q}A")
    bm[96:112] = f("L3_attn_oA")
    ob = np.zeros((128, D), np.float32)
    ob[96:112] = f("L3_attn_oB").T
    out["L3a_B"], out["L3a_A"], out["L3a_oB"] = bm, am.reshape(128, -1), ob
    out["L3a_norm"] = np.ascontiguousarray(f("L3_attn_norm_w").reshape(2, 128).T)
    co, si = rope(T, 128)
    sg = np.where(pp < 64, 1.0, -1.0).astype(np.float32)[:, None]
    out["L3a_rope"] = np.ascontiguousarray(np.concatenate([co.T[pp % 64], si.T[pp % 64] * sg], 1))
    return out


def kernel(**inputs):
    import numpy as _np
    import concourse.bacc as _bacc
    from concourse.bass_utils import run_bass_kernel_spmd as _run

    nc = _bacc.Bacc("TRN2", target_bir_lowering=False, num_devices=1)
    arrays, dram = {}, {}
    for name, a in lay_out(inputs, _np).items():
        a = _np.ascontiguousarray(a)
        arrays["in_" + name] = a
        dram[name] = nc.dram_tensor("in_" + name, a.shape, mybir.dt.from_np(a.dtype), kind="ExternalInput").ap()
    out = nc.dram_tensor("out_0", (B, T, D), F32, kind="ExternalOutput").ap()
    decoder_program(nc, dram, out)
    r = _run(nc, [arrays], core_ids=[0])
    return r.results[0]["out_0"]
```
